# Optimizing a Trainium2 kernel written in Bass

```python
import numpy as np
import jax
import jax.numpy as jnp

def _softmax(x, axis=-1):
    return jax.nn.softmax(x, axis=axis)
def _gelu(x):
    return jax.nn.gelu(x, approximate=True)
def _silu(x):
    return jax.nn.silu(x)
def _sigmoid(x):
    return jax.nn.sigmoid(x)
def _layernorm(x, axis=-1, eps=1e-5):
    m = jnp.mean(x, axis=axis, keepdims=True)
    v = jnp.var(x, axis=axis, keepdims=True)
    return (x - m) / jnp.sqrt(v + eps)
def _scatter_add(tgt, idx, src, axis=0):
    return tgt.at[idx].add(src)
def _segment_sum(src, seg, n):
    return jax.ops.segment_sum(src, seg, n)

kernel_name = 'mk_conv_preact_d2_conv_nchw8_879afc'

def setup_inputs(seed: int = 0):
    np.random.seed(seed)
    _w = jnp.asarray
    def _rec_inputs():
        import jax
        import jax.numpy as jnp
        _gk = jax.random.key(seed)
        x = -0.0005207 + 1.001 * jax.random.normal(jax.random.fold_in(_gk, 1), (1, 8, 256, 1024), jnp.float32)
        return x
    x = _rec_inputs()
    def _L0_conv_setup():
        import math
        import jax, jax.numpy as jnp
        import numpy as np
        B, C, NH, F, W = (1, 8, 8, 256, 1024)
        D = F // NH

        def mc_linear(x, Wpw, bpw=None):
            y = jnp.einsum('bchw,cgh->bcgw', x, Wpw)
            if bpw is not None:
                y = y + bpw
            return y

        def conv_w3(x, Wc, bc):
            y = jax.lax.conv_general_dilated(x, Wc, window_strides=(1, 1), padding=[(0, 0), (1, 1)], dimension_numbers=('NCHW', 'OIHW', 'NCHW'))
            return y + bc[None, :, None, None]

        def rotary(x):
            w, d = (x.shape[-2], x.shape[-1])
            inv_freq = 1.0 / 10000.0 ** (jnp.arange(0, d, 2, dtype=jnp.float32) / d)
            freqs = jnp.arange(w, dtype=jnp.float32)[:, None] * inv_freq
            freqs = jnp.repeat(freqs, 2, axis=-1)
            cos, sin = (jnp.cos(freqs), jnp.sin(freqs))
            x2 = x.reshape(*x.shape[:-1], d // 2, 2)
            xr = jnp.stack([-x2[..., 1], x2[..., 0]], axis=-1).reshape(x.shape)
            return x * cos + xr * sin
        key = jax.random.key(seed)
        ks = jax.random.split(key, 16)
        s = 0.05
        rn = lambda k, shape: jax.random.normal(k, shape, jnp.float32) * s
        inp = {'x': jax.random.normal(ks[0], (B, C, F, W), jnp.float32)}
        for i, n in enumerate(['q', 'k', 'v']):
            inp[f'W{n}_pw'] = rn(ks[1 + 4 * i], (C, F, F))
            inp[f'b{n}_pw'] = rn(ks[2 + 4 * i], (C, F, 1))
            inp[f'W{n}_conv'] = rn(ks[3 + 4 * i], (C, C, 1, 3))
            inp[f'b{n}_conv'] = rn(ks[4 + 4 * i], (C,))
        inp['Wo_pw'] = rn(ks[13], (C, F, F))
        inp['Wo_dw'] = rn(ks[14], (C, C))
        return inp
    _L0_conv_all = _L0_conv_setup()
    _L0_conv_in = {k: v for k, v in _L0_conv_all.items() if k in ('Wq_pw', 'bq_pw', 'Wq_conv', 'bq_conv', 'Wk_pw', 'bk_pw', 'Wk_conv', 'bk_conv', 'Wv_pw', 'bv_pw', 'Wv_conv', 'bv_conv', 'Wo_pw', 'Wo_dw', )}
    del _L0_conv_all

    def _L1_conv_setup():
        import jax, jax.numpy as jnp
        import numpy as np
        D_STATE = 16
        DT_RANK = 16
        D_CONV = 4
        EXPAND = 2
        LN_EPS = 1e-05

        def _ln_over_D(x, g, b):
            m = jnp.mean(x, axis=2, keepdims=True)
            v = jnp.var(x, axis=2, keepdims=True)
            return (x - m) / jnp.sqrt(v + LN_EPS) * g[None, None, :, None] + b[None, None, :, None]

        def _causal_dwconv(x, w, b):
            di = w.shape[0]
            xT = jnp.transpose(x, (0, 2, 1))
            xp = jnp.pad(xT, ((0, 0), (0, 0), (D_CONV - 1, 0)))
            out = jax.lax.conv_general_dilated(xp, w[:, None, :], (1,), 'VALID', feature_group_count=di, dimension_numbers=('NCH', 'OIH', 'NCH'))
            out = out + b[None, :, None]
            return jnp.transpose(out, (0, 2, 1))

        def _selective_scan(u, dt, A, Bm, Cm, D_skip):
            N, L, di = u.shape
            ds = A.shape[1]

            def step(h, inp):
                dt_t, B_t, u_t, C_t = inp
                dA = jnp.exp(dt_t[:, :, None] * A)
                h = h * dA + (dt_t * u_t)[:, :, None] * B_t[:, None, :]
                y = jnp.einsum('nds,ns->nd', h, C_t)
                return (h, y)
            h0 = jnp.zeros((N, di, ds), u.dtype)
            xs = (jnp.moveaxis(dt, 1, 0), jnp.moveaxis(Bm, 1, 0), jnp.moveaxis(u, 1, 0), jnp.moveaxis(Cm, 1, 0))
            _, ys = jax.lax.scan(step, h0, xs)
            return jnp.moveaxis(ys, 0, 1) + u * D_skip
        key = jax.random.key(seed)
        ks = jax.random.split(key, 10)
        f = jnp.float32
        B, C, D, L = (2, 8, 256, 1024)
        di = EXPAND * D
        MD = C * D
        p = {}
        p['x'] = jax.random.normal(ks[0], (B, C, D, L), f)
        p['n1_g'] = jnp.ones((D,), f)
        p['n1_b'] = jnp.zeros((D,), f)
        p['n2_g'] = jnp.ones((D,), f)
        p['n2_b'] = jnp.zeros((D,), f)
        p['in_proj_w'] = jax.random.normal(ks[1], (2 * di, D), f) * 0.06
        p['conv_w'] = jax.random.normal(ks[2], (di, D_CONV), f) * 0.5
        p['conv_b'] = jnp.zeros((di,), f)
        p['x_proj_w'] = jax.random.normal(ks[3], (DT_RANK + 2 * D_STATE, di), f) * 0.04
        p['dt_proj_w'] = jax.random.normal(ks[4], (di, DT_RANK), f) * 0.1
        p['dt_proj_b'] = jnp.full((di,), -4.0, f)
        p['A_log'] = jnp.log(jnp.broadcast_to(jnp.arange(1, D_STATE + 1, dtype=f), (di, D_STATE)))
        p['D_skip'] = jnp.ones((di,), f)
        p['out_proj_w'] = jax.random.normal(ks[5], (D, di), f) * 0.04
        p['pw1_w'] = jax.random.normal(ks[6], (2 * MD, MD), f) * 0.02
        p['pw1_b'] = jnp.zeros((2 * MD,), f)
        p['pw2_w'] = jax.random.normal(ks[7], (MD, 2 * MD), f) * 0.02
        p['pw2_b'] = jnp.zeros((MD,), f)
        return p
    _L1_conv_all = _L1_conv_setup()
    _L1_conv_in = {k: v for k, v in _L1_conv_all.items() if k in ('n1_g', 'n1_b', 'n2_g', 'n2_b', 'in_proj_w', 'conv_w', 'conv_b', 'x_proj_w', 'dt_proj_w', 'dt_proj_b', 'A_log', 'D_skip', 'out_proj_w', 'pw1_w', 'pw1_b', 'pw2_w', 'pw2_b', )}
    del _L1_conv_all

    return {
        "x": x,
        "L0_conv_Wq_pw": _L0_conv_in["Wq_pw"],
        "L0_conv_bq_pw": _L0_conv_in["bq_pw"],
        "L0_conv_Wq_conv": _L0_conv_in["Wq_conv"],
        "L0_conv_bq_conv": _L0_conv_in["bq_conv"],
        "L0_conv_Wk_pw": _L0_conv_in["Wk_pw"],
        "L0_conv_bk_pw": _L0_conv_in["bk_pw"],
        "L0_conv_Wk_conv": _L0_conv_in["Wk_conv"],
        "L0_conv_bk_conv": _L0_conv_in["bk_conv"],
        "L0_conv_Wv_pw": _L0_conv_in["Wv_pw"],
        "L0_conv_bv_pw": _L0_conv_in["bv_pw"],
        "L0_conv_Wv_conv": _L0_conv_in["Wv_conv"],
        "L0_conv_bv_conv": _L0_conv_in["bv_conv"],
        "L0_conv_Wo_pw": _L0_conv_in["Wo_pw"],
        "L0_conv_Wo_dw": _L0_conv_in["Wo_dw"],
        "L1_conv_n1_g": _L1_conv_in["n1_g"],
        "L1_conv_n1_b": _L1_conv_in["n1_b"],
        "L1_conv_n2_g": _L1_conv_in["n2_g"],
        "L1_conv_n2_b": _L1_conv_in["n2_b"],
        "L1_conv_in_proj_w": _L1_conv_in["in_proj_w"],
        "L1_conv_conv_w": _L1_conv_in["conv_w"],
        "L1_conv_conv_b": _L1_conv_in["conv_b"],
        "L1_conv_x_proj_w": _L1_conv_in["x_proj_w"],
        "L1_conv_dt_proj_w": _L1_conv_in["dt_proj_w"],
        "L1_conv_dt_proj_b": _L1_conv_in["dt_proj_b"],
        "L1_conv_A_log": _L1_conv_in["A_log"],
        "L1_conv_D_skip": _L1_conv_in["D_skip"],
        "L1_conv_out_proj_w": _L1_conv_in["out_proj_w"],
        "L1_conv_pw1_w": _L1_conv_in["pw1_w"],
        "L1_conv_pw1_b": _L1_conv_in["pw1_b"],
        "L1_conv_pw2_w": _L1_conv_in["pw2_w"],
        "L1_conv_pw2_b": _L1_conv_in["pw2_b"],
    }

def reference(x, L0_conv_Wq_pw, L0_conv_bq_pw, L0_conv_Wq_conv, L0_conv_bq_conv, L0_conv_Wk_pw, L0_conv_bk_pw, L0_conv_Wk_conv, L0_conv_bk_conv, L0_conv_Wv_pw, L0_conv_bv_pw, L0_conv_Wv_conv, L0_conv_bv_conv, L0_conv_Wo_pw, L0_conv_Wo_dw, L1_conv_n1_g, L1_conv_n1_b, L1_conv_n2_g, L1_conv_n2_b, L1_conv_in_proj_w, L1_conv_conv_w, L1_conv_conv_b, L1_conv_x_proj_w, L1_conv_dt_proj_w, L1_conv_dt_proj_b, L1_conv_A_log, L1_conv_D_skip, L1_conv_out_proj_w, L1_conv_pw1_w, L1_conv_pw1_b, L1_conv_pw2_w, L1_conv_pw2_b):
    import jax
    import jax.numpy as jnp
    def _L0_conv_ref(x, Wq_pw, bq_pw, Wq_conv, bq_conv, Wk_pw, bk_pw, Wk_conv, bk_conv, Wv_pw, bv_pw, Wv_conv, bv_conv, Wo_pw, Wo_dw):
        import math
        import jax, jax.numpy as jnp
        import numpy as np
        B, C, NH, F, W = (1, 8, 8, 256, 1024)
        D = F // NH

        def mc_linear(x, Wpw, bpw=None):
            y = jnp.einsum('bchw,cgh->bcgw', x, Wpw)
            if bpw is not None:
                y = y + bpw
            return y

        def conv_w3(x, Wc, bc):
            y = jax.lax.conv_general_dilated(x, Wc, window_strides=(1, 1), padding=[(0, 0), (1, 1)], dimension_numbers=('NCHW', 'OIHW', 'NCHW'))
            return y + bc[None, :, None, None]

        def rotary(x):
            w, d = (x.shape[-2], x.shape[-1])
            inv_freq = 1.0 / 10000.0 ** (jnp.arange(0, d, 2, dtype=jnp.float32) / d)
            freqs = jnp.arange(w, dtype=jnp.float32)[:, None] * inv_freq
            freqs = jnp.repeat(freqs, 2, axis=-1)
            cos, sin = (jnp.cos(freqs), jnp.sin(freqs))
            x2 = x.reshape(*x.shape[:-1], d // 2, 2)
            xr = jnp.stack([-x2[..., 1], x2[..., 0]], axis=-1).reshape(x.shape)
            return x * cos + xr * sin
        b, c, h, w = x.shape

        def proj_heads(Wpw, bpw, Wc, bc):
            y = conv_w3(mc_linear(x, Wpw, bpw), Wc, bc)
            y = y.transpose(0, 1, 3, 2)
            return y.reshape(b, c, w, NH, D).transpose(0, 1, 3, 2, 4)
        q = rotary(proj_heads(Wq_pw, bq_pw, Wq_conv, bq_conv))
        k = rotary(proj_heads(Wk_pw, bk_pw, Wk_conv, bk_conv))
        v = proj_heads(Wv_pw, bv_pw, Wv_conv, bv_conv)
        scores = jnp.einsum('bcnqd,bcnkd->bcnqk', q, k) / math.sqrt(h)
        a = jnp.einsum('bcnqk,bcnkd->bcnqd', jax.nn.softmax(scores, axis=-1), v)
        a = a.transpose(0, 1, 3, 2, 4).reshape(b, c, w, h).transpose(0, 1, 3, 2)
        out = mc_linear(a, Wo_pw)
        out = jnp.einsum('bchw,oc->bohw', out, Wo_dw)
        return out

    def _L1_conv_ref(x, n1_g, n1_b, n2_g, n2_b, in_proj_w, conv_w, conv_b, x_proj_w, dt_proj_w, dt_proj_b, A_log, D_skip, out_proj_w, pw1_w, pw1_b, pw2_w, pw2_b):
        import jax, jax.numpy as jnp
        import numpy as np
        D_STATE = 16
        DT_RANK = 16
        D_CONV = 4
        EXPAND = 2
        LN_EPS = 1e-05

        def _ln_over_D(x, g, b):
            m = jnp.mean(x, axis=2, keepdims=True)
            v = jnp.var(x, axis=2, keepdims=True)
            return (x - m) / jnp.sqrt(v + LN_EPS) * g[None, None, :, None] + b[None, None, :, None]

        def _causal_dwconv(x, w, b):
            di = w.shape[0]
            xT = jnp.transpose(x, (0, 2, 1))
            xp = jnp.pad(xT, ((0, 0), (0, 0), (D_CONV - 1, 0)))
            out = jax.lax.conv_general_dilated(xp, w[:, None, :], (1,), 'VALID', feature_group_count=di, dimension_numbers=('NCH', 'OIH', 'NCH'))
            out = out + b[None, :, None]
            return jnp.transpose(out, (0, 2, 1))

        def _selective_scan(u, dt, A, Bm, Cm, D_skip):
            N, L, di = u.shape
            ds = A.shape[1]

            def step(h, inp):
                dt_t, B_t, u_t, C_t = inp
                dA = jnp.exp(dt_t[:, :, None] * A)
                h = h * dA + (dt_t * u_t)[:, :, None] * B_t[:, None, :]
                y = jnp.einsum('nds,ns->nd', h, C_t)
                return (h, y)
            h0 = jnp.zeros((N, di, ds), u.dtype)
            xs = (jnp.moveaxis(dt, 1, 0), jnp.moveaxis(Bm, 1, 0), jnp.moveaxis(u, 1, 0), jnp.moveaxis(Cm, 1, 0))
            _, ys = jax.lax.scan(step, h0, xs)
            return jnp.moveaxis(ys, 0, 1) + u * D_skip
        B, C, D, L = x.shape
        res = x
        h = _ln_over_D(x, n1_g, n1_b)
        u = jnp.transpose(h.reshape(B * C, D, L), (0, 2, 1))
        xz = u @ in_proj_w.T
        di = in_proj_w.shape[0] // 2
        xi, z = (xz[..., :di], xz[..., di:])
        xi = jax.nn.silu(_causal_dwconv(xi, conv_w, conv_b))
        x_dbl = xi @ x_proj_w.T
        dt = jax.nn.softplus(x_dbl[..., :DT_RANK] @ dt_proj_w.T + dt_proj_b)
        Bm = x_dbl[..., DT_RANK:DT_RANK + D_STATE]
        Cm = x_dbl[..., DT_RANK + D_STATE:]
        A = -jnp.exp(A_log)
        y = _selective_scan(xi, dt, A, Bm, Cm, D_skip)
        y = y * jax.nn.silu(z)
        out = y @ out_proj_w.T
        x = res + jnp.transpose(out, (0, 2, 1)).reshape(B, C, D, L)
        res = x
        h = _ln_over_D(x, n2_g, n2_b)
        hh = h.reshape(B, C * D, L)
        hh = jax.nn.relu(jnp.einsum('oc,bcl->bol', pw1_w, hh) + pw1_b[:, None])
        hh = jnp.einsum('oc,bcl->bol', pw2_w, hh) + pw2_b[:, None]
        return res + hh.reshape(B, C, D, L)

    def _gn(v, G=4, eps=1e-5):
        B_, C_, H_, W_ = v.shape
        g = v.reshape(B_, G, C_ // G, H_, W_)
        m = jnp.mean(g, axis=(2, 3, 4), keepdims=True)
        s = jnp.var(g, axis=(2, 3, 4), keepdims=True)
        return ((g - m) / jnp.sqrt(s + eps)).reshape(v.shape)

    def _ln_c(v, eps=1e-6):
        m = jnp.mean(v, axis=1, keepdims=True)
        s = jnp.var(v, axis=1, keepdims=True)
        return (v - m) / jnp.sqrt(s + eps)

    def _ln_t(v, eps=1e-5):
        m = jnp.mean(v, axis=-1, keepdims=True)
        s = jnp.var(v, axis=-1, keepdims=True)
        return (v - m) / jnp.sqrt(s + eps)

    def _to_tokens(v):
        B_, C_, H_, W_ = v.shape
        return v.reshape(B_, C_, H_ * W_).transpose(0, 2, 1)
    def _from_tokens(t, like):
        B_, C_, H_, W_ = like.shape
        return t.transpose(0, 2, 1).reshape(B_, C_, H_, W_)

    x = x + _L0_conv_ref(_gn(x), L0_conv_Wq_pw, L0_conv_bq_pw, L0_conv_Wq_conv, L0_conv_bq_conv, L0_conv_Wk_pw, L0_conv_bk_pw, L0_conv_Wk_conv, L0_conv_bk_conv, L0_conv_Wv_pw, L0_conv_bv_pw, L0_conv_Wv_conv, L0_conv_bv_conv, L0_conv_Wo_pw, L0_conv_Wo_dw)
    x = x + _L1_conv_ref(_gn(x), L1_conv_n1_g, L1_conv_n1_b, L1_conv_n2_g, L1_conv_n2_b, L1_conv_in_proj_w, L1_conv_conv_w, L1_conv_conv_b, L1_conv_x_proj_w, L1_conv_dt_proj_w, L1_conv_dt_proj_b, L1_conv_A_log, L1_conv_D_skip, L1_conv_out_proj_w, L1_conv_pw1_w, L1_conv_pw1_b, L1_conv_pw2_w, L1_conv_pw2_b)
    return x


_drawn_inputs = setup_inputs


def setup_inputs(seed=0):
    import zlib

    import numpy as np

    out = dict(_drawn_inputs(seed))
    spreads = {'L1_conv_n1_g': (1.0, 0.2),
     'L1_conv_n1_b': (0.0, 0.1),
     'L1_conv_n2_g': (1.0, 0.6),
     'L1_conv_n2_b': (0.0, 0.8),
     'L1_conv_conv_b': (0.0, 0.414),
     'L1_conv_dt_proj_b': (-4.0, 0.6),
     'L1_conv_D_skip': (1.0, 0.6),
     'L1_conv_pw1_b': (0.0, 0.8),
     'L1_conv_pw2_b': (0.0, 0.8)}
    factors = {'L0_conv_Wq_pw': 8.0,
     'L0_conv_bq_pw': 8.0,
     'L0_conv_Wq_conv': 8.0,
     'L0_conv_bq_conv': 8.0,
     'L0_conv_Wk_pw': 8.0,
     'L0_conv_bk_pw': 8.0,
     'L0_conv_Wk_conv': 8.0,
     'L0_conv_bk_conv': 8.0,
     'L0_conv_Wv_pw': 8.0,
     'L0_conv_bv_pw': 8.0,
     'L0_conv_Wv_conv': 8.0,
     'L0_conv_bv_conv': 8.0,
     'L0_conv_Wo_pw': 8.0,
     'L0_conv_Wo_dw': 8.0,
     'L1_conv_x_proj_w': 3.567,
     'L1_conv_dt_proj_w': 8.0,
     'L1_conv_A_log': 4.78,
     'L1_conv_pw1_w': 6.684,
     'L1_conv_pw2_w': 5.392}
    for name, (base, spread) in spreads.items():
        noise = np.random.default_rng([zlib.crc32(name.encode()), seed]).standard_normal(out[name].shape)
        drawn = base * np.exp(spread * noise) if base else spread * noise
        out[name] = jnp.asarray(drawn.astype(out[name].dtype))
    for name, factor in factors.items():
        out[name] = (out[name] * factor).astype(out[name].dtype)
    return out
```

```python
import numpy as np

import concourse.bass as bass
from concourse import mybir
from contextlib import ExitStack

F32 = mybir.dt.float32
F32R = mybir.dt.float32r
ALU = mybir.AluOpType
ACT = mybir.ActivationFunctionType
AX = mybir.AxisListType

P = 128
C = 8
H = 256
W = 1024
HT = H // P
NW = 512
HALVES = W // NW
HB = P // C
NB = H // HB
GROUP = 2
NG = C // GROUP
HEADS = 8
D = H // HEADS
NH = C * HEADS
KT = W // P
DI = 512
DT = DI // P
DS = 16
RANK = 16
TAPS = 4
CT = 3
HID = 4096
MT = HID // P
CD = C * H
KD = CD // P
EPS = 1e-5


class Scope:

    def __init__(self, nc, stack, name):
        self.nc, self.stack, self.name, self.own = nc, stack, name, []
        stack.callback(self.give_back)

    def give_back(self):
        self.nc.all_engine_barrier()
        self.nc.clear_and_free_semaphores(self.own)
        self.nc.all_engine_barrier()

    def sb(self, name, shape, dt=F32):
        return self.stack.enter_context(self.nc.sbuf_tensor(f"{self.name}_{name}", shape, dt))

    def ps(self, name, shape, dt=F32):
        return self.stack.enter_context(self.nc.psum_tensor(f"{self.name}_{name}", shape, dt))

    def sem(self, name):
        self.own.append(self.nc.alloc_semaphore(f"{self.name}_{name}"))
        return self.own[-1]

    def sems(self, name, n):
        return [self.sem(f"{name}{i}") for i in range(n)]


class Chain:

    def __init__(self, eng, sem, base=0):
        self.eng, self.sem, self.base, self.n = eng, sem, base, 0

    def link(self, ins):
        self.n += 1
        ins.then_inc(self.sem, 1)
        self.eng.wait_ge(self.sem, self.base + self.n)


def halves(t):
    return [slice(i * NW, (i + 1) * NW) for i in range(HALVES)]


def stage_project(nc, x, w_qkv, y):
    with ExitStack() as stack:
        s_ = Scope(nc, stack, "project")
        X = s_.sb("x", [P, C, HT, W])
        WB = HT * H
        NWT = 3 * WB + 3 * HT
        w = [s_.sb(f"w{s}", [P, NWT]) for s in range(2)]
        xn = [s_.sb(f"xn{s}", [P, HT, W]) for s in range(2)]
        ybuf = [s_.sb(f"y{s}", [P, W]) for s in range(4)]
        stats = s_.sb("stats", [P, C, 4, 6])
        mv = s_.sb("mv", [P, NG, 2])
        avg = s_.sb("avg", [P, P])
        mean = s_.sb("mean", [P, NG])
        dev = s_.sb("dev", [P, NG])
        var = s_.sb("var", [P, NG])
        rstd = s_.sb("rstd", [P, NG])
        shift = s_.sb("shift", [P, NG])
        epsc = s_.sb("eps", [P, 1])
        acc = [s_.ps(f"acc{k}", [P, W]) for k in range(4)]
        x_loaded = s_.sems("x_loaded", C)
        w_loaded = s_.sems("w_loaded", 2)
        dve = s_.sem("dve")
        stat_ready, stat_summed = s_.sem("stat_ready"), s_.sem("stat_summed")
        var_ready, sd_ready, norm_ready = s_.sem("var_ready"), s_.sem("sd_ready"), s_.sem("norm_ready")
        xn_ready = s_.sem("xn_ready")
        multiplied = s_.sem("multiplied")
        biased = s_.sem("biased")
        stored = s_.sems("stored", 4)
        TILES = 3 * HT

        with nc.Block() as block:
            @block.sync
            def _(sp):
                for c in range(C):
                    sp.dma_start(X[:, c], x[0, c].rearrange("(k p) w -> p k w", p=P)).then_inc(x_loaded[c], 16)
                for s in range(2):
                    sp.dma_start(w[s][:, :], w_qkv[s]).then_inc(w_loaded[s], 16)

                def store(c, i, s):
                    for n in range(TILES):
                        k = s * TILES + n
                        sp.wait_ge(biased, c * TILES + n + 1)
                        sp.dma_start(y[n // HT, c, (n % HT) * P:(n % HT + 1) * P, :],
                                     ybuf[k % 4][:, :]).then_inc(stored[k % 4], 16)

                with sp.Fori(0, C // 2 - 1) as i:
                    for s in range(2):
                        store(2 * i + s, i, s)
                        sp.dma_start(w[s][:, :], w_qkv[2 * i + 2 + s]).then_inc(w_loaded[s], 16)
                for s in range(2):
                    store(C - 2 + s, C // 2 - 1, s)
                for k in range(4):
                    sp.wait_ge(stored[k], 16 * (C * TILES // 4))

            @block.vector
            def _(v):
                nc.vector.memset(avg[:, :], 1.0 / P).then_inc(dve, 1)
                nc.vector.memset(epsc[:, :], EPS).then_inc(dve, 1)
                for c in range(C):
                    v.wait_ge(x_loaded[c], 16)
                    for q in range(4):
                        nc.vector.bn_stats(stats[:, c, q], X[:, c, q // 2, (q % 2) * NW:(q % 2 + 1) * NW]).then_inc(dve, 1)
                chain = Chain(v, dve, 2 + 4 * C)
                v.wait_ge(dve, 2 + 4 * C)
                for g in range(NG):
                    chain.link(nc.vector.bn_aggr(mv[:, g], stats[:, GROUP * g:GROUP * (g + 1)].rearrange("p c q s -> p (c q s)")))
                v.sem_inc(stat_ready, 1)
                v.wait_ge(stat_summed, 1)
                chain.link(nc.vector.tensor_copy(mean[:, :], acc[0][:, 0:NG]))
                chain.link(nc.vector.tensor_tensor(dev[:, :], mv[:, :, 0], mean[:, :], ALU.subtract))
                chain.link(nc.vector.tensor_tensor(dev[:, :], dev[:, :], dev[:, :], ALU.mult))
                nc.vector.tensor_tensor(var[:, :], dev[:, :], mv[:, :, 1], ALU.add).then_inc(var_ready, 1)
                v.wait_ge(sd_ready, 1)
                chain.link(nc.vector.reciprocal(rstd[:, :], dev[:, :]))
                nc.vector.scalar_tensor_tensor(shift[:, :], mean[:, :], -1.0, rstd[:, :], ALU.mult, ALU.mult).then_inc(norm_ready, 1)
                v.wait_ge(norm_ready, 1)
                with v.Fori(0, C // 2) as i:
                    for s in range(2):
                        v.wait_ge(multiplied, i * (2 * TILES))
                        nc.vector.tensor_scalar(xn[s][:, :, :], X[:, bass.ds(2 * i + s, 1)].rearrange("p o k w -> p (o k) w"),
                                                rstd[:, bass.ds(i, 1)], shift[:, bass.ds(i, 1)],
                                                ALU.mult, ALU.add).then_inc(xn_ready, 1)

            @block.tensor
            def _(pe):
                pe.wait_ge(stat_ready, 1)
                nc.tensor.matmul(acc[0][:, 0:NG], avg[:, :], mv[:, :, 0], start=True, stop=True).then_inc(stat_summed, 1)
                pe.wait_ge(var_ready, 1)
                nc.tensor.matmul(acc[1][:, 0:NG], avg[:, :], var[:, :], start=True, stop=True).then_inc(stat_summed, 1)
                pe.wait_ge(norm_ready, 1)
                with pe.Fori(0, C // 2) as i:
                    for s in range(2):
                        pe.wait_ge(w_loaded[s], 16 * i + 16)
                        pe.wait_ge(xn_ready, 2 * i + s + 1)
                        for n in range(TILES):
                            k = s * TILES + n
                            if k >= 4:
                                pe.wait_ge(biased, i * 2 * TILES + k - 3)
                            else:
                                pe.wait_ge(biased, i * 2 * TILES)
                            a = acc[k % 4]
                            for h in halves(a):
                                for kt in range(HT):
                                    o = (n // HT) * WB + kt * H + (n % HT) * P
                                    last = nc.tensor.matmul(a[:, h], w[s][:, o:o + P], xn[s][:, kt, h],
                                                            start=kt == 0, stop=kt == HT - 1)
                            last.then_inc(multiplied, 1)

            @block.scalar
            def _(act):
                act.wait_ge(stat_summed, 2)
                nc.scalar.activation(dev[:, :], acc[1][:, 0:NG], ACT.Sqrt, bias=epsc[:, :]).then_inc(sd_ready, 1)
                with act.Fori(0, C // 2) as i:
                    for s in range(2):
                        for n in range(TILES):
                            k = s * TILES + n
                            act.wait_ge(multiplied, i * 2 * TILES + k + 1)
                            act.wait_ge(stored[k % 4], 16 * (i * (2 * TILES // 4) + k // 4))
                            nc.scalar.activation(ybuf[k % 4][:, :], acc[k % 4][:, :], ACT.Identity,
                                                 bias=w[s][:, 3 * WB + n:3 * WB + n + 1]).then_inc(biased, 1)


def stage_convolve(nc, y, kron_d, cbias_d, vbias_d, rot_d, cos_d, sin_d, q_parts, k_parts, v_heads):
    with ExitStack() as stack:
        s_ = Scope(nc, stack, "conv")
        kron = s_.sb("kron", [P, 3, CT, P])
        cbias = s_.sb("cbias", [P, 2])
        vbias = s_.sb("vbias", [P, P])
        rot = s_.sb("rot", [P, P])
        cos = s_.sb("cos", [P, 2, W])
        sin = s_.sb("sin", [P, 2, W])
        yin = [[s_.sb(f"y{s}{n}", [P, W + 2]) for n in range(3)] for s in range(2)]
        qk = [s_.sb(f"qk{n}", [P, W]) for n in range(2)]
        turned = [s_.sb(f"turned{n}", [P, W]) for n in range(2)]
        kept = [s_.sb(f"kept{n}", [P, W]) for n in range(2)]
        hi = [s_.sb(f"hi{n}", [P, W], F32R) for n in range(2)]
        lo = [s_.sb(f"lo{n}", [P, W], F32R) for n in range(2)]
        vst = s_.sb("vst", [P, C, KT, 2 * HB])
        conv_ps = [s_.ps(f"conv{n}", [P, W]) for n in range(2)]
        rot_ps = s_.ps("turned", [P, W])
        v_ps = s_.ps("v", [P, W])
        consts = s_.sem("consts")
        padded = s_.sem("padded")
        y_loaded = [s_.sems(f"y_loaded{s}", 3) for s in range(2)]
        conv_done = s_.sem("conv_done")
        v_done = s_.sem("v_done")
        rot_done = s_.sem("rot_done")
        qk_ready = s_.sem("qk_ready")
        turn_taken = s_.sem("turn_taken")
        kept_ready = s_.sem("kept_ready")
        sum_ready = s_.sem("sum_ready")
        hi_ready = s_.sem("hi_ready")
        lo_ready = s_.sem("lo_ready")
        v_taken = s_.sem("v_taken")
        hi_stored, lo_stored = s_.sems("hi_stored", 2), s_.sems("lo_stored", 2)
        v_stored = s_.sem("v_stored")
        parts = [q_parts, k_parts]

        def rows(t, j):
            return t.rearrange("(c b r) w -> b c r w", c=C, r=HB)[j]

        with nc.Block() as block:
            @block.sync
            def _(sp):
                for dst, src in ((kron[:, :, :, :], kron_d), (cbias[:, :], cbias_d), (vbias[:, :], vbias_d),
                                 (rot[:, :], rot_d), (cos[:, :, :], cos_d), (sin[:, :, :], sin_d)):
                    sp.dma_start(dst, src).then_inc(consts, 16)
                sp.wait_ge(padded, 12)

                def load(j, s):
                    for n in range(3):
                        sp.dma_start(yin[s][n][:, 1:W + 1], y[n].rearrange("c (b r) w -> b c r w", r=HB)[j]).then_inc(y_loaded[s][n], 16)

                for s in range(2):
                    load(s, s)
                with sp.Fori(0, NB // 2 - 1) as i:
                    for s in range(2):
                        sp.wait_ge(conv_done, 4 * i + 2 * s + 2)
                        sp.wait_ge(v_done, 2 * i + s + 1)
                        load(2 * i + 2 + s, s)

            @block.gpsimd
            def _(gp):
                for s in range(2):
                    for n in range(3):
                        nc.gpsimd.memset(yin[s][n][:, 0:1], 0.0).then_inc(padded, 1)
                        nc.gpsimd.memset(yin[s][n][:, W + 1:W + 2], 0.0).then_inc(padded, 1)
                gp.wait_ge(consts, 96)
                with gp.Fori(0, NB // 2) as i:
                    for s in range(2):
                        for n in range(2):
                            m = 2 * s + n
                            gp.wait_ge(qk_ready, 4 * i + m + 1)
                            gp.wait_ge(sum_ready, 4 * i + m - 1 if m >= 1 else 4 * i)
                            nc.gpsimd.tensor_tensor(kept[n][:, :], qk[n][:, :], cos[:, s], ALU.mult).then_inc(kept_ready, 1)

            @block.tensor
            def _(pe):
                pe.wait_ge(consts, 96)
                with pe.Fori(0, NB // 2) as i:
                    for s in range(2):
                        for n in range(2):
                            m = 2 * s + n
                            pe.wait_ge(y_loaded[s][n], 16 * i + 16)
                            pe.wait_ge(qk_ready, 4 * i + m - 1 if m >= 1 else 4 * i)
                            for h in range(HALVES):
                                for t in range(CT):
                                    last = nc.tensor.matmul(conv_ps[n][:, h * NW:(h + 1) * NW], kron[:, n, t],
                                                            yin[s][n][:, h * NW + t:h * NW + t + NW],
                                                            start=t == 0, stop=t == CT - 1)
                            last.then_inc(conv_done, 1)
                        pe.wait_ge(y_loaded[s][2], 16 * i + 16)
                        pe.wait_ge(v_taken, 2 * i + s)
                        for wt in range(KT):
                            for t in range(CT):
                                last = nc.tensor.matmul(v_ps[:, wt * P:(wt + 1) * P], yin[s][2][:, wt * P + t:wt * P + t + P],
                                                        kron[:, 2, t], start=t == 0, stop=t == CT - 1)
                        last.then_inc(v_done, 1)
                        for n in range(2):
                            m = 2 * s + n
                            pe.wait_ge(qk_ready, 4 * i + m + 1)
                            pe.wait_ge(turn_taken, 4 * i + m)
                            for h in range(HALVES):
                                last = nc.tensor.matmul(rot_ps[:, h * NW:(h + 1) * NW], rot[:, :], qk[n][:, h * NW:(h + 1) * NW],
                                                        start=True, stop=True)
                            last.then_inc(rot_done, 1)

            @block.scalar
            def _(act):
                act.wait_ge(consts, 96)

                def biases(i, s):
                    for n in range(2):
                        m = 2 * s + n
                        act.wait_ge(conv_done, 4 * i + m + 1)
                        if m >= 2:
                            act.wait_ge(rot_done, 4 * i + m - 1)
                            act.wait_ge(kept_ready, 4 * i + m - 1)
                        else:
                            act.wait_ge(rot_done, 4 * i)
                            act.wait_ge(kept_ready, 4 * i)
                        nc.scalar.activation(qk[n][:, :], conv_ps[n][:, :], ACT.Identity, bias=cbias[:, n:n + 1]).then_inc(qk_ready, 1)

                with act.Fori(0, NB // 2) as i:
                    for s in range(2):
                        biases(i, s)
                        for n in range(2):
                            m = 2 * s + n
                            act.wait_ge(sum_ready, 4 * i + m + 1)
                            act.wait_ge(hi_stored[n], 16 * (2 * i + s))
                            act.wait_ge(lo_ready, 4 * i + m)
                            nc.scalar.activation(hi[n][:, :], turned[n][:, :], ACT.Copy).then_inc(hi_ready, 1)
                            act.wait_ge(hi_ready, 4 * i + m + 1)
                            act.dma_start(rows(parts[n][0], 2 * i + s), hi[n][:, :].bitcast(F32)).then_inc(hi_stored[n], 16)
                            act.wait_ge(lo_ready, 4 * i + m + 1)
                            act.dma_start(rows(parts[n][1], 2 * i + s), lo[n][:, :].bitcast(F32)).then_inc(lo_stored[n], 16)
                    act.wait_ge(v_taken, 2 * i + 2)
                    for c in range(C):
                        act.dma_start(v_heads[HEADS * c + i], vst[:, c].rearrange("p t d -> p (t d)")).then_inc(v_stored, 16)
                for n in range(2):
                    act.wait_ge(hi_stored[n], 16 * NB)
                    act.wait_ge(lo_stored[n], 16 * NB)
                act.wait_ge(v_stored, 16 * C * (NB // 2))

            @block.vector
            def _(v):
                v.wait_ge(consts, 96)
                with v.Fori(0, NB // 2) as i:
                    for s in range(2):
                        v.wait_ge(v_done, 2 * i + s + 1)
                        v.wait_ge(v_stored, 16 * C * i)
                        nc.vector.tensor_tensor(
                            vst[:, :, :, s * HB:(s + 1) * HB].rearrange("p c t r -> p t c r"),
                            v_ps[:, :].rearrange("p (t c r) -> p t c r", t=KT, c=C),
                            vbias[:, :].rearrange("p (o c r) -> p o c r", o=1, c=C).broadcast_to([P, KT, C, HB]),
                            ALU.add).then_inc(v_taken, 1)
                        for n in range(2):
                            m = 2 * s + n
                            v.wait_ge(rot_done, 4 * i + m + 1)
                            v.wait_ge(hi_ready, 4 * i + m - 1 if m >= 1 else 4 * i)
                            nc.vector.tensor_tensor(turned[n][:, :], rot_ps[:, :], sin[:, s], ALU.mult).then_inc(turn_taken, 1)
                            v.wait_ge(turn_taken, 4 * i + m + 1)
                            v.wait_ge(kept_ready, 4 * i + m + 1)
                            nc.vector.tensor_tensor(turned[n][:, :], turned[n][:, :], kept[n][:, :], ALU.add).then_inc(sum_ready, 1)
                            v.wait_ge(hi_ready, 4 * i + m + 1)
                            v.wait_ge(lo_stored[n], 16 * (2 * i + s))
                            nc.vector.tensor_tensor(lo[n][:, :], turned[n][:, :], hi[n][:, :].bitcast(F32), ALU.subtract).then_inc(lo_ready, 1)


def stage_attend(nc, q_parts, k_parts, v_heads, ident_d, mask_d, att, den):
    with ExitStack() as stack:
        s_ = Scope(nc, stack, "attend")
        SLOTS = 4
        Q = [s_.sb(f"q{s}", [P, W], F32R) for s in range(SLOTS)]
        K = [s_.sb(f"k{s}", [P, W], F32R) for s in range(SLOTS)]
        V = [s_.sb(f"v{s}", [P, KT * D]) for s in range(SLOTS)]
        PT = [s_.sb(f"probs{t}", [P, W]) for t in range(2)]
        shift = [s_.sb(f"shift{t}", [P, W], F32R) for t in range(2)]
        osb = [s_.sb(f"o{s}", [P, NW]) for s in range(SLOTS)]
        nm = s_.sb("negmax", [P, KT])
        m16 = s_.sb("maxparts", [P, 2 * KT], F32R)
        ident = s_.sb("ident", [P, P])
        mask = s_.sb("mask", [2 * KT, KT, P])
        ones = s_.sb("ones", [P, D])
        onesf = s_.sb("onesf", [P, P])
        onesr = s_.sb("onesr", [P, P], F32R)
        zeros = s_.sb("zeros", [P, W])
        row_ps = s_.ps("rows", [P, W])
        st_ps = [s_.ps(f"cols{t}", [P, W]) for t in range(2)]
        o_ps = [s_.ps(f"out{t}", [P, NW]) for t in range(2)]
        consts = s_.sem("consts")
        set_up = s_.sem("set_up")
        loaded = s_.sems("loaded", SLOTS)
        row_ready = s_.sem("row_ready")
        row_taken = s_.sem("row_taken")
        max_split = s_.sem("max_split")
        dve = s_.sem("dve")
        st_ready = s_.sem("st_ready")
        exp_done = s_.sem("exp_done")
        pv_done = s_.sem("pv_done")
        o_copied = s_.sem("o_copied")
        stored = s_.sems("stored", SLOTS)
        PER = KT + 1

        with nc.Block() as block:
            @block.sync
            def _(sp):
                sp.dma_start(ident[:, :], ident_d).then_inc(consts, 16)
                sp.dma_start(mask[:, :, :], mask_d).then_inc(consts, 16)

                def load(h, s):
                    q = Q[s][:, :].bitcast(F32)
                    k = K[s][:, :].bitcast(F32)
                    qs = q_parts.rearrange("a (h d) w -> h a d w", d=D)[h]
                    ks = k_parts.rearrange("a (h d) w -> h a d w", d=D)[h]
                    sp.dma_start(q[0:2 * D, :], qs).then_inc(loaded[s], 16)
                    sp.dma_start(k[0:2 * D, :], ks).then_inc(loaded[s], 16)
                    sp.dma_start(k[2 * D:4 * D, :], ks).then_inc(loaded[s], 16)
                    sp.dma_start(q[2 * D:3 * D, :], qs[1]).then_inc(loaded[s], 16)
                    sp.dma_start(q[3 * D:4 * D, :], qs[0]).then_inc(loaded[s], 16)
                    sp.dma_start(V[s][:, :], v_heads[h]).then_inc(loaded[s], 16)

                def store(h, s):
                    sp.wait_ge(o_copied, h + 3)
                    for half in range(HALVES):
                        r = 2 * D * half
                        sp.dma_start(att[h, :, half * NW:(half + 1) * NW], osb[s][r:r + D, :]).then_inc(stored[s], 16)
                        sp.dma_start(den[bass.ds(h, 1) if not isinstance(h, int) else slice(h, h + 1), half * NW:(half + 1) * NW],
                                     osb[s][r + D:r + D + 1, :]).then_inc(stored[s], 16)

                for s in range(SLOTS):
                    load(s, s)
                with sp.Fori(0, NH // SLOTS - 1) as i:
                    for s in range(SLOTS):
                        h = SLOTS * i + s
                        sp.wait_ge(pv_done, KT * (h + 1))
                        load(h + SLOTS, s)
                        store(h, s)
                for s in range(SLOTS):
                    store(NH - SLOTS + s, s)
                for s in range(SLOTS):
                    sp.wait_ge(stored[s], 64 * (NH // SLOTS))

            @block.gpsimd
            def _(gp):
                nc.gpsimd.memset(ones[:, :], 1.0).then_inc(set_up, 1)

            def on_heads(eng, head):
                with eng.Fori(0, NH // SLOTS - 1) as i:
                    for s in range(SLOTS):
                        head(SLOTS * i + s, i, s, True)
                for s in range(SLOTS):
                    head(NH - SLOTS + s, NH // SLOTS - 1, s, s < SLOTS - 1)

            @block.tensor
            def _(pe):
                pe.wait_ge(consts, 32)
                pe.wait_ge(set_up, 4)

                def row_scores(h, s, j):
                    pe.wait_ge(row_taken, PER * h + j)
                    if j < KT:
                        for half in halves(row_ps):
                            last = nc.tensor.matmul(row_ps[:, half], Q[s][:, j * P:(j + 1) * P], K[s][:, half], start=True, stop=True)
                    else:
                        pe.wait_ge(max_split, h + 1)
                        last = nc.tensor.matmul(row_ps[0:2 * KT, 0:P], m16[:, :].bitcast(F32), ident[:, :], start=True, stop=True)
                    last.then_inc(row_ready, 1)

                def values(h, s, t):
                    pe.wait_ge(exp_done, KT * h + t + 1)
                    for half in range(HALVES):
                        for sums in range(2):
                            g = D * (2 * half + sums)
                            lhs = ones[:, :] if sums else V[s][:, t * D:(t + 1) * D]
                            last = nc.tensor.matmul(o_ps[s % 2][g:g + D, :], lhs, PT[t % 2][:, half * NW:(half + 1) * NW],
                                                    start=t == 0, stop=t == KT - 1)
                    last.then_inc(pv_done, 1)

                AHEAD = {0: (0, 1), 1: (2, 3), 2: (4, 5), 3: (6,), 4: (7,), 6: (KT,)}

                def head(h, i, s, following):
                    nh, ns, ni = h + 1, (s + 1) % SLOTS, i + (s + 1) // SLOTS
                    if following:
                        pe.wait_ge(loaded[ns], 96 * (ni + 1))
                    pe.wait_ge(row_taken, PER * (h + 1))
                    for t in range(KT):
                        for half in halves(st_ps[0]):
                            nc.tensor.matmul(st_ps[t % 2][:, half], K[s][:, t * P:(t + 1) * P], Q[s][:, half], start=True, stop=False)
                            last = nc.tensor.matmul(st_ps[t % 2][:, half], onesr[:, :], shift[s % 2][:, half], start=False, stop=True)
                        last.then_inc(st_ready, 1)
                        ahead = AHEAD.get(t, ()) if following else ()
                        for j in ahead[:1]:
                            row_scores(nh, ns, j)
                        if t >= 1:
                            if t == 1:
                                pe.wait_ge(o_copied, h + 1)
                            values(h, s, t - 1)
                        for j in ahead[1:]:
                            row_scores(nh, ns, j)
                    values(h, s, KT - 1)

                pe.wait_ge(loaded[0], 96)
                for j in range(PER):
                    row_scores(0, 0, j)
                on_heads(pe, head)

            @block.scalar
            def _(act):
                def head(h, i, s, following):
                    for t in range(KT):
                        act.wait_ge(st_ready, KT * h + t + 1)
                        nc.scalar.activation(PT[t % 2][:, :], st_ps[t % 2][:, :], ACT.Exp,
                                             scale=float(H) ** -0.5).then_inc(exp_done, 1)
                on_heads(act, head)

            @block.vector
            def _(v):
                for t in range(2):
                    nc.vector.memset(shift[t][:, :].bitcast(mybir.dt.uint32), 0).then_inc(set_up, 1)
                nc.vector.memset(onesf[:, :], 1.0).then_inc(dve, 1)
                v.wait_ge(dve, 1)
                nc.vector.tensor_copy(onesr[:, :], onesf[:, :]).then_inc(set_up, 1)
                v.sem_inc(o_copied, 2)
                v.wait_ge(consts, 32)

                def maximum(h, s):
                    for j in range(KT):
                        v.wait_ge(row_ready, PER * h + j + 1)
                        nc.vector.tensor_reduce(nm[:, j:j + 1], row_ps[:, :], AX.X, ALU.max, negate=True).then_inc(row_taken, 1)
                    v.wait_ge(row_taken, PER * h + KT)
                    nc.vector.tensor_copy(m16[:, 0:KT], nm[:, :]).then_inc(dve, 1)
                    v.wait_ge(dve, h + 2)
                    nc.vector.tensor_tensor(m16[:, KT:2 * KT], nm[:, :], m16[:, 0:KT].bitcast(F32), ALU.subtract).then_inc(max_split, 1)
                    v.wait_ge(row_ready, PER * (h + 1))
                    nc.vector.tensor_tensor(shift[s % 2][0:2 * KT, :].rearrange("r (t q) -> r t q", t=KT),
                                            row_ps[0:2 * KT, 0:P].rearrange("r (o q) -> r o q", o=1).broadcast_to([2 * KT, KT, P]),
                                            mask[:, :, :], ALU.mult).then_inc(row_taken, 1)

                def head(h, i, s, following):
                    if following:
                        maximum(h + 1, (s + 1) % SLOTS)
                    v.wait_ge(pv_done, KT * (h + 1))
                    v.wait_ge(stored[s], 64 * i)
                    nc.vector.tensor_copy(osb[s][:, :], o_ps[s % 2][:, :]).then_inc(o_copied, 1)

                maximum(0, 0)
                on_heads(v, head)


def stage_recombine(nc, att, den, rden, wo_d, mixed):
    with ExitStack() as stack:
        s_ = Scope(nc, stack, "recombine")
        dsb = s_.sb("den", [P, NW])
        rsb = s_.sb("rden", [P, NW])
        a = [s_.sb(f"a{s}", [P, HT, W]) for s in range(2)]
        r = [s_.sb(f"r{s}", [P, HT, W]) for s in range(2)]
        w = [s_.sb(f"w{s}", [P, HT, H]) for s in range(2)]
        out = [s_.sb(f"out{k}", [P, W]) for k in range(4)]
        acc = [s_.ps(f"acc{k}", [P, W]) for k in range(4)]
        den_loaded, inverted, inverse_stored = s_.sem("den_loaded"), s_.sem("inverted"), s_.sem("inverse_stored")
        loaded = s_.sems("loaded", 2)
        divided, multiplied, copied = s_.sem("divided"), s_.sem("multiplied"), s_.sem("copied")
        stored = s_.sems("stored", 4)
        N4 = P // D

        with nc.Block() as block:
            @block.sync
            def _(sp):
                view = lambda t: t.rearrange("h (a w) -> (h a) w", a=HALVES)
                sp.dma_start(dsb[:, :], view(den)).then_inc(den_loaded, 16)
                sp.wait_ge(inverted, 1)
                sp.dma_start(view(rden), rsb[:, :]).then_inc(inverse_stored, 16)
                sp.wait_ge(inverse_stored, 16)

                def load(c, s):
                    sp.dma_start(a[s][:, :, :], att.rearrange("(c k n) d w -> c (n d) k w", c=C, k=HT)[c]).then_inc(loaded[s], 16)
                    sp.dma_start(w[s][:, :, :], wo_d[c]).then_inc(loaded[s], 16)
                    for k in range(HT):
                        src = rden.rearrange("(c k n o) w -> c k n o w", c=C, k=HT, o=1)[c, k]
                        sp.dma_start(r[s][:, k, :], src.broadcast_to([N4, D, W])).then_inc(loaded[s], 16)

                def store(c, s):
                    for g in range(HT):
                        k = HT * s + g
                        sp.wait_ge(copied, HT * c + g + 1)
                        sp.dma_start(mixed[c, g * P:(g + 1) * P, :], out[k][:, :]).then_inc(stored[k], 16)

                for s in range(2):
                    load(s, s)
                with sp.Fori(0, C // 2 - 1) as i:
                    for s in range(2):
                        store(2 * i + s, s)
                        load(2 * i + s + 2, s)
                for s in range(2):
                    store(C - 2 + s, s)
                for k in range(4):
                    sp.wait_ge(stored[k], 16 * (C // 2))

            @block.vector
            def _(v):
                v.wait_ge(den_loaded, 16)
                nc.vector.reciprocal(rsb[:, :], dsb[:, :]).then_inc(inverted, 1)
                with v.Fori(0, C // 2) as i:
                    for s in range(2):
                        v.wait_ge(loaded[s], 64 * i + 64)
                        nc.vector.tensor_tensor(a[s][:, :, :], a[s][:, :, :], r[s][:, :, :], ALU.mult).then_inc(divided, 1)

            @block.tensor
            def _(pe):
                with pe.Fori(0, C // 2) as i:
                    for s in range(2):
                        pe.wait_ge(divided, 2 * i + s + 1)
                        pe.wait_ge(copied, 4 * i)
                        for g in range(HT):
                            for half in range(HALVES):
                                for k in range(HT):
                                    last = nc.tensor.matmul(acc[HT * s + g][:, half * NW:(half + 1) * NW], w[s][:, k, g * P:(g + 1) * P],
                                                            a[s][:, k, half * NW:(half + 1) * NW], start=k == 0, stop=k == HT - 1)
                            last.then_inc(multiplied, 1)

            @block.scalar
            def _(act):
                with act.Fori(0, C // 2) as i:
                    for k in range(4):
                        act.wait_ge(multiplied, 4 * i + k + 1)
                        act.wait_ge(stored[k], 16 * i)
                        nc.scalar.activation(out[k][:, :], acc[k][:, :], ACT.Copy).then_inc(copied, 1)


def stage_mix(nc, mixed, kmix_d, x, gavg_d, sel_d, x1, norm):
    with ExitStack() as stack:
        s_ = Scope(nc, stack, "mix")
        kmix = s_.sb("kmix", [P, P])
        gavg = s_.sb("gavg", [P, P])
        sel = s_.sb("sel", [P, C])
        ones = s_.sb("ones", [P, P])
        eps = s_.sb("eps", [P, 1])
        a = [s_.sb(f"a{s}", [P, W]) for s in range(2)]
        xb = [s_.sb(f"x{s}", [P, W]) for s in range(2)]
        out = [s_.sb(f"out{s}", [P, W]) for s in range(2)]
        stats = s_.sb("stats", [P, NB * HALVES, 6])
        mv = s_.sb("mv", [P, 2])
        dev = s_.sb("dev", [P, 1])
        var = s_.sb("var", [P, 1])
        both = s_.sb("both", [P, 2])
        spread = s_.sb("spread", [P, 2, C])
        acc = [s_.ps(f"acc{s}", [P, W]) for s in range(2)]
        small = [s_.ps(f"small{k}", [P, NW]) for k in range(3)]
        consts = s_.sem("consts")
        loaded = s_.sems("loaded", 2)
        multiplied, added, measured = s_.sem("multiplied"), s_.sem("added"), s_.sem("measured")
        stored = s_.sems("stored", 2)
        dve, stat_ready, summed, sd_ready = s_.sem("dve"), s_.sem("stat_ready"), s_.sem("summed"), s_.sem("sd_ready")

        with nc.Block() as block:
            @block.sync
            def _(sp):
                for dst, src in ((kmix[:, :], kmix_d), (gavg[:, :], gavg_d), (sel[:, :], sel_d)):
                    sp.dma_start(dst, src).then_inc(consts, 16)

                def load(j, s):
                    sp.dma_start(a[s][:, :], mixed.rearrange("c (b r) w -> b c r w", r=HB)[j]).then_inc(loaded[s], 16)
                    sp.dma_start(xb[s][:, :], x[0].rearrange("c (b r) w -> b c r w", r=HB)[j]).then_inc(loaded[s], 16)

                def store(j, s):
                    sp.wait_ge(added, j + 1)
                    sp.dma_start(x1.rearrange("c (b r) w -> b c r w", r=HB)[j], out[s][:, :]).then_inc(stored[s], 16)

                for s in range(2):
                    load(s, s)
                with sp.Fori(0, NB // 2 - 1) as i:
                    for s in range(2):
                        store(2 * i + s, s)
                        load(2 * i + s + 2, s)
                for s in range(2):
                    store(NB - 2 + s, s)
                for s in range(2):
                    sp.wait_ge(stored[s], 16 * (NB // 2))

            @block.tensor
            def _(pe):
                pe.wait_ge(consts, 48)
                with pe.Fori(0, NB // 2) as i:
                    for s in range(2):
                        pe.wait_ge(loaded[s], 32 * i + 32)
                        pe.wait_ge(added, 2 * i)
                        for half in range(HALVES):
                            last = nc.tensor.matmul(acc[s][:, half * NW:(half + 1) * NW], kmix[:, :], a[s][:, half * NW:(half + 1) * NW],
                                                    start=True, stop=True)
                        last.then_inc(multiplied, 1)
                pe.wait_ge(stat_ready, 1)
                nc.tensor.matmul(small[0][:, 0:1], gavg[:, :], mv[:, 0:1], start=True, stop=True).then_inc(summed, 1)
                pe.wait_ge(stat_ready, 2)
                nc.tensor.matmul(small[1][:, 0:1], gavg[:, :], var[:, :], start=True, stop=True).then_inc(summed, 1)
                pe.wait_ge(stat_ready, 3)
                nc.tensor.matmul(small[2][:, 0:2 * C], ones[:, :], spread[:, :, :].rearrange("p a c -> p (a c)"),
                                 start=True, stop=True).then_inc(summed, 1)

            @block.scalar
            def _(act):
                act.wait_ge(summed, 2)
                nc.scalar.activation(dev[:, :], small[1][:, 0:1], ACT.Sqrt, bias=eps[:, :]).then_inc(sd_ready, 1)

            @block.vector
            def _(v):
                nc.vector.memset(ones[:, :], 1.0)
                nc.vector.memset(eps[:, :], EPS)
                with v.Fori(0, NB // 2) as i:
                    for s in range(2):
                        v.wait_ge(multiplied, 2 * i + s + 1)
                        v.wait_ge(stored[s], 16 * i)
                        nc.vector.tensor_tensor(out[s][:, :], acc[s][:, :], xb[s][:, :], ALU.add).then_inc(added, 1)
                        v.wait_ge(added, 2 * i + s + 1)
                        for half in range(HALVES):
                            nc.vector.bn_stats(stats[:, bass.ds(4 * i + 2 * s + half, 1)].rearrange("p o k -> p (o k)"),
                                               out[s][:, half * NW:(half + 1) * NW]).then_inc(measured, 1)
                v.wait_ge(measured, 2 * NB)
                v.wait_ge(consts, 48)
                chain = Chain(v, dve)
                chain.link(nc.vector.bn_aggr(mv[:, :], stats[:, :, :].rearrange("p q k -> p (q k)")))
                v.sem_inc(stat_ready, 1)
                v.wait_ge(summed, 1)
                chain.link(nc.vector.tensor_copy(both[:, 1:2], small[0][:, 0:1]))
                chain.link(nc.vector.tensor_tensor(dev[:, :], mv[:, 0:1], both[:, 1:2], ALU.subtract))
                chain.link(nc.vector.tensor_tensor(dev[:, :], dev[:, :], dev[:, :], ALU.mult))
                chain.link(nc.vector.tensor_tensor(var[:, :], dev[:, :], mv[:, 1:2], ALU.add))
                v.sem_inc(stat_ready, 1)
                v.wait_ge(sd_ready, 1)
                chain.link(nc.vector.reciprocal(both[:, 0:1], dev[:, :]))
                chain.link(nc.vector.scalar_tensor_tensor(both[:, 1:2], both[:, 1:2], -1.0, both[:, 0:1], ALU.mult, ALU.mult))
                for k in range(2):
                    chain.link(nc.vector.tensor_scalar(spread[:, k], sel[:, :], both[:, k:k + 1], None, ALU.mult))
                v.sem_inc(stat_ready, 1)
                v.wait_ge(summed, 3)
                chain.link(nc.vector.tensor_copy(norm[:, :], small[2][:, 0:2 * C]))


def stage_inner(nc, x1, norm, avg_d, inw_d, lnp_d, taps_d, xpw_d, dtw_d, bc, u_d, z_d, dt_d, dtu_d):
    with ExitStack() as stack:
        s_ = Scope(nc, stack, "inner")
        MI = 2 * DT
        avg = s_.sb("avg", [P, P])
        inw = s_.sb("inw", [P, HT, 2 * DI])
        lnp = s_.sb("lnp", [P, HT, 2])
        taps = s_.sb("taps", [P, DT, TAPS + 2])
        xpw = s_.sb("xpw", [P, DT, RANK + 2 * DS])
        dtw = s_.sb("dtw", [RANK, DI])
        xc = s_.sb("x", [P, HT, W])
        xg = s_.sb("xg", [P, HT, W])
        cen = s_.sb("cen", [P, HT, W])
        sq = s_.sb("sq", [P, HT, W])
        var = s_.sb("var", [P, W])
        rstd = s_.sb("rstd", [P, W])
        eps = s_.sb("eps", [P, 1])
        hn = s_.sb("hn", [P, HT, W])
        xi = s_.sb("xi", [P, DT, TAPS - 1 + W])
        pre = [s_.sb(f"pre{k}", [P, W]) for k in range(2)]
        sigu = [s_.sb(f"sigu{k}", [P, W]) for k in range(2)]
        sigz = [s_.sb(f"sigz{k}", [P, W]) for k in range(2)]
        z = [s_.sb(f"z{k}", [P, W]) for k in range(2)]
        u = s_.sb("u", [P, DT, W])
        xd = s_.sb("xd", [RANK + 2 * DS, W])
        raw = [s_.sb(f"raw{k}", [P, W]) for k in range(2)]
        soft = [s_.sb(f"soft{k}", [P, W]) for k in range(2)]
        dt = [s_.sb(f"dt{k}", [P, W]) for k in range(2)]
        dtu = [s_.sb(f"dtu{k}", [P, W]) for k in range(2)]
        acc = [s_.ps(f"acc{k}", [P, W]) for k in range(4)]
        consts, padded = s_.sem("consts"), s_.sem("padded")
        x_loaded = s_.sem("x_loaded")
        xg_ready, mean_ready, cen_ready = s_.sem("xg_ready"), s_.sem("mean_ready"), s_.sem("cen_ready")
        sq_ready, var_ready, var_copied = s_.sem("sq_ready"), s_.sem("var_ready"), s_.sem("var_copied")
        rstd_ready, hn_ready, h_ready = s_.sem("rstd_ready"), s_.sem("hn_ready"), s_.sem("h_ready")
        in_ready = s_.sem("in_ready")
        xi_ready, tap_done, pre_ready, sigu_ready, u_ready = (s_.sem(k) for k in ("xi_ready", "tap_done", "pre_ready", "sigu_ready", "u_ready"))
        sigz_ready, z_ready = s_.sem("sigz_ready"), s_.sem("z_ready")
        xd_ready, xd_copied = s_.sem("xd_ready"), s_.sem("xd_copied")
        dtp_ready, raw_ready, soft_step, soft_ready = (s_.sem(k) for k in ("dtp_ready", "raw_ready", "soft_step", "soft_ready"))
        dt_ready, dtu_ready = s_.sem("dt_ready"), s_.sem("dtu_ready")
        u_stored, z_stored = s_.sems("u_stored", DT), s_.sems("z_stored", 2)
        dt_stored, dtu_stored, bc_stored = s_.sems("dt_stored", 2), s_.sems("dtu_stored", 2), s_.sem("bc_stored")

        def before(i, m):
            return DT * i + max(m - 1, 0)

        with nc.Block() as block:
            @block.sync
            def _(sp):
                for dst, src in ((avg[:, :], avg_d), (inw[:, :, :], inw_d), (lnp[:, :, :], lnp_d), (taps[:, :, :], taps_d),
                                 (xpw[:, :, :], xpw_d), (dtw[:, :], dtw_d)):
                    sp.dma_start(dst, src).then_inc(consts, 16)

                def load(c):
                    sp.dma_start(xc[:, :, :], x1.rearrange("c (k p) w -> c p k w", p=P)[c]).then_inc(x_loaded, 16)

                def sequence(c, more):
                    if more:
                        sp.wait_ge(xg_ready, c + 1)
                        load(c + 1)
                    for m in range(DT):
                        sp.wait_ge(z_ready, DT * c + m + 1)
                        sp.dma_start(z_d[c, :, m], z[m % 2][:, :]).then_inc(z_stored[m % 2], 16)
                        sp.wait_ge(u_ready, DT * c + m + 1)
                        sp.dma_start(u_d[c, :, m], u[:, m]).then_inc(u_stored[m], 16)
                    sp.wait_ge(xd_copied, c + 1)
                    sp.dma_start(bc[c], xd[RANK:, :]).then_inc(bc_stored, 16)
                    for m in range(DT):
                        sp.wait_ge(dt_ready, DT * c + m + 1)
                        sp.dma_start(dt_d[c, :, m], dt[m % 2][:, :]).then_inc(dt_stored[m % 2], 16)
                        sp.wait_ge(dtu_ready, DT * c + m + 1)
                        sp.dma_start(dtu_d[c, :, m], dtu[m % 2][:, :]).then_inc(dtu_stored[m % 2], 16)

                load(0)
                with sp.Fori(0, C - 1) as c:
                    sequence(c, True)
                sequence(C - 1, False)
                for m in range(DT):
                    sp.wait_ge(u_stored[m], 16 * C)
                for k in range(2):
                    for t in (z_stored, dt_stored, dtu_stored):
                        sp.wait_ge(t[k], 16 * C * DT // 2)
                sp.wait_ge(bc_stored, 16 * C)

            @block.tensor
            def _(pe):
                pe.wait_ge(consts, 96)

                def product(a, rows, lhs, rhs, n):
                    for half in range(HALVES):
                        for k in range(n):
                            last = nc.tensor.matmul(acc[a][0:rows, half * NW:(half + 1) * NW], lhs(k), rhs(k, slice(half * NW, (half + 1) * NW)),
                                                    start=k == 0, stop=k == n - 1)
                    return last

                with pe.Fori(0, C) as i:
                    pe.wait_ge(xg_ready, i + 1)
                    pe.wait_ge(raw_ready, DT * i)
                    product(0, P, lambda k: avg[:, :], lambda k, h: xg[:, k, h], HT).then_inc(mean_ready, 1)
                    pe.wait_ge(sq_ready, i + 1)
                    product(1, P, lambda k: avg[:, :], lambda k, h: sq[:, k, h], HT).then_inc(var_ready, 1)
                    pe.wait_ge(h_ready, HT * i + HT)
                    for m in range(MI):
                        q = 2 + m
                        if m == 2:
                            pe.wait_ge(cen_ready, HT * i + HT)
                        if m == 3:
                            pe.wait_ge(var_copied, i + 1)
                        if m >= DT:
                            pe.wait_ge(xi_ready, DT * i + m - DT + 1)
                        product(q % 4, P, lambda k: inw[:, k, m * P:(m + 1) * P], lambda k, h: hn[:, k, h], HT).then_inc(in_ready, 1)
                    pe.wait_ge(z_ready, DT * i + 1)
                    pe.wait_ge(u_ready, DT * i + DT)
                    product(2, RANK + 2 * DS, lambda k: xpw[:, k], lambda k, h: u[:, k, h], DT).then_inc(xd_ready, 1)
                    pe.wait_ge(xd_copied, i + 1)
                    for m in range(DT):
                        pe.wait_ge(z_ready, DT * i + min(m + 2, DT))
                        product((11 + m) % 4, P, lambda k: dtw[:, m * P:(m + 1) * P], lambda k, h: xd[0:RANK, h], 1).then_inc(dtp_ready, 1)

            @block.scalar
            def _(act):
                act.wait_ge(consts, 96)
                act.wait_ge(padded, 2)
                with act.Fori(0, C) as i:
                    act.wait_ge(cen_ready, HT * i + HT)
                    nc.scalar.activation(sq[:, :, :], cen[:, :, :], ACT.Square).then_inc(sq_ready, 1)
                    act.wait_ge(var_ready, i + 1)
                    nc.scalar.activation(var[:, :], acc[1][:, :], ACT.Sqrt, bias=eps[:, :]).then_inc(var_copied, 1)
                    for k in range(HT):
                        act.wait_ge(hn_ready, HT * i + k + 1)
                        nc.scalar.activation(hn[:, k], hn[:, k], ACT.Identity, scale=lnp[:, k, 0:1], bias=lnp[:, k, 1:2]).then_inc(h_ready, 1)
                    for m in range(DT):
                        act.wait_ge(in_ready, MI * i + m + 1)
                        act.wait_ge(pre_ready, DT * i)
                        nc.scalar.activation(xi[:, m, TAPS - 1:], acc[(2 + m) % 4][:, :], ACT.Copy).then_inc(xi_ready, 1)
                    for m in range(DT):
                        act.wait_ge(in_ready, MI * i + DT + m + 1)
                        act.wait_ge(z_ready, before(i, m))
                        nc.scalar.activation(sigz[m % 2][:, :], acc[(2 + DT + m) % 4][:, :], ACT.Sigmoid).then_inc(sigz_ready, 1)
                        act.wait_ge(pre_ready, DT * i + m + 1)
                        act.wait_ge(u_ready, before(i, m))
                        nc.scalar.activation(sigu[m % 2][:, :], pre[m % 2][:, :], ACT.Sigmoid).then_inc(sigu_ready, 1)
                    act.wait_ge(xd_ready, i + 1)
                    act.wait_ge(bc_stored, 16 * i)
                    nc.scalar.activation(xd[:, :], acc[2][0:RANK + 2 * DS, :], ACT.Copy).then_inc(xd_copied, 1)
                    for m in range(DT):
                        chain = Chain(act, soft_step, 2 * (DT * i + m))
                        act.wait_ge(raw_ready, DT * i + m + 1)
                        act.wait_ge(dt_ready, before(i, m))
                        chain.link(nc.scalar.activation(soft[m % 2][:, :], raw[m % 2][:, :], ACT.Abs))
                        chain.link(nc.scalar.activation(soft[m % 2][:, :], soft[m % 2][:, :], ACT.Exp, scale=-1.0))
                        nc.scalar.activation(soft[m % 2][:, :], soft[m % 2][:, :], ACT.Ln, bias=1.0).then_inc(soft_ready, 1)

            @block.gpsimd
            def _(gp):
                nc.gpsimd.memset(xi[:, :, 0:TAPS - 1], 0.0).then_inc(padded, 1)
                nc.gpsimd.memset(eps[:, :], EPS).then_inc(padded, 1)
                with gp.Fori(0, C) as i:
                    for m in range(DT):
                        gp.wait_ge(dt_ready, DT * i + m + 1)
                        gp.wait_ge(dtu_stored[m % 2], 16 * (2 * i + m // 2))
                        nc.gpsimd.tensor_tensor(dtu[m % 2][:, :], dt[m % 2][:, :], u[:, m], ALU.mult).then_inc(dtu_ready, 1)

            @block.vector
            def _(v):
                v.wait_ge(consts, 96)
                with v.Fori(0, C) as i:
                    v.wait_ge(x_loaded, 16 * i + 16)
                    v.wait_ge(mean_ready, i)
                    nc.vector.tensor_scalar(xg[:, :, :], xc[:, :, :], norm[:, bass.ds(i, 1)], norm[:, bass.ds(C + i, 1)],
                                            ALU.mult, ALU.add).then_inc(xg_ready, 1)
                    v.wait_ge(mean_ready, i + 1)
                    v.wait_ge(xg_ready, i + 1)
                    v.wait_ge(sq_ready, i)
                    for k in range(HT):
                        nc.vector.tensor_tensor(cen[:, k], xg[:, k], acc[0][:, :], ALU.subtract).then_inc(cen_ready, 1)
                    v.wait_ge(var_copied, i + 1)
                    nc.vector.reciprocal(rstd[:, :], var[:, :]).then_inc(rstd_ready, 1)
                    v.wait_ge(rstd_ready, i + 1)
                    v.wait_ge(cen_ready, HT * i + HT)
                    v.wait_ge(in_ready, MI * i)
                    for k in range(HT):
                        nc.vector.tensor_tensor(hn[:, k], cen[:, k], rstd[:, :], ALU.mult).then_inc(hn_ready, 1)
                    for m in range(DT):
                        chain = Chain(v, tap_done, (TAPS - 1) * (DT * i + m))
                        p = pre[m % 2][:, :]
                        v.wait_ge(xi_ready, DT * i + m + 1)
                        chain.link(nc.vector.tensor_scalar(p, xi[:, m, 0:W], taps[:, m, 0:1], taps[:, m, TAPS:TAPS + 1], ALU.mult, ALU.add))
                        for t in range(1, TAPS):
                            step = nc.vector.scalar_tensor_tensor(p, xi[:, m, t:t + W], taps[:, m, t:t + 1], p, ALU.mult, ALU.add)
                            if t < TAPS - 1:
                                chain.link(step)
                            else:
                                step.then_inc(pre_ready, 1)
                        v.wait_ge(sigz_ready, DT * i + m + 1)
                        v.wait_ge(z_stored[m % 2], 16 * (2 * i + m // 2))
                        nc.vector.tensor_tensor(z[m % 2][:, :], acc[(2 + DT + m) % 4][:, :], sigz[m % 2][:, :], ALU.mult).then_inc(z_ready, 1)
                        v.wait_ge(sigu_ready, DT * i + m + 1)
                        v.wait_ge(u_stored[m], 16 * i)
                        v.wait_ge(dtu_ready, DT * i)
                        nc.vector.tensor_tensor(u[:, m], p, sigu[m % 2][:, :], ALU.mult).then_inc(u_ready, 1)
                    for m in range(DT):
                        v.wait_ge(dtp_ready, DT * i + m + 1)
                        nc.vector.tensor_scalar(raw[m % 2][:, :], acc[(11 + m) % 4][:, :], taps[:, m, TAPS + 1:TAPS + 2], None, ALU.add).then_inc(raw_ready, 1)
                        v.wait_ge(raw_ready, DT * i + m + 1)
                        v.wait_ge(soft_ready, DT * i + m + 1)
                        v.wait_ge(dt_stored[m % 2], 16 * (2 * i + m // 2))
                        v.wait_ge(dtu_ready, before(i, m))
                        nc.vector.scalar_tensor_tensor(dt[m % 2][:, :], raw[m % 2][:, :], 0.0, soft[m % 2][:, :], ALU.max, ALU.add).then_inc(dt_ready, 1)


def stage_scan(nc, dt_d, dtu_d, u_d, z_d, bc, alog_d, dskip_d, ident_d, gated_d):
    with ExitStack() as stack:
        s_ = Scope(nc, stack, "scan")
        RING = DT
        dt = [s_.sb(f"dt{s}", [P, DT, W]) for s in range(2)]
        dtu = [s_.sb(f"dtu{s}", [P, DT, W]) for s in range(2)]
        u = s_.sb("u", [P, DT, W])
        z = s_.sb("z", [P, DT, W])
        BC = [s_.sb(f"bc{k}", [P, 2, W]) for k in range(4)]
        decay = [s_.sb(f"decay{k}", [P, W]) for k in range(RING)]
        drive = [s_.sb(f"drive{k}", [P, W]) for k in range(RING)]
        state = [s_.sb(f"state{k}", [P, W]) for k in range(RING)]
        seen = [s_.sb(f"seen{k}", [P, W]) for k in range(RING)]
        alog = s_.sb("alog", [P, DT, DS])
        neg_a = s_.sb("a", [P, DT, DS])
        dskip = s_.sb("dskip", [P, DT])
        ident = s_.sb("ident", [P, P])
        diag = s_.sb("diag", [P, DT, P])
        zero = s_.sb("zero", [P, NW], mybir.dt.bfloat16)
        y = [s_.ps(f"y{m}", [P, W]) for m in range(DT)]
        consts, set_up = s_.sem("consts"), s_.sem("set_up")
        steps_loaded = s_.sems("steps_loaded", 2)
        uz_loaded = s_.sem("uz_loaded")
        bc_loaded = s_.sems("bc_loaded", 4)
        decay_ready, drive_ready = s_.sem("decay_ready"), s_.sem("drive_ready")
        scanned, seen_ready, summed = s_.sem("scanned"), s_.sem("seen_ready"), s_.sem("summed")
        y_ready, gated, stored = s_.sem("y_ready"), s_.sem("gated"), s_.sem("stored")
        dve = s_.sem("dve")
        FREE = RING - 1

        def count(c, g, k, m):
            return (DS * c + 4 * g + k) * DT + m

        with nc.Block() as block:
            @block.sync
            def _(sp):
                for dst, src in ((alog[:, :, :], alog_d), (dskip[:, :], dskip_d), (ident[:, :], ident_d)):
                    sp.dma_start(dst, src).then_inc(consts, 16)

                def load_bc(c, g, k):
                    row = bc.rearrange("c (k n) w -> c n k w", k=2)[c, bass.ds(4 * g + k, 1) if not isinstance(g, int) else slice(4 * g + k, 4 * g + k + 1)]
                    sp.dma_start(BC[k][:, :, :], row.broadcast_to([P, 2, W])).then_inc(bc_loaded[k], 16)

                def load_steps(c, s):
                    sp.dma_start(dt[s][:, :, :], dt_d[c]).then_inc(steps_loaded[s], 16)
                    sp.dma_start(dtu[s][:, :, :], dtu_d[c]).then_inc(steps_loaded[s], 16)

                def wait_bc(c, g, k):
                    sp.wait_ge(drive_ready, count(c, g, k, 0) - 3 * DT)
                    sp.wait_ge(seen_ready, count(c, g, k, 0) - 3 * DT)

                def sequence(c, s, more):
                    sp.wait_ge(stored, 16 * c)
                    sp.dma_start(u[:, :, :], u_d[c]).then_inc(uz_loaded, 16)
                    sp.dma_start(z[:, :, :], z_d[c]).then_inc(uz_loaded, 16)
                    if more:
                        load_steps(c + 1, 1 - s)
                    with sp.Fori(1, DS // 4) as g:
                        for k in range(4):
                            wait_bc(c, g, k)
                            load_bc(c, g, k)
                    if more:
                        for k in range(4):
                            wait_bc(c + 1, 0, k)
                            load_bc(c + 1, 0, k)
                    sp.wait_ge(gated, DT * c + DT)
                    sp.dma_start(gated_d[c], z[:, :, :]).then_inc(stored, 16)

                load_steps(0, 0)
                for k in range(4):
                    load_bc(0, 0, k)
                with sp.Fori(0, C // 2 - 1) as i:
                    for s in range(2):
                        sequence(2 * i + s, s, True)
                for s in range(2):
                    sequence(C - 2 + s, s, s == 0)
                sp.wait_ge(stored, 16 * C)

            def on_states(eng, before, state_step, after):
                with eng.Fori(0, C // 2) as i:
                    for s in range(2):
                        before(i, 2 * i + s, s)
                        with eng.Fori(0, DS // 4) as g:
                            for k in range(4):
                                state_step(i, 2 * i + s, s, g, k)
                        after(i, 2 * i + s, s)

            @block.scalar
            def _(act):
                act.wait_ge(consts, 48)
                nc.scalar.activation(neg_a[:, :, :], alog[:, :, :], ACT.Exp).then_inc(set_up, 1)
                act.wait_ge(set_up, 4)

                def before(i, c, s):
                    act.wait_ge(steps_loaded[s], 32 * i + 32)

                def step(i, c, s, g, k):
                    for m in range(DT):
                        act.wait_ge(scanned, count(c, g, k, m))
                        nc.scalar.activation(decay[m][:, :], dt[s][:, m], ACT.Exp,
                                             scale=neg_a[:, m, bass.ds(4 * g + k, 1)]).then_inc(decay_ready, 1)
                on_states(act, before, step, lambda i, c, s: None)

            @block.gpsimd
            def _(gp):
                nc.gpsimd.memset(zero[:, :], 0.0).then_inc(set_up, 1)

                def step(i, c, s, g, k):
                    if k == 0:
                        gp.wait_ge(steps_loaded[s], 32 * i + 32)
                    gp.wait_ge(bc_loaded[k], 16 * (4 * c + g + 1))
                    for m in range(DT):
                        gp.wait_ge(scanned, count(c, g, k, m))
                        nc.gpsimd.tensor_tensor(drive[m][:, :], dtu[s][:, m], BC[k][:, 0], ALU.mult).then_inc(drive_ready, 1)
                on_states(gp, lambda i, c, s: None, step, lambda i, c, s: None)

            @block.vector
            def _(v):
                v.wait_ge(consts, 48)
                v.wait_ge(set_up, 2)
                chain = Chain(v, dve)
                chain.link(nc.vector.tensor_scalar(neg_a[:, :, :], neg_a[:, :, :], -1.0, None, ALU.mult))
                v.sem_inc(set_up, 1)
                for m in range(DT):
                    chain.link(nc.vector.tensor_scalar(diag[:, m], ident[:, :], dskip[:, m:m + 1], None, ALU.mult))
                v.sem_inc(set_up, 1)
                v.sem_inc(scanned, FREE)

                def step(i, c, s, g, k):
                    v.wait_ge(bc_loaded[k], 16 * (4 * c + g + 1))

                    def scan(m):
                        n = count(c, g, k, m)
                        v.wait_ge(decay_ready, n + 1)
                        v.wait_ge(drive_ready, n + 1)
                        nc.vector.tensor_tensor_scan(state[m][:, :], decay[m][:, :], drive[m][:, :], 0.0, ALU.mult, ALU.add).then_inc(scanned, 1)

                    def see(m):
                        n = count(c, g, k, m)
                        v.wait_ge(summed, n)
                        v.wait_ge(scanned, n + 1 + FREE)
                        nc.vector.tensor_tensor(seen[m][:, :], state[m][:, :], BC[k][:, 1], ALU.mult).then_inc(seen_ready, 1)

                    scan(0)
                    for m in range(1, DT):
                        scan(m)
                        see(m - 1)
                    see(DT - 1)

                def after(i, c, s):
                    v.wait_ge(uz_loaded, 32 * c + 32)
                    for m in range(DT):
                        v.wait_ge(y_ready, DT * c + m + 1)
                        nc.vector.tensor_tensor(z[:, m], z[:, m], y[m][:, :], ALU.mult).then_inc(gated, 1)
                on_states(v, lambda i, c, s: None, step, after)

            @block.tensor
            def _(pe):
                pe.wait_ge(set_up, 4)
                pe.sem_inc(summed, FREE)

                def before(i, c, s):
                    pe.wait_ge(gated, DT * c)
                    for m in range(DT):
                        for half in range(HALVES):
                            nc.tensor.matmul(y[m][:, half * NW:(half + 1) * NW], zero[:, 0:P], zero[:, :], start=True, stop=False)

                def step(i, c, s, g, k):
                    for m in range(DT):
                        pe.wait_ge(seen_ready, count(c, g, k, m) + 1)
                        for half in range(HALVES):
                            last = nc.tensor.matmul(y[m][:, half * NW:(half + 1) * NW], ident[:, :], seen[m][:, half * NW:(half + 1) * NW],
                                                    start=False, stop=False)
                        last.then_inc(summed, 1)

                def after(i, c, s):
                    pe.wait_ge(uz_loaded, 32 * c + 32)
                    for m in range(DT):
                        for half in range(HALVES):
                            last = nc.tensor.matmul(y[m][:, half * NW:(half + 1) * NW], diag[:, m], u[:, m, half * NW:(half + 1) * NW],
                                                    start=False, stop=True)
                        last.then_inc(y_ready, 1)
                on_states(pe, before, step, after)


def stage_outer(nc, gated_d, x1, norm, avg_d, outw_d, lnp_d, res_d, h2_d):
    with ExitStack() as stack:
        s_ = Scope(nc, stack, "outer")
        avg = s_.sb("avg", [P, P])
        outw = s_.sb("outw", [P, DT, H])
        lnp = s_.sb("lnp", [P, HT, 2])
        gate = [s_.sb(f"gated{s}", [P, DT, W]) for s in range(2)]
        xc = [s_.sb(f"x{s}", [P, HT, W]) for s in range(2)]
        xg = s_.sb("xg", [P, HT, W])
        x2 = s_.sb("x2", [P, HT, W])
        res = s_.sb("res", [P, HT, W])
        cen = s_.sb("cen", [P, HT, W])
        sq = s_.sb("sq", [P, HT, W])
        var = s_.sb("var", [P, W])
        rstd = s_.sb("rstd", [P, W])
        eps = s_.sb("eps", [P, 1])
        hn = s_.sb("hn", [P, HT, W])
        acc = [s_.ps(f"acc{k}", [P, W]) for k in range(2)]
        mean_ps, var_ps = s_.ps("mean_acc", [P, W]), s_.ps("var_acc", [P, W])
        consts, set_up = s_.sem("consts"), s_.sem("set_up")
        loaded = s_.sems("loaded", 2)
        out_ready, xg_ready, x2_ready, res_ready = (s_.sem(k) for k in ("out_ready", "xg_ready", "x2_ready", "res_ready"))
        mean_ready, cen_ready, sq_ready, var_ready = (s_.sem(k) for k in ("mean_ready", "cen_ready", "sq_ready", "var_ready"))
        var_copied, rstd_ready, hn_ready, h_ready = (s_.sem(k) for k in ("var_copied", "rstd_ready", "hn_ready", "h_ready"))
        res_stored, h_stored = s_.sem("res_stored"), s_.sem("h_stored")

        with nc.Block() as block:
            @block.sync
            def _(sp):
                for dst, src in ((avg[:, :], avg_d), (outw[:, :, :], outw_d), (lnp[:, :, :], lnp_d)):
                    sp.dma_start(dst, src).then_inc(consts, 16)

                def load(c, s):
                    sp.dma_start(gate[s][:, :, :], gated_d[c]).then_inc(loaded[s], 16)
                    sp.dma_start(xc[s][:, :, :], x1.rearrange("c (k p) w -> c p k w", p=P)[c]).then_inc(loaded[s], 16)

                def store(c, s):
                    view = lambda t: t.rearrange("c (k p) w -> c p k w", p=P)[c]
                    sp.wait_ge(res_ready, c + 1)
                    sp.dma_start(view(res_d), res[:, :, :]).then_inc(res_stored, 16)
                    sp.wait_ge(h_ready, HT * c + HT)
                    sp.dma_start(view(h2_d), hn[:, :, :]).then_inc(h_stored, 16)

                for s in range(2):
                    load(s, s)
                with sp.Fori(0, C // 2 - 1) as i:
                    for s in range(2):
                        store(2 * i + s, s)
                        load(2 * i + s + 2, s)
                for s in range(2):
                    store(C - 2 + s, s)
                sp.wait_ge(res_stored, 16 * C)
                sp.wait_ge(h_stored, 16 * C)

            @block.tensor
            def _(pe):
                pe.wait_ge(consts, 48)
                with pe.Fori(0, C // 2) as i:
                    for s in range(2):
                        c = 2 * i + s
                        pe.wait_ge(loaded[s], 32 * i + 32)
                        for g in range(HT):
                            pe.wait_ge(x2_ready, HT * c)
                            for half in range(HALVES):
                                for k in range(DT):
                                    last = nc.tensor.matmul(acc[g][:, half * NW:(half + 1) * NW], outw[:, k, g * P:(g + 1) * P],
                                                            gate[s][:, k, half * NW:(half + 1) * NW], start=k == 0, stop=k == DT - 1)
                            last.then_inc(out_ready, 1)
                        for src, ready, n, dst, done in ((x2, x2_ready, HT, mean_ps, mean_ready), (sq, sq_ready, 1, var_ps, var_ready)):
                            pe.wait_ge(ready, n * c + n)
                            for half in range(HALVES):
                                for k in range(HT):
                                    last = nc.tensor.matmul(dst[:, half * NW:(half + 1) * NW], avg[:, :], src[:, k, half * NW:(half + 1) * NW],
                                                            start=k == 0, stop=k == HT - 1)
                            last.then_inc(done, 1)

            @block.scalar
            def _(act):
                act.wait_ge(consts, 48)
                act.wait_ge(set_up, 1)
                with act.Fori(0, C) as c:
                    act.wait_ge(cen_ready, HT * c + HT)
                    nc.scalar.activation(sq[:, :, :], cen[:, :, :], ACT.Square).then_inc(sq_ready, 1)
                    act.wait_ge(var_ready, c + 1)
                    nc.scalar.activation(var[:, :], var_ps[:, :], ACT.Sqrt, bias=eps[:, :]).then_inc(var_copied, 1)
                    for k in range(HT):
                        act.wait_ge(hn_ready, HT * c + k + 1)
                        nc.scalar.activation(hn[:, k], hn[:, k], ACT.Identity, scale=lnp[:, k, 0:1], bias=lnp[:, k, 1:2]).then_inc(h_ready, 1)

            @block.gpsimd
            def _(gp):
                nc.gpsimd.memset(eps[:, :], EPS).then_inc(set_up, 1)
                with gp.Fori(0, C // 2) as i:
                    for s in range(2):
                        c = 2 * i + s
                        gp.wait_ge(x2_ready, HT * c + HT)
                        gp.wait_ge(res_stored, 16 * c)
                        nc.gpsimd.tensor_tensor(res[:, :, :], xc[s][:, :, :], x2[:, :, :], ALU.add).then_inc(res_ready, 1)

            @block.vector
            def _(v):
                with v.Fori(0, C // 2) as i:
                    for s in range(2):
                        c = 2 * i + s
                        v.wait_ge(loaded[s], 32 * i + 32)
                        nc.vector.tensor_scalar(xg[:, :, :], xc[s][:, :, :], norm[:, bass.ds(c, 1)], norm[:, bass.ds(C + c, 1)],
                                                ALU.mult, ALU.add).then_inc(xg_ready, 1)
                        v.wait_ge(xg_ready, c + 1)
                        v.wait_ge(res_ready, c)
                        for g in range(HT):
                            v.wait_ge(out_ready, HT * c + g + 1)
                            nc.vector.tensor_tensor(x2[:, g], acc[g][:, :], xg[:, g], ALU.add).then_inc(x2_ready, 1)
                        v.wait_ge(mean_ready, c + 1)
                        v.wait_ge(x2_ready, HT * c + HT)
                        for k in range(HT):
                            nc.vector.tensor_tensor(cen[:, k], x2[:, k], mean_ps[:, :], ALU.subtract).then_inc(cen_ready, 1)
                        v.wait_ge(var_copied, c + 1)
                        nc.vector.reciprocal(rstd[:, :], var[:, :]).then_inc(rstd_ready, 1)
                        v.wait_ge(rstd_ready, c + 1)
                        v.wait_ge(cen_ready, HT * c + HT)
                        v.wait_ge(h_stored, 16 * c)
                        for k in range(HT):
                            nc.vector.tensor_tensor(hn[:, k], cen[:, k], rstd[:, :], ALU.mult).then_inc(hn_ready, 1)


def stage_perceptron(nc, name, w_d, src_d, kt, mt, finish, dst_d, add_d=None):
    with ExitStack() as stack:
        s_ = Scope(nc, stack, name)
        RING = 4 if kt * P * 4 <= 8192 else 2
        NP = 4
        src = s_.sb("src", [P, kt, W])
        w = [s_.sb(f"w{s}", [P, kt * P + 1]) for s in range(RING)]
        out = [s_.sb(f"out{s}", [P, W]) for s in range(NP)]
        add = [s_.sb(f"add{s}", [P, W]) for s in range(NP)] if add_d is not None else None
        acc = [s_.ps(f"acc{s}", [P, W]) for s in range(NP)]
        src_loaded = s_.sems("src_loaded", kt)
        w_loaded = s_.sems("w_loaded", RING)
        add_loaded = s_.sems("add_loaded", NP)
        multiplied, finished = s_.sem("multiplied"), s_.sem("finished")
        stored = s_.sems("stored", NP)

        with nc.Block() as block:
            @block.sync
            def _(sp):
                def load_w(m, s):
                    sp.dma_start(w[s % RING][:, :], w_d[m]).then_inc(w_loaded[s % RING], 16)

                def load_add(m, s):
                    if add_d is not None:
                        sp.dma_start(add[s][:, :], add_d[m]).then_inc(add_loaded[s], 16)

                load_w(0, 0)
                for k in range(kt):
                    sp.dma_start(src[:, k], src_d[k]).then_inc(src_loaded[k], 16)
                for s in range(1, RING):
                    load_w(s, s)
                for s in range(NP):
                    load_add(s, s)

                def store(m, s):
                    sp.wait_ge(finished, m + 1)
                    sp.dma_start(dst_d[m], out[s][:, :]).then_inc(stored[s], 16)

                with sp.Fori(0, mt // NP - 1) as i:
                    for s in range(NP):
                        store(NP * i + s, s)
                        load_w(NP * i + s + RING, s)
                        load_add(NP * i + s + NP, s)
                for s in range(NP):
                    store(mt - NP + s, s)
                    if s + RING < NP:
                        load_w(mt - NP + s + RING, s)
                for s in range(NP):
                    sp.wait_ge(stored[s], 16 * (mt // NP))

            @block.tensor
            def _(pe):
                for k in range(kt):
                    pe.wait_ge(src_loaded[k], 16)
                with pe.Fori(0, mt // NP) as i:
                    for s in range(NP):
                        pe.wait_ge(w_loaded[s % RING], 16 * (NP // RING * i + s // RING + 1))
                        pe.wait_ge(finished, NP * i)
                        for half in range(HALVES):
                            for k in range(kt):
                                last = nc.tensor.matmul(acc[s][:, half * NW:(half + 1) * NW], w[s % RING][:, k * P:(k + 1) * P],
                                                        src[:, k, half * NW:(half + 1) * NW], start=k == 0, stop=k == kt - 1)
                        last.then_inc(multiplied, 1)

            if add_d is None:
                @block.scalar
                def _(act):
                    with act.Fori(0, mt // NP) as i:
                        for s in range(NP):
                            act.wait_ge(multiplied, NP * i + s + 1)
                            act.wait_ge(stored[s], 16 * i)
                            nc.scalar.activation(out[s][:, :], acc[s][:, :], finish, bias=w[s % RING][:, kt * P:]).then_inc(finished, 1)
            else:
                @block.vector
                def _(v):
                    with v.Fori(0, mt // NP) as i:
                        for s in range(NP):
                            v.wait_ge(multiplied, NP * i + s + 1)
                            v.wait_ge(add_loaded[s], 16 * i + 16)
                            v.wait_ge(stored[s], 16 * i)
                            nc.vector.scalar_tensor_tensor(out[s][:, :], acc[s][:, :], w[s % RING][:, kt * P:], add[s][:, :],
                                                           ALU.add, ALU.add).then_inc(finished, 1)


def build(nc, t, out):
    def scratch(name, shape):
        return nc.dram_tensor(f"scratch_{name}", shape, F32, kind="Internal").ap()

    y = scratch("y", [3, C, H, W])
    q_parts, k_parts = scratch("q", [2, C * H, W]), scratch("k", [2, C * H, W])
    v_heads = scratch("v", [NH, P, KT * D])
    att, den, rden = scratch("att", [NH, D, W]), scratch("den", [NH, W]), scratch("rden", [NH, W])
    mixed, x1 = scratch("mixed", [C, H, W]), scratch("x1", [C, H, W])
    u_d, z_d, dt_d, dtu_d, gated_d = (scratch(k, [C, P, DT, W]) for k in ("u", "z", "dt", "dtu", "gated"))
    bc = scratch("bc", [C, 2 * DS, W])
    res_d, h2_d = scratch("res", [C, H, W]), scratch("h2", [C, H, W])
    hid_d = scratch("hid", [MT, P, W])
    norm = nc.alloc_sbuf_tensor("norm", [P, 2 * C], F32)

    stage_project(nc, t["x"], t["w_qkv"], y)
    stage_convolve(nc, y, t["kron"], t["cbias"], t["vbias"], t["rot"], t["cos"], t["sin"], q_parts, k_parts, v_heads)
    stage_attend(nc, q_parts, k_parts, v_heads, t["ident"], t["mask"], att, den)
    stage_recombine(nc, att, den, rden, t["wo"], mixed)
    stage_mix(nc, mixed, t["kmix"], t["x"], t["gavg"], t["sel"], x1, norm)
    stage_inner(nc, x1, norm, t["avg"], t["inw"], t["ln1"], t["taps"], t["xpw"], t["dtw"], bc, u_d, z_d, dt_d, dtu_d)
    stage_scan(nc, dt_d, dtu_d, u_d, z_d, bc, t["alog"], t["dskip"], t["ident"], gated_d)
    stage_outer(nc, gated_d, x1, norm, t["avg"], t["outw"], t["ln2"], res_d, h2_d)
    tiles = lambda a: a.rearrange("c (k p) w -> (c k) p w", p=P)
    stage_perceptron(nc, "up", t["w1"], tiles(h2_d), KD, MT, ACT.Relu, hid_d)
    stage_perceptron(nc, "down", t["w2"], hid_d, MT, KD, None, tiles(out[0]), tiles(res_d))


def constants():
    p = np.arange(P)
    out = {"ident": np.eye(P, dtype=np.float32)}
    rot = np.zeros((P, P), np.float32)
    rot[p ^ 1, p] = 1
    out["rot"] = rot
    inv = np.float32(1.0) / np.float32(10000.0) ** (np.arange(0, D, 2, dtype=np.float32) / np.float32(D))
    freqs = np.repeat(np.arange(W, dtype=np.float32)[:, None] * inv.astype(np.float32), 2, axis=-1)
    d = p[:, None] % HB + HB * np.arange(2)[None, :]
    sign = np.where(d % 2 == 0, -1.0, 1.0).astype(np.float32)
    out["cos"] = np.ascontiguousarray(np.cos(freqs).T[d])
    out["sin"] = np.ascontiguousarray(np.sin(freqs).T[d] * sign[:, :, None])
    mask = np.zeros((2 * KT, KT, P), np.float32)
    for t in range(KT):
        mask[t, t] = mask[KT + t, t] = 1
    out["mask"] = mask
    out["gavg"] = (p[:, None] // (GROUP * HB) == p[None, :] // (GROUP * HB)).astype(np.float32) / (GROUP * HB)
    out["sel"] = (p[:, None] // HB == np.arange(C)[None, :]).astype(np.float32) / HB
    out["avg"] = np.full((P, P), 1.0 / H, np.float32)
    return out


def spread_rows(m):
    k = np.zeros((C, HB, C, HB), np.float32)
    for r in range(HB):
        k[:, r, :, r] = m.T
    return k.reshape(P, P)


def cols(v, n):
    return v.reshape(n, P).T


def lay_out(i):
    t = constants()
    t["x"] = i["x"]
    L0, L1 = "L0_conv_", "L1_conv_"

    def contraction_first(w):
        w = np.swapaxes(w, -1, -2)
        w = w.reshape(*w.shape[:-2], w.shape[-2] // P, P, w.shape[-1])
        return np.swapaxes(w, -3, -2)

    parts = [contraction_first(i[f"{L0}W{n}_pw"]).reshape(C, P, HT * H) for n in "qkv"]
    parts += [np.swapaxes(i[f"{L0}b{n}_pw"].reshape(C, HT, P), 1, 2) for n in "qkv"]
    t["w_qkv"] = np.concatenate(parts, axis=2)
    t["kron"] = np.stack([np.stack([spread_rows(i[f"{L0}W{n}_conv"][:, :, 0, tap]) for tap in range(CT)], 1) for n in "qkv"], 1)
    t["cbias"] = np.stack([np.repeat(i[f"{L0}b{n}_conv"], HB) for n in "qk"], 1)
    t["vbias"] = np.broadcast_to(np.repeat(i[f"{L0}bv_conv"], HB), (P, P))
    t["wo"] = contraction_first(i[L0 + "Wo_pw"])
    t["kmix"] = spread_rows(i[L0 + "Wo_dw"])
    t["inw"] = contraction_first(i[L1 + "in_proj_w"])
    for n in "12":
        t["ln" + n] = np.stack([cols(i[f"{L1}n{n}_g"], HT), cols(i[f"{L1}n{n}_b"], HT)], 2)
    taps = [cols(i[L1 + "conv_w"][:, k], DT) for k in range(TAPS)] + [cols(i[L1 + "conv_b"], DT), cols(i[L1 + "dt_proj_b"], DT)]
    t["taps"] = np.stack(taps, 2)
    t["xpw"] = contraction_first(i[L1 + "x_proj_w"])
    t["dtw"] = i[L1 + "dt_proj_w"].T
    t["alog"] = np.swapaxes(i[L1 + "A_log"].reshape(DT, P, DS), 0, 1)
    t["dskip"] = cols(i[L1 + "D_skip"], DT)
    t["outw"] = contraction_first(i[L1 + "out_proj_w"])
    for n, kt, mt in (("1", KD, MT), ("2", MT, KD)):
        w = i[f"{L1}pw{n}_w"].reshape(mt, P, kt, P).transpose(0, 3, 2, 1).reshape(mt, P, kt * P)
        t["w" + n] = np.concatenate([w, i[f"{L1}pw{n}_b"].reshape(mt, P, 1)], axis=2)
    return t


def kernel(**inputs):
    import concourse.bacc as bacc
    from concourse.bass_utils import run_bass_kernel_spmd

    nc = bacc.Bacc("TRN2", target_bir_lowering=False, num_devices=1)
    arrays, t = {}, {}
    for name, a in lay_out({k: np.asarray(v) for k, v in inputs.items()}).items():
        a = np.ascontiguousarray(a)
        arrays[f"in_{name}"] = a
        t[name] = nc.dram_tensor(f"in_{name}", a.shape, mybir.dt.from_np(a.dtype), kind="ExternalInput").ap()
    out = nc.dram_tensor("out", (1, C, H, W), F32, kind="ExternalOutput").ap()
    build(nc, t, out)
    r = run_bass_kernel_spmd(nc, [arrays], core_ids=[0])
    return r.results[0]["out"]
```

```python
import numpy as np

import concourse.bass as bass
from concourse import mybir
from contextlib import ExitStack

F32 = mybir.dt.float32
F32R = mybir.dt.float32r
ALU = mybir.AluOpType
ACT = mybir.ActivationFunctionType
AX = mybir.AxisListType

P = 128
C = 8
H = 256
W = 1024
HT = H // P
NW = 512
HALVES = W // NW
HB = P // C
NB = H // HB
GROUP = 2
NG = C // GROUP
HEADS = 8
D = H // HEADS
NH = C * HEADS
KT = W // P
DI = 512
DT = DI // P
DS = 16
RANK = 16
TAPS = 4
CT = 3
HID = 4096
MT = HID // P
CD = C * H
KD = CD // P
EPS = 1e-5
START = 1


class Scope:

    def __init__(self, nc, stack, name):
        self.nc, self.stack, self.name, self.own = nc, stack, name, []
        stack.callback(self.give_back)

    def give_back(self):
        self.nc.all_engine_barrier()
        self.nc.clear_and_free_semaphores(self.own)
        self.nc.all_engine_barrier()

    def start(self):
        for sem in self.own:
            self.nc.sync.sem_inc(sem, START)
        self.nc.all_engine_barrier()

    def sb(self, name, shape, dt=F32):
        return self.stack.enter_context(self.nc.sbuf_tensor(f"{self.name}_{name}", shape, dt))

    def ps(self, name, shape, dt=F32):
        return self.stack.enter_context(self.nc.psum_tensor(f"{self.name}_{name}", shape, dt))

    def sem(self, name):
        self.own.append(self.nc.alloc_semaphore(f"{self.name}_{name}"))
        return self.own[-1]

    def sems(self, name, n):
        return [self.sem(f"{name}{i}") for i in range(n)]


class Chain:

    def __init__(self, eng, sem, base=0):
        self.eng, self.sem, self.base, self.n = eng, sem, base, 0

    def link(self, ins):
        self.n += 1
        ins.then_inc(self.sem, 1)
        self.eng.wait_ge(self.sem, START + self.base + self.n)


def halves(t):
    return [slice(i * NW, (i + 1) * NW) for i in range(HALVES)]


def stage_project(nc, x, w_qkv, y):
    with ExitStack() as stack:
        s_ = Scope(nc, stack, "project")
        X = s_.sb("x", [P, C, HT, W])
        WB = HT * H
        NWT = 3 * WB + 3 * HT
        w = [s_.sb(f"w{s}", [P, NWT]) for s in range(2)]
        xn = [s_.sb(f"xn{s}", [P, HT, W]) for s in range(2)]
        ybuf = [s_.sb(f"y{s}", [P, W]) for s in range(4)]
        stats = s_.sb("stats", [P, C, 4, 6])
        mv = s_.sb("mv", [P, NG, 2])
        avg = s_.sb("avg", [P, P])
        mean = s_.sb("mean", [P, NG])
        dev = s_.sb("dev", [P, NG])
        var = s_.sb("var", [P, NG])
        rstd = s_.sb("rstd", [P, NG])
        shift = s_.sb("shift", [P, NG])
        epsc = s_.sb("eps", [P, 1])
        acc = [s_.ps(f"acc{k}", [P, W]) for k in range(4)]
        x_loaded = s_.sems("x_loaded", C)
        w_loaded = s_.sems("w_loaded", 2)
        dve = s_.sem("dve")
        stat_ready, stat_summed = s_.sem("stat_ready"), s_.sem("stat_summed")
        var_ready, sd_ready, norm_ready = s_.sem("var_ready"), s_.sem("sd_ready"), s_.sem("norm_ready")
        xn_ready = s_.sem("xn_ready")
        multiplied = s_.sem("multiplied")
        biased = s_.sem("biased")
        stored = s_.sems("stored", 4)
        TILES = 3 * HT

        s_.start()
        with nc.Block() as block:
            @block.sync
            def _(sp):
                for c in range(C):
                    sp.dma_start(X[:, c], x[0, c].rearrange("(k p) w -> p k w", p=P)).then_inc(x_loaded[c], 16)
                for s in range(2):
                    sp.dma_start(w[s][:, :], w_qkv[s]).then_inc(w_loaded[s], 16)

                def store(c, i, s):
                    for n in range(TILES):
                        k = s * TILES + n
                        sp.wait_ge(biased, START + c * TILES + n + 1)
                        sp.dma_start(y[n // HT, c, (n % HT) * P:(n % HT + 1) * P, :],
                                     ybuf[k % 4][:, :]).then_inc(stored[k % 4], 16)

                with sp.Fori(0, C // 2 - 1) as i:
                    for s in range(2):
                        store(2 * i + s, i, s)
                        sp.dma_start(w[s][:, :], w_qkv[2 * i + 2 + s]).then_inc(w_loaded[s], 16)
                for s in range(2):
                    store(C - 2 + s, C // 2 - 1, s)
                for k in range(4):
                    sp.wait_ge(stored[k], START + 16 * (C * TILES // 4))

            @block.vector
            def _(v):
                nc.vector.memset(avg[:, :], 1.0 / P).then_inc(dve, 1)
                nc.vector.memset(epsc[:, :], EPS).then_inc(dve, 1)
                for c in range(C):
                    v.wait_ge(x_loaded[c], START + 16)
                    for q in range(4):
                        nc.vector.bn_stats(stats[:, c, q], X[:, c, q // 2, (q % 2) * NW:(q % 2 + 1) * NW]).then_inc(dve, 1)
                chain = Chain(v, dve, 2 + 4 * C)
                v.wait_ge(dve, START + 2 + 4 * C)
                for g in range(NG):
                    chain.link(nc.vector.bn_aggr(mv[:, g], stats[:, GROUP * g:GROUP * (g + 1)].rearrange("p c q s -> p (c q s)")))
                v.sem_inc(stat_ready, 1)
                v.wait_ge(stat_summed, START + 1)
                chain.link(nc.vector.tensor_copy(mean[:, :], acc[0][:, 0:NG]))
                chain.link(nc.vector.tensor_tensor(dev[:, :], mv[:, :, 0], mean[:, :], ALU.subtract))
                chain.link(nc.vector.tensor_tensor(dev[:, :], dev[:, :], dev[:, :], ALU.mult))
                nc.vector.tensor_tensor(var[:, :], dev[:, :], mv[:, :, 1], ALU.add).then_inc(var_ready, 1)
                v.wait_ge(sd_ready, START + 1)
                chain.link(nc.vector.reciprocal(rstd[:, :], dev[:, :]))
                nc.vector.scalar_tensor_tensor(shift[:, :], mean[:, :], -1.0, rstd[:, :], ALU.mult, ALU.mult).then_inc(norm_ready, 1)
                v.wait_ge(norm_ready, START + 1)
                with v.Fori(0, C // 2) as i:
                    for s in range(2):
                        v.wait_ge(multiplied, START + i * (2 * TILES))
                        nc.vector.tensor_scalar(xn[s][:, :, :], X[:, bass.ds(2 * i + s, 1)].rearrange("p o k w -> p (o k) w"),
                                                rstd[:, bass.ds(i, 1)], shift[:, bass.ds(i, 1)],
                                                ALU.mult, ALU.add).then_inc(xn_ready, 1)

            @block.tensor
            def _(pe):
                pe.wait_ge(stat_ready, START + 1)
                nc.tensor.matmul(acc[0][:, 0:NG], avg[:, :], mv[:, :, 0], start=True, stop=True).then_inc(stat_summed, 1)
                pe.wait_ge(var_ready, START + 1)
                nc.tensor.matmul(acc[1][:, 0:NG], avg[:, :], var[:, :], start=True, stop=True).then_inc(stat_summed, 1)
                pe.wait_ge(norm_ready, START + 1)
                with pe.Fori(0, C // 2) as i:
                    for s in range(2):
                        pe.wait_ge(w_loaded[s], START + 16 * i + 16)
                        pe.wait_ge(xn_ready, START + 2 * i + s + 1)
                        for n in range(TILES):
                            k = s * TILES + n
                            if k >= 4:
                                pe.wait_ge(biased, START + i * 2 * TILES + k - 3)
                            else:
                                pe.wait_ge(biased, START + i * 2 * TILES)
                            a = acc[k % 4]
                            for h in halves(a):
                                for kt in range(HT):
                                    o = (n // HT) * WB + kt * H + (n % HT) * P
                                    last = nc.tensor.matmul(a[:, h], w[s][:, o:o + P], xn[s][:, kt, h],
                                                            start=kt == 0, stop=kt == HT - 1)
                            last.then_inc(multiplied, 1)

            @block.scalar
            def _(act):
                act.wait_ge(stat_summed, START + 2)
                nc.scalar.activation(dev[:, :], acc[1][:, 0:NG], ACT.Sqrt, bias=epsc[:, :]).then_inc(sd_ready, 1)
                with act.Fori(0, C // 2) as i:
                    for s in range(2):
                        for n in range(TILES):
                            k = s * TILES + n
                            act.wait_ge(multiplied, START + i * 2 * TILES + k + 1)
                            act.wait_ge(stored[k % 4], START + 16 * (i * (2 * TILES // 4) + k // 4))
                            nc.scalar.activation(ybuf[k % 4][:, :], acc[k % 4][:, :], ACT.Identity,
                                                 bias=w[s][:, 3 * WB + n:3 * WB + n + 1]).then_inc(biased, 1)


def stage_convolve(nc, y, kron_d, cbias_d, vbias_d, rot_d, cos_d, sin_d, q_parts, k_parts, v_heads):
    with ExitStack() as stack:
        s_ = Scope(nc, stack, "conv")
        kron = s_.sb("kron", [P, 3, CT, P])
        cbias = s_.sb("cbias", [P, 2])
        vbias = s_.sb("vbias", [P, P])
        rot = s_.sb("rot", [P, P])
        cos = s_.sb("cos", [P, 2, W])
        sin = s_.sb("sin", [P, 2, W])
        yin = [[s_.sb(f"y{s}{n}", [P, W + 2]) for n in range(3)] for s in range(2)]
        qk = [s_.sb(f"qk{n}", [P, W]) for n in range(2)]
        turned = [s_.sb(f"turned{n}", [P, W]) for n in range(2)]
        kept = [s_.sb(f"kept{n}", [P, W]) for n in range(2)]
        hi = [s_.sb(f"hi{n}", [P, W], F32R) for n in range(2)]
        lo = [s_.sb(f"lo{n}", [P, W], F32R) for n in range(2)]
        vst = s_.sb("vst", [P, C, KT, 2 * HB])
        conv_ps = [s_.ps(f"conv{n}", [P, W]) for n in range(2)]
        rot_ps = s_.ps("turned", [P, W])
        v_ps = s_.ps("v", [P, W])
        consts = s_.sem("consts")
        padded = s_.sem("padded")
        y_loaded = [s_.sems(f"y_loaded{s}", 3) for s in range(2)]
        conv_done = s_.sem("conv_done")
        v_done = s_.sem("v_done")
        rot_done = s_.sem("rot_done")
        qk_ready = s_.sem("qk_ready")
        turn_taken = s_.sem("turn_taken")
        kept_ready = s_.sem("kept_ready")
        sum_ready = s_.sem("sum_ready")
        hi_ready = s_.sem("hi_ready")
        lo_ready = s_.sem("lo_ready")
        v_taken = s_.sem("v_taken")
        hi_stored, lo_stored = s_.sems("hi_stored", 2), s_.sems("lo_stored", 2)
        v_stored = s_.sem("v_stored")
        parts = [q_parts, k_parts]

        def rows(t, j):
            return t.rearrange("(c b r) w -> b c r w", c=C, r=HB)[j]

        s_.start()
        with nc.Block() as block:
            @block.sync
            def _(sp):
                for dst, src in ((kron[:, :, :, :], kron_d), (cbias[:, :], cbias_d), (vbias[:, :], vbias_d),
                                 (rot[:, :], rot_d), (cos[:, :, :], cos_d), (sin[:, :, :], sin_d)):
                    sp.dma_start(dst, src).then_inc(consts, 16)
                sp.wait_ge(padded, START + 12)

                def load(j, s):
                    for n in range(3):
                        sp.dma_start(yin[s][n][:, 1:W + 1], y[n].rearrange("c (b r) w -> b c r w", r=HB)[j]).then_inc(y_loaded[s][n], 16)

                for s in range(2):
                    load(s, s)
                with sp.Fori(1, NB // 2) as i:
                    for s in range(2):
                        sp.wait_ge(v_done, START + 2 * i + s - 1)
                        load(2 * i + s, s)

            @block.gpsimd
            def _(gp):
                for s in range(2):
                    for n in range(3):
                        nc.gpsimd.memset(yin[s][n][:, 0:1], 0.0).then_inc(padded, 1)
                        nc.gpsimd.memset(yin[s][n][:, W + 1:W + 2], 0.0).then_inc(padded, 1)
                gp.wait_ge(consts, START + 96)
                with gp.Fori(0, NB // 2) as i:
                    for s in range(2):
                        for n in range(2):
                            m = 2 * s + n
                            gp.wait_ge(qk_ready, START + 4 * i + m + 1)
                            gp.wait_ge(sum_ready, START + (4 * i + m - 1 if m >= 1 else 4 * i))
                            nc.gpsimd.tensor_tensor(kept[n][:, :], qk[n][:, :], cos[:, s], ALU.mult).then_inc(kept_ready, 1)

            @block.tensor
            def _(pe):
                pe.wait_ge(consts, START + 96)
                with pe.Fori(0, NB // 2) as i:
                    for s in range(2):
                        for n in range(2):
                            m = 2 * s + n
                            pe.wait_ge(y_loaded[s][n], START + 16 * i + 16)
                            pe.wait_ge(qk_ready, START + (4 * i + m - 1 if m >= 1 else 4 * i))
                            for h in range(HALVES):
                                for t in range(CT):
                                    last = nc.tensor.matmul(conv_ps[n][:, h * NW:(h + 1) * NW], kron[:, n, t],
                                                            yin[s][n][:, h * NW + t:h * NW + t + NW],
                                                            start=t == 0, stop=t == CT - 1)
                            last.then_inc(conv_done, 1)
                        pe.wait_ge(y_loaded[s][2], START + 16 * i + 16)
                        pe.wait_ge(v_taken, START + 2 * i + s)
                        for wt in range(KT):
                            for t in range(CT):
                                last = nc.tensor.matmul(v_ps[:, wt * P:(wt + 1) * P], yin[s][2][:, wt * P + t:wt * P + t + P],
                                                        kron[:, 2, t], start=t == 0, stop=t == CT - 1)
                        last.then_inc(v_done, 1)
                        for n in range(2):
                            m = 2 * s + n
                            pe.wait_ge(qk_ready, START + 4 * i + m + 1)
                            pe.wait_ge(turn_taken, START + 4 * i + m)
                            for h in range(HALVES):
                                last = nc.tensor.matmul(rot_ps[:, h * NW:(h + 1) * NW], rot[:, :], qk[n][:, h * NW:(h + 1) * NW],
                                                        start=True, stop=True)
                            last.then_inc(rot_done, 1)

            @block.scalar
            def _(act):
                act.wait_ge(consts, START + 96)

                def biases(i, s):
                    for n in range(2):
                        m = 2 * s + n
                        act.wait_ge(conv_done, START + 4 * i + m + 1)
                        if m >= 2:
                            act.wait_ge(rot_done, START + 4 * i + m - 1)
                            act.wait_ge(kept_ready, START + 4 * i + m - 1)
                        else:
                            act.wait_ge(rot_done, START + 4 * i)
                            act.wait_ge(kept_ready, START + 4 * i)
                        nc.scalar.activation(qk[n][:, :], conv_ps[n][:, :], ACT.Identity, bias=cbias[:, n:n + 1]).then_inc(qk_ready, 1)

                with act.Fori(0, NB // 2) as i:
                    for s in range(2):
                        biases(i, s)
                        for n in range(2):
                            m = 2 * s + n
                            act.wait_ge(sum_ready, START + 4 * i + m + 1)
                            act.wait_ge(hi_stored[n], START + 16 * (2 * i + s))
                            act.wait_ge(lo_ready, START + 4 * i + m)
                            nc.scalar.activation(hi[n][:, :], turned[n][:, :], ACT.Copy).then_inc(hi_ready, 1)
                            act.wait_ge(hi_ready, START + 4 * i + m + 1)
                            act.dma_start(rows(parts[n][0], 2 * i + s), hi[n][:, :].bitcast(F32)).then_inc(hi_stored[n], 16)
                            act.wait_ge(lo_ready, START + 4 * i + m + 1)
                            act.dma_start(rows(parts[n][1], 2 * i + s), lo[n][:, :].bitcast(F32)).then_inc(lo_stored[n], 16)
                    act.wait_ge(v_taken, START + 2 * i + 2)
                    for c in range(C):
                        act.dma_start(v_heads[HEADS * c + i], vst[:, c].rearrange("p t d -> p (t d)")).then_inc(v_stored, 16)
                for n in range(2):
                    act.wait_ge(hi_stored[n], START + 16 * NB)
                    act.wait_ge(lo_stored[n], START + 16 * NB)
                act.wait_ge(v_stored, START + 16 * C * (NB // 2))

            @block.vector
            def _(v):
                v.wait_ge(consts, START + 96)
                with v.Fori(0, NB // 2) as i:
                    for s in range(2):
                        v.wait_ge(v_done, START + 2 * i + s + 1)
                        v.wait_ge(v_stored, START + 16 * C * i)
                        nc.vector.tensor_tensor(
                            vst[:, :, :, s * HB:(s + 1) * HB].rearrange("p c t r -> p t c r"),
                            v_ps[:, :].rearrange("p (t c r) -> p t c r", t=KT, c=C),
                            vbias[:, :].rearrange("p (o c r) -> p o c r", o=1, c=C).broadcast_to([P, KT, C, HB]),
                            ALU.add).then_inc(v_taken, 1)
                        for n in range(2):
                            m = 2 * s + n
                            v.wait_ge(rot_done, START + 4 * i + m + 1)
                            v.wait_ge(hi_ready, START + (4 * i + m - 1 if m >= 1 else 4 * i))
                            nc.vector.tensor_tensor(turned[n][:, :], rot_ps[:, :], sin[:, s], ALU.mult).then_inc(turn_taken, 1)
                            v.wait_ge(turn_taken, START + 4 * i + m + 1)
                            v.wait_ge(kept_ready, START + 4 * i + m + 1)
                            nc.vector.tensor_tensor(turned[n][:, :], turned[n][:, :], kept[n][:, :], ALU.add).then_inc(sum_ready, 1)
                            v.wait_ge(hi_ready, START + 4 * i + m + 1)
                            v.wait_ge(lo_stored[n], START + 16 * (2 * i + s))
                            nc.vector.tensor_tensor(lo[n][:, :], turned[n][:, :], hi[n][:, :].bitcast(F32), ALU.subtract).then_inc(lo_ready, 1)


def stage_attend(nc, q_parts, k_parts, v_heads, ident_d, mask_d, att, den):
    with ExitStack() as stack:
        s_ = Scope(nc, stack, "attend")
        SLOTS = 4
        Q = [s_.sb(f"q{s}", [P, W], F32R) for s in range(SLOTS)]
        K = [s_.sb(f"k{s}", [P, W], F32R) for s in range(SLOTS)]
        V = [s_.sb(f"v{s}", [P, KT * D]) for s in range(SLOTS)]
        PT = [s_.sb(f"probs{t}", [P, W]) for t in range(2)]
        shift = [s_.sb(f"shift{t}", [P, W], F32R) for t in range(2)]
        osb = [s_.sb(f"o{s}", [P, NW]) for s in range(SLOTS)]
        nm2 = s_.sb("negmax_halves", [P, KT, HALVES])
        nm = s_.sb("negmax", [P, KT])
        m16 = s_.sb("maxparts", [P, 2 * KT], F32R)
        ident = s_.sb("ident", [P, P])
        mask = s_.sb("mask", [2 * KT, KT, P])
        ones = s_.sb("ones", [P, D])
        onesf = s_.sb("onesf", [P, P])
        onesr = s_.sb("onesr", [P, P], F32R)
        zeros = s_.sb("zeros", [P, W])
        row_ps = [s_.ps(f"rows{half}", [P, NW]) for half in range(HALVES)]
        st_ps = [s_.ps(f"cols{t}", [P, W]) for t in range(2)]
        o_ps = [s_.ps(f"out{t}", [P, NW]) for t in range(2)]
        consts = s_.sem("consts")
        set_up = s_.sem("set_up")
        loaded = s_.sems("loaded", SLOTS)
        row_ready = s_.sem("row_ready")
        row_taken = s_.sem("row_taken")
        max_split = s_.sem("max_split")
        dve = s_.sem("dve")
        st_ready = s_.sem("st_ready")
        exp_done = s_.sem("exp_done")
        pv_done = s_.sem("pv_done")
        o_copied = s_.sem("o_copied")
        stored = s_.sems("stored", SLOTS)
        PER = HALVES * KT + 1

        s_.start()
        with nc.Block() as block:
            @block.sync
            def _(sp):
                sp.dma_start(ident[:, :], ident_d).then_inc(consts, 16)
                sp.dma_start(mask[:, :, :], mask_d).then_inc(consts, 16)

                def load(h, s):
                    q = Q[s][:, :].bitcast(F32)
                    k = K[s][:, :].bitcast(F32)
                    qs = q_parts.rearrange("a (h d) w -> h a d w", d=D)[h]
                    ks = k_parts.rearrange("a (h d) w -> h a d w", d=D)[h]
                    sp.dma_start(q[0:2 * D, :], qs).then_inc(loaded[s], 16)
                    sp.dma_start(k[0:2 * D, :], ks).then_inc(loaded[s], 16)
                    sp.dma_start(k[2 * D:4 * D, :], ks).then_inc(loaded[s], 16)
                    sp.dma_start(q[2 * D:3 * D, :], qs[1]).then_inc(loaded[s], 16)
                    sp.dma_start(q[3 * D:4 * D, :], qs[0]).then_inc(loaded[s], 16)
                    sp.dma_start(V[s][:, :], v_heads[h]).then_inc(loaded[s], 16)

                def store(h, s):
                    sp.wait_ge(o_copied, START + h + 3)
                    for half in range(HALVES):
                        r = 2 * D * half
                        sp.dma_start(att[h, :, half * NW:(half + 1) * NW], osb[s][r:r + D, :]).then_inc(stored[s], 16)
                        sp.dma_start(den[bass.ds(h, 1) if not isinstance(h, int) else slice(h, h + 1), half * NW:(half + 1) * NW],
                                     osb[s][r + D:r + D + 1, :]).then_inc(stored[s], 16)

                for s in range(SLOTS):
                    load(s, s)
                with sp.Fori(0, NH // SLOTS - 1) as i:
                    for s in range(SLOTS):
                        h = SLOTS * i + s
                        sp.wait_ge(pv_done, START + KT * (h + 1))
                        load(h + SLOTS, s)
                        store(h, s)
                for s in range(SLOTS):
                    store(NH - SLOTS + s, s)
                for s in range(SLOTS):
                    sp.wait_ge(stored[s], START + 64 * (NH // SLOTS))

            @block.gpsimd
            def _(gp):
                nc.gpsimd.memset(ones[:, :], 1.0).then_inc(set_up, 1)

            def on_heads(eng, head):
                with eng.Fori(0, NH // SLOTS - 1) as i:
                    for s in range(SLOTS):
                        head(SLOTS * i + s, i, s, True)
                for s in range(SLOTS):
                    head(NH - SLOTS + s, NH // SLOTS - 1, s, s < SLOTS - 1)

            @block.tensor
            def _(pe):
                pe.wait_ge(consts, START + 32)
                pe.wait_ge(set_up, START + 4)

                def row_scores(h, s, j):
                    if j < KT:
                        for half in range(HALVES):
                            n = PER * h + HALVES * j + half
                            pe.wait_ge(row_taken, START + (n - 1 if j else n))
                            nc.tensor.matmul(row_ps[half][:, :], Q[s][:, j * P:(j + 1) * P], K[s][:, half * NW:(half + 1) * NW],
                                             start=True, stop=True).then_inc(row_ready, 1)
                    else:
                        pe.wait_ge(max_split, START + h + 1)
                        nc.tensor.matmul(row_ps[0][0:2 * KT, 0:P], m16[:, :].bitcast(F32), ident[:, :], start=True, stop=True).then_inc(row_ready, 1)

                def column_scores(h, s, t):
                    for half in halves(st_ps[0]):
                        nc.tensor.matmul(st_ps[t % 2][:, half], K[s][:, t * P:(t + 1) * P], Q[s][:, half], start=True, stop=False)
                        last = nc.tensor.matmul(st_ps[t % 2][:, half], onesr[:, :], shift[s % 2][:, half], start=False, stop=True)
                    last.then_inc(st_ready, 1)

                def values(h, s, t):
                    pe.wait_ge(exp_done, START + KT * h + t + 1)
                    for half in range(HALVES):
                        for sums in range(2):
                            g = D * (2 * half + sums)
                            lhs = ones[:, :] if sums else V[s][:, t * D:(t + 1) * D]
                            last = nc.tensor.matmul(o_ps[s % 2][g:g + D, :], lhs, PT[t % 2][:, half * NW:(half + 1) * NW],
                                                    start=t == 0, stop=t == KT - 1)
                    last.then_inc(pv_done, 1)

                AHEAD = {0: (0, 1), 1: (2, 3), 2: (4, 5), 3: (6,), 4: (7,), 6: (KT,)}

                def head(h, i, s, following):
                    nh, ns, ni = h + 1, (s + 1) % SLOTS, i + (s + 1) // SLOTS
                    if following:
                        pe.wait_ge(loaded[ns], START + 96 * (ni + 1))
                    for t in range(KT):
                        if t + 1 < KT:
                            column_scores(h, s, t + 1)
                        elif following:
                            pe.wait_ge(row_taken, START + PER * (nh + 1))
                            column_scores(nh, ns, 0)
                        ahead = AHEAD.get(t, ()) if following else ()
                        for j in ahead[:1]:
                            row_scores(nh, ns, j)
                        if t == 0:
                            pe.wait_ge(o_copied, START + h + 1)
                        values(h, s, t)
                        for j in ahead[1:]:
                            row_scores(nh, ns, j)

                pe.wait_ge(loaded[0], START + 96)
                for j in range(KT + 1):
                    row_scores(0, 0, j)
                pe.wait_ge(row_taken, START + PER)
                column_scores(0, 0, 0)
                on_heads(pe, head)

            @block.scalar
            def _(act):
                def head(h, i, s, following):
                    for t in range(KT):
                        act.wait_ge(st_ready, START + KT * h + t + 1)
                        nc.scalar.activation(PT[t % 2][:, :], st_ps[t % 2][:, :], ACT.Exp,
                                             scale=float(H) ** -0.5).then_inc(exp_done, 1)
                on_heads(act, head)

            @block.vector
            def _(v):
                for t in range(2):
                    nc.vector.memset(shift[t][:, :].bitcast(mybir.dt.uint32), 0).then_inc(set_up, 1)
                nc.vector.memset(onesf[:, :], 1.0).then_inc(dve, 1)
                v.wait_ge(dve, START + 1)
                nc.vector.tensor_copy(onesr[:, :], onesf[:, :]).then_inc(set_up, 1)
                v.sem_inc(o_copied, 2)
                v.wait_ge(consts, START + 32)

                def maximum(h, s):
                    for n in range(HALVES * KT):
                        v.wait_ge(row_ready, START + PER * h + n + 1)
                        nc.vector.tensor_reduce(nm2[:, n // HALVES, n % HALVES:n % HALVES + 1], row_ps[n % HALVES][:, :],
                                                AX.X, ALU.max, negate=True).then_inc(row_taken, 1)
                    v.wait_ge(row_taken, START + PER * h + HALVES * KT)
                    nc.vector.tensor_reduce(nm[:, :], nm2[:, :, :], AX.X, ALU.min).then_inc(dve, 1)
                    v.wait_ge(dve, START + 2 * h + 2)
                    nc.vector.tensor_copy(m16[:, 0:KT], nm[:, :]).then_inc(dve, 1)
                    v.wait_ge(dve, START + 2 * h + 3)
                    nc.vector.tensor_tensor(m16[:, KT:2 * KT], nm[:, :], m16[:, 0:KT].bitcast(F32), ALU.subtract).then_inc(max_split, 1)
                    v.wait_ge(row_ready, START + PER * (h + 1))
                    nc.vector.tensor_tensor(shift[s % 2][0:2 * KT, :].rearrange("r (t q) -> r t q", t=KT),
                                            row_ps[0][0:2 * KT, 0:P].rearrange("r (o q) -> r o q", o=1).broadcast_to([2 * KT, KT, P]),
                                            mask[:, :, :], ALU.mult).then_inc(row_taken, 1)

                def head(h, i, s, following):
                    if following:
                        maximum(h + 1, (s + 1) % SLOTS)
                    v.wait_ge(pv_done, START + KT * (h + 1))
                    v.wait_ge(stored[s], START + 64 * i)
                    nc.vector.tensor_copy(osb[s][:, :], o_ps[s % 2][:, :]).then_inc(o_copied, 1)

                maximum(0, 0)
                on_heads(v, head)


def stage_recombine(nc, att, den, rden, wo_d, mixed):
    with ExitStack() as stack:
        s_ = Scope(nc, stack, "recombine")
        dsb = s_.sb("den", [P, NW])
        rsb = s_.sb("rden", [P, NW])
        a = [s_.sb(f"a{s}", [P, HT, W]) for s in range(2)]
        r = [s_.sb(f"r{s}", [P, HT, W]) for s in range(2)]
        w = [s_.sb(f"w{s}", [P, HT, H]) for s in range(2)]
        out = [s_.sb(f"out{k}", [P, W]) for k in range(4)]
        acc = [s_.ps(f"acc{k}", [P, W]) for k in range(4)]
        den_loaded, inverted, inverse_stored = s_.sem("den_loaded"), s_.sem("inverted"), s_.sem("inverse_stored")
        loaded = s_.sems("loaded", 2)
        divided, multiplied, copied = s_.sem("divided"), s_.sem("multiplied"), s_.sem("copied")
        stored = s_.sems("stored", 4)
        N4 = P // D

        s_.start()
        with nc.Block() as block:
            @block.sync
            def _(sp):
                view = lambda t: t.rearrange("h (a w) -> (h a) w", a=HALVES)
                sp.dma_start(dsb[:, :], view(den)).then_inc(den_loaded, 16)
                sp.wait_ge(inverted, START + 1)
                sp.dma_start(view(rden), rsb[:, :]).then_inc(inverse_stored, 16)
                sp.wait_ge(inverse_stored, START + 16)

                def load(c, s):
                    sp.dma_start(a[s][:, :, :], att.rearrange("(c k n) d w -> c (n d) k w", c=C, k=HT)[c]).then_inc(loaded[s], 16)
                    sp.dma_start(w[s][:, :, :], wo_d[c]).then_inc(loaded[s], 16)
                    for k in range(HT):
                        src = rden.rearrange("(c k n o) w -> c k n o w", c=C, k=HT, o=1)[c, k]
                        sp.dma_start(r[s][:, k, :], src.broadcast_to([N4, D, W])).then_inc(loaded[s], 16)

                def store(c, s):
                    for g in range(HT):
                        k = HT * s + g
                        sp.wait_ge(copied, START + HT * c + g + 1)
                        sp.dma_start(mixed[c, g * P:(g + 1) * P, :], out[k][:, :]).then_inc(stored[k], 16)

                for s in range(2):
                    load(s, s)
                with sp.Fori(0, C // 2 - 1) as i:
                    for s in range(2):
                        store(2 * i + s, s)
                        load(2 * i + s + 2, s)
                for s in range(2):
                    store(C - 2 + s, s)
                for k in range(4):
                    sp.wait_ge(stored[k], START + 16 * (C // 2))

            @block.vector
            def _(v):
                v.wait_ge(den_loaded, START + 16)
                nc.vector.reciprocal(rsb[:, :], dsb[:, :]).then_inc(inverted, 1)
                with v.Fori(0, C // 2) as i:
                    for s in range(2):
                        v.wait_ge(loaded[s], START + 64 * i + 64)
                        nc.vector.tensor_tensor(a[s][:, :, :], a[s][:, :, :], r[s][:, :, :], ALU.mult).then_inc(divided, 1)

            @block.tensor
            def _(pe):
                with pe.Fori(0, C // 2) as i:
                    for s in range(2):
                        pe.wait_ge(divided, START + 2 * i + s + 1)
                        pe.wait_ge(copied, START + 4 * i)
                        for g in range(HT):
                            for half in range(HALVES):
                                for k in range(HT):
                                    last = nc.tensor.matmul(acc[HT * s + g][:, half * NW:(half + 1) * NW], w[s][:, k, g * P:(g + 1) * P],
                                                            a[s][:, k, half * NW:(half + 1) * NW], start=k == 0, stop=k == HT - 1)
                            last.then_inc(multiplied, 1)

            @block.scalar
            def _(act):
                with act.Fori(0, C // 2) as i:
                    for k in range(4):
                        act.wait_ge(multiplied, START + 4 * i + k + 1)
                        act.wait_ge(stored[k], START + 16 * i)
                        nc.scalar.activation(out[k][:, :], acc[k][:, :], ACT.Copy).then_inc(copied, 1)


def stage_mix(nc, mixed, kmix_d, x, gavg_d, sel_d, x1, norm):
    with ExitStack() as stack:
        s_ = Scope(nc, stack, "mix")
        kmix = s_.sb("kmix", [P, P])
        gavg = s_.sb("gavg", [P, P])
        sel = s_.sb("sel", [P, C])
        ones = s_.sb("ones", [P, P])
        eps = s_.sb("eps", [P, 1])
        a = [s_.sb(f"a{s}", [P, W]) for s in range(2)]
        xb = [s_.sb(f"x{s}", [P, W]) for s in range(2)]
        out = [s_.sb(f"out{s}", [P, W]) for s in range(2)]
        stats = s_.sb("stats", [P, NB * HALVES, 6])
        mv = s_.sb("mv", [P, 2])
        dev = s_.sb("dev", [P, 1])
        var = s_.sb("var", [P, 1])
        both = s_.sb("both", [P, 2])
        spread = s_.sb("spread", [P, 2, C])
        acc = [s_.ps(f"acc{s}", [P, W]) for s in range(2)]
        small = [s_.ps(f"small{k}", [P, NW]) for k in range(3)]
        consts = s_.sem("consts")
        loaded = s_.sems("loaded", 2)
        multiplied, added, measured = s_.sem("multiplied"), s_.sem("added"), s_.sem("measured")
        stored = s_.sems("stored", 2)
        dve, stat_ready, summed, sd_ready = s_.sem("dve"), s_.sem("stat_ready"), s_.sem("summed"), s_.sem("sd_ready")

        s_.start()
        with nc.Block() as block:
            @block.sync
            def _(sp):
                for dst, src in ((kmix[:, :], kmix_d), (gavg[:, :], gavg_d), (sel[:, :], sel_d)):
                    sp.dma_start(dst, src).then_inc(consts, 16)

                def load(j, s):
                    sp.dma_start(a[s][:, :], mixed.rearrange("c (b r) w -> b c r w", r=HB)[j]).then_inc(loaded[s], 16)
                    sp.dma_start(xb[s][:, :], x[0].rearrange("c (b r) w -> b c r w", r=HB)[j]).then_inc(loaded[s], 16)

                def store(j, s):
                    sp.wait_ge(added, START + j + 1)
                    sp.dma_start(x1.rearrange("c (b r) w -> b c r w", r=HB)[j], out[s][:, :]).then_inc(stored[s], 16)

                for s in range(2):
                    load(s, s)
                with sp.Fori(0, NB // 2 - 1) as i:
                    for s in range(2):
                        store(2 * i + s, s)
                        load(2 * i + s + 2, s)
                for s in range(2):
                    store(NB - 2 + s, s)
                for s in range(2):
                    sp.wait_ge(stored[s], START + 16 * (NB // 2))

            @block.tensor
            def _(pe):
                pe.wait_ge(consts, START + 48)
                with pe.Fori(0, NB // 2) as i:
                    for s in range(2):
                        pe.wait_ge(loaded[s], START + 32 * i + 32)
                        pe.wait_ge(added, START + 2 * i)
                        for half in range(HALVES):
                            last = nc.tensor.matmul(acc[s][:, half * NW:(half + 1) * NW], kmix[:, :], a[s][:, half * NW:(half + 1) * NW],
                                                    start=True, stop=True)
                        last.then_inc(multiplied, 1)
                pe.wait_ge(stat_ready, START + 1)
                nc.tensor.matmul(small[0][:, 0:1], gavg[:, :], mv[:, 0:1], start=True, stop=True).then_inc(summed, 1)
                pe.wait_ge(stat_ready, START + 2)
                nc.tensor.matmul(small[1][:, 0:1], gavg[:, :], var[:, :], start=True, stop=True).then_inc(summed, 1)
                pe.wait_ge(stat_ready, START + 3)
                nc.tensor.matmul(small[2][:, 0:2 * C], ones[:, :], spread[:, :, :].rearrange("p a c -> p (a c)"),
                                 start=True, stop=True).then_inc(summed, 1)

            @block.scalar
            def _(act):
                act.wait_ge(summed, START + 2)
                nc.scalar.activation(dev[:, :], small[1][:, 0:1], ACT.Sqrt, bias=eps[:, :]).then_inc(sd_ready, 1)

            @block.vector
            def _(v):
                nc.vector.memset(ones[:, :], 1.0)
                nc.vector.memset(eps[:, :], EPS)
                with v.Fori(0, NB // 2) as i:
                    for s in range(2):
                        v.wait_ge(multiplied, START + 2 * i + s + 1)
                        v.wait_ge(stored[s], START + 16 * i)
                        nc.vector.tensor_tensor(out[s][:, :], acc[s][:, :], xb[s][:, :], ALU.add).then_inc(added, 1)
                        v.wait_ge(added, START + 2 * i + s + 1)
                        for half in range(HALVES):
                            nc.vector.bn_stats(stats[:, bass.ds(4 * i + 2 * s + half, 1)].rearrange("p o k -> p (o k)"),
                                               out[s][:, half * NW:(half + 1) * NW]).then_inc(measured, 1)
                v.wait_ge(measured, START + 2 * NB)
                v.wait_ge(consts, START + 48)
                chain = Chain(v, dve)
                chain.link(nc.vector.bn_aggr(mv[:, :], stats[:, :, :].rearrange("p q k -> p (q k)")))
                v.sem_inc(stat_ready, 1)
                v.wait_ge(summed, START + 1)
                chain.link(nc.vector.tensor_copy(both[:, 1:2], small[0][:, 0:1]))
                chain.link(nc.vector.tensor_tensor(dev[:, :], mv[:, 0:1], both[:, 1:2], ALU.subtract))
                chain.link(nc.vector.tensor_tensor(dev[:, :], dev[:, :], dev[:, :], ALU.mult))
                chain.link(nc.vector.tensor_tensor(var[:, :], dev[:, :], mv[:, 1:2], ALU.add))
                v.sem_inc(stat_ready, 1)
                v.wait_ge(sd_ready, START + 1)
                chain.link(nc.vector.reciprocal(both[:, 0:1], dev[:, :]))
                chain.link(nc.vector.scalar_tensor_tensor(both[:, 1:2], both[:, 1:2], -1.0, both[:, 0:1], ALU.mult, ALU.mult))
                for k in range(2):
                    chain.link(nc.vector.tensor_scalar(spread[:, k], sel[:, :], both[:, k:k + 1], None, ALU.mult))
                v.sem_inc(stat_ready, 1)
                v.wait_ge(summed, START + 3)
                chain.link(nc.vector.tensor_copy(norm[:, :], small[2][:, 0:2 * C]))


def stage_inner(nc, x1, norm, avg_d, inw_d, lnp_d, taps_d, xpw_d, dtw_d, bc, u_d, z_d, dt_d, dtu_d):
    with ExitStack() as stack:
        s_ = Scope(nc, stack, "inner")
        MI = 2 * DT
        avg = s_.sb("avg", [P, P])
        inw = s_.sb("inw", [P, HT, 2 * DI])
        lnp = s_.sb("lnp", [P, HT, 2])
        taps = s_.sb("taps", [P, DT, TAPS + 2])
        xpw = s_.sb("xpw", [P, DT, RANK + 2 * DS])
        dtw = s_.sb("dtw", [RANK, DI])
        xc = s_.sb("x", [P, HT, W])
        xg = s_.sb("xg", [P, HT, W])
        cen = s_.sb("cen", [P, HT, W])
        sq = s_.sb("sq", [P, HT, W])
        var = s_.sb("var", [P, W])
        rstd = s_.sb("rstd", [P, W])
        eps = s_.sb("eps", [P, 1])
        hn = s_.sb("hn", [P, HT, W])
        xi = s_.sb("xi", [P, DT, TAPS - 1 + W])
        pre = [s_.sb(f"pre{k}", [P, W]) for k in range(2)]
        sigu = [s_.sb(f"sigu{k}", [P, W]) for k in range(2)]
        sigz = [s_.sb(f"sigz{k}", [P, W]) for k in range(2)]
        z = [s_.sb(f"z{k}", [P, W]) for k in range(2)]
        u = s_.sb("u", [P, DT, W])
        xd = s_.sb("xd", [RANK + 2 * DS, W])
        raw = [s_.sb(f"raw{k}", [P, W]) for k in range(2)]
        soft = [s_.sb(f"soft{k}", [P, W]) for k in range(2)]
        dt = [s_.sb(f"dt{k}", [P, W]) for k in range(2)]
        dtu = [s_.sb(f"dtu{k}", [P, W]) for k in range(2)]
        acc = [s_.ps(f"acc{k}", [P, W]) for k in range(4)]
        consts, padded = s_.sem("consts"), s_.sem("padded")
        x_loaded = s_.sem("x_loaded")
        xg_ready, mean_ready, cen_ready = s_.sem("xg_ready"), s_.sem("mean_ready"), s_.sem("cen_ready")
        sq_ready, var_ready, var_copied = s_.sem("sq_ready"), s_.sem("var_ready"), s_.sem("var_copied")
        rstd_ready, hn_ready, h_ready = s_.sem("rstd_ready"), s_.sem("hn_ready"), s_.sem("h_ready")
        in_ready = s_.sem("in_ready")
        xi_ready, tap_done, pre_ready, sigu_ready, u_ready = (s_.sem(k) for k in ("xi_ready", "tap_done", "pre_ready", "sigu_ready", "u_ready"))
        sigz_ready, z_ready = s_.sem("sigz_ready"), s_.sem("z_ready")
        xd_ready, xd_copied = s_.sem("xd_ready"), s_.sem("xd_copied")
        dtp_ready, raw_ready, soft_step, soft_ready = (s_.sem(k) for k in ("dtp_ready", "raw_ready", "soft_step", "soft_ready"))
        dt_ready, dtu_ready = s_.sem("dt_ready"), s_.sem("dtu_ready")
        u_stored, z_stored = s_.sems("u_stored", DT), s_.sems("z_stored", 2)
        dt_stored, dtu_stored, bc_stored = s_.sems("dt_stored", 2), s_.sems("dtu_stored", 2), s_.sem("bc_stored")

        def before(i, m):
            return DT * i + max(m - 1, 0)

        s_.start()
        with nc.Block() as block:
            @block.sync
            def _(sp):
                for dst, src in ((avg[:, :], avg_d), (inw[:, :, :], inw_d), (lnp[:, :, :], lnp_d), (taps[:, :, :], taps_d),
                                 (xpw[:, :, :], xpw_d), (dtw[:, :], dtw_d)):
                    sp.dma_start(dst, src).then_inc(consts, 16)

                def load(c):
                    sp.dma_start(xc[:, :, :], x1.rearrange("c (k p) w -> c p k w", p=P)[c]).then_inc(x_loaded, 16)

                def sequence(c, more):
                    if more:
                        sp.wait_ge(xg_ready, START + c + 1)
                        load(c + 1)
                    for m in range(DT):
                        sp.wait_ge(z_ready, START + DT * c + m + 1)
                        sp.dma_start(z_d[c, :, m], z[m % 2][:, :]).then_inc(z_stored[m % 2], 16)
                        sp.wait_ge(u_ready, START + DT * c + m + 1)
                        sp.dma_start(u_d[c, :, m], u[:, m]).then_inc(u_stored[m], 16)
                    sp.wait_ge(xd_copied, START + c + 1)
                    sp.dma_start(bc[c], xd[RANK:, :]).then_inc(bc_stored, 16)
                    for m in range(DT):
                        sp.wait_ge(dt_ready, START + DT * c + m + 1)
                        sp.dma_start(dt_d[c, :, m], dt[m % 2][:, :]).then_inc(dt_stored[m % 2], 16)
                        sp.wait_ge(dtu_ready, START + DT * c + m + 1)
                        sp.dma_start(dtu_d[c, :, m], dtu[m % 2][:, :]).then_inc(dtu_stored[m % 2], 16)

                load(0)
                with sp.Fori(0, C - 1) as c:
                    sequence(c, True)
                sequence(C - 1, False)
                for m in range(DT):
                    sp.wait_ge(u_stored[m], START + 16 * C)
                for k in range(2):
                    for t in (z_stored, dt_stored, dtu_stored):
                        sp.wait_ge(t[k], START + 16 * C * DT // 2)
                sp.wait_ge(bc_stored, START + 16 * C)

            @block.tensor
            def _(pe):
                pe.wait_ge(consts, START + 96)

                def product(a, rows, lhs, rhs, n):
                    for half in range(HALVES):
                        for k in range(n):
                            last = nc.tensor.matmul(acc[a][0:rows, half * NW:(half + 1) * NW], lhs(k), rhs(k, slice(half * NW, (half + 1) * NW)),
                                                    start=k == 0, stop=k == n - 1)
                    return last

                with pe.Fori(0, C) as i:
                    pe.wait_ge(xg_ready, START + i + 1)
                    pe.wait_ge(raw_ready, START + DT * i)
                    product(0, P, lambda k: avg[:, :], lambda k, h: xg[:, k, h], HT).then_inc(mean_ready, 1)
                    pe.wait_ge(sq_ready, START + i + 1)
                    product(1, P, lambda k: avg[:, :], lambda k, h: sq[:, k, h], HT).then_inc(var_ready, 1)
                    pe.wait_ge(h_ready, START + HT * i + HT)
                    for m in range(MI):
                        q = 2 + m
                        if m == 2:
                            pe.wait_ge(cen_ready, START + HT * i + HT)
                        if m == 3:
                            pe.wait_ge(var_copied, START + i + 1)
                        if m >= DT:
                            pe.wait_ge(xi_ready, START + DT * i + m - DT + 1)
                        product(q % 4, P, lambda k: inw[:, k, m * P:(m + 1) * P], lambda k, h: hn[:, k, h], HT).then_inc(in_ready, 1)
                    pe.wait_ge(z_ready, START + DT * i + 1)
                    pe.wait_ge(u_ready, START + DT * i + DT)
                    product(2, RANK + 2 * DS, lambda k: xpw[:, k], lambda k, h: u[:, k, h], DT).then_inc(xd_ready, 1)
                    pe.wait_ge(xd_copied, START + i + 1)
                    for m in range(DT):
                        pe.wait_ge(z_ready, START + DT * i + min(m + 2, DT))
                        product((11 + m) % 4, P, lambda k: dtw[:, m * P:(m + 1) * P], lambda k, h: xd[0:RANK, h], 1).then_inc(dtp_ready, 1)

            @block.scalar
            def _(act):
                act.wait_ge(consts, START + 96)
                act.wait_ge(padded, START + 2)
                with act.Fori(0, C) as i:
                    act.wait_ge(cen_ready, START + HT * i + HT)
                    nc.scalar.activation(sq[:, :, :], cen[:, :, :], ACT.Square).then_inc(sq_ready, 1)
                    act.wait_ge(var_ready, START + i + 1)
                    nc.scalar.activation(var[:, :], acc[1][:, :], ACT.Sqrt, bias=eps[:, :]).then_inc(var_copied, 1)
                    for k in range(HT):
                        act.wait_ge(hn_ready, START + HT * i + k + 1)
                        nc.scalar.activation(hn[:, k], hn[:, k], ACT.Identity, scale=lnp[:, k, 0:1], bias=lnp[:, k, 1:2]).then_inc(h_ready, 1)
                    for m in range(DT):
                        act.wait_ge(in_ready, START + MI * i + m + 1)
                        act.wait_ge(pre_ready, START + DT * i)
                        nc.scalar.activation(xi[:, m, TAPS - 1:], acc[(2 + m) % 4][:, :], ACT.Copy).then_inc(xi_ready, 1)
                    for m in range(DT):
                        act.wait_ge(in_ready, START + MI * i + DT + m + 1)
                        act.wait_ge(z_ready, START + before(i, m))
                        nc.scalar.activation(sigz[m % 2][:, :], acc[(2 + DT + m) % 4][:, :], ACT.Sigmoid).then_inc(sigz_ready, 1)
                        act.wait_ge(pre_ready, START + DT * i + m + 1)
                        act.wait_ge(u_ready, START + before(i, m))
                        nc.scalar.activation(sigu[m % 2][:, :], pre[m % 2][:, :], ACT.Sigmoid).then_inc(sigu_ready, 1)
                    act.wait_ge(xd_ready, START + i + 1)
                    act.wait_ge(bc_stored, START + 16 * i)
                    nc.scalar.activation(xd[:, :], acc[2][0:RANK + 2 * DS, :], ACT.Copy).then_inc(xd_copied, 1)
                    for m in range(DT):
                        chain = Chain(act, soft_step, 2 * (DT * i + m))
                        act.wait_ge(raw_ready, START + DT * i + m + 1)
                        act.wait_ge(dt_ready, START + before(i, m))
                        chain.link(nc.scalar.activation(soft[m % 2][:, :], raw[m % 2][:, :], ACT.Abs))
                        chain.link(nc.scalar.activation(soft[m % 2][:, :], soft[m % 2][:, :], ACT.Exp, scale=-1.0))
                        nc.scalar.activation(soft[m % 2][:, :], soft[m % 2][:, :], ACT.Ln, bias=1.0).then_inc(soft_ready, 1)

            @block.gpsimd
            def _(gp):
                nc.gpsimd.memset(xi[:, :, 0:TAPS - 1], 0.0).then_inc(padded, 1)
                nc.gpsimd.memset(eps[:, :], EPS).then_inc(padded, 1)
                with gp.Fori(0, C) as i:
                    for m in range(DT):
                        gp.wait_ge(dt_ready, START + DT * i + m + 1)
                        gp.wait_ge(dtu_stored[m % 2], START + 16 * (2 * i + m // 2))
                        nc.gpsimd.tensor_tensor(dtu[m % 2][:, :], dt[m % 2][:, :], u[:, m], ALU.mult).then_inc(dtu_ready, 1)

            @block.vector
            def _(v):
                v.wait_ge(consts, START + 96)
                with v.Fori(0, C) as i:
                    v.wait_ge(x_loaded, START + 16 * i + 16)
                    v.wait_ge(mean_ready, START + i)
                    nc.vector.tensor_scalar(xg[:, :, :], xc[:, :, :], norm[:, bass.ds(i, 1)], norm[:, bass.ds(C + i, 1)],
                                            ALU.mult, ALU.add).then_inc(xg_ready, 1)
                    v.wait_ge(mean_ready, START + i + 1)
                    v.wait_ge(xg_ready, START + i + 1)
                    v.wait_ge(sq_ready, START + i)
                    for k in range(HT):
                        nc.vector.tensor_tensor(cen[:, k], xg[:, k], acc[0][:, :], ALU.subtract).then_inc(cen_ready, 1)
                    v.wait_ge(var_copied, START + i + 1)
                    nc.vector.reciprocal(rstd[:, :], var[:, :]).then_inc(rstd_ready, 1)
                    v.wait_ge(rstd_ready, START + i + 1)
                    v.wait_ge(cen_ready, START + HT * i + HT)
                    v.wait_ge(in_ready, START + MI * i)
                    for k in range(HT):
                        nc.vector.tensor_tensor(hn[:, k], cen[:, k], rstd[:, :], ALU.mult).then_inc(hn_ready, 1)
                    for m in range(DT):
                        chain = Chain(v, tap_done, (TAPS - 1) * (DT * i + m))
                        p = pre[m % 2][:, :]
                        v.wait_ge(xi_ready, START + DT * i + m + 1)
                        chain.link(nc.vector.tensor_scalar(p, xi[:, m, 0:W], taps[:, m, 0:1], taps[:, m, TAPS:TAPS + 1], ALU.mult, ALU.add))
                        for t in range(1, TAPS):
                            step = nc.vector.scalar_tensor_tensor(p, xi[:, m, t:t + W], taps[:, m, t:t + 1], p, ALU.mult, ALU.add)
                            if t < TAPS - 1:
                                chain.link(step)
                            else:
                                step.then_inc(pre_ready, 1)
                        v.wait_ge(sigz_ready, START + DT * i + m + 1)
                        v.wait_ge(z_stored[m % 2], START + 16 * (2 * i + m // 2))
                        nc.vector.tensor_tensor(z[m % 2][:, :], acc[(2 + DT + m) % 4][:, :], sigz[m % 2][:, :], ALU.mult).then_inc(z_ready, 1)
                        v.wait_ge(sigu_ready, START + DT * i + m + 1)
                        v.wait_ge(u_stored[m], START + 16 * i)
                        v.wait_ge(dtu_ready, START + DT * i)
                        nc.vector.tensor_tensor(u[:, m], p, sigu[m % 2][:, :], ALU.mult).then_inc(u_ready, 1)
                    for m in range(DT):
                        v.wait_ge(dtp_ready, START + DT * i + m + 1)
                        nc.vector.tensor_scalar(raw[m % 2][:, :], acc[(11 + m) % 4][:, :], taps[:, m, TAPS + 1:TAPS + 2], None, ALU.add).then_inc(raw_ready, 1)
                        v.wait_ge(raw_ready, START + DT * i + m + 1)
                        v.wait_ge(soft_ready, START + DT * i + m + 1)
                        v.wait_ge(dt_stored[m % 2], START + 16 * (2 * i + m // 2))
                        v.wait_ge(dtu_ready, START + before(i, m))
                        nc.vector.scalar_tensor_tensor(dt[m % 2][:, :], raw[m % 2][:, :], 0.0, soft[m % 2][:, :], ALU.max, ALU.add).then_inc(dt_ready, 1)


def stage_scan(nc, dt_d, dtu_d, u_d, z_d, bc, alog_d, dskip_d, ident_d, gated_d):
    with ExitStack() as stack:
        s_ = Scope(nc, stack, "scan")
        RING = DT
        dt = [s_.sb(f"dt{s}", [P, DT, W]) for s in range(2)]
        dtu = [s_.sb(f"dtu{s}", [P, DT, W]) for s in range(2)]
        u = s_.sb("u", [P, DT, W])
        z = s_.sb("z", [P, DT, W])
        BC = [s_.sb(f"bc{k}", [P, 2, W]) for k in range(4)]
        decay = [s_.sb(f"decay{k}", [P, W]) for k in range(RING)]
        drive = [s_.sb(f"drive{k}", [P, W]) for k in range(RING)]
        state = [s_.sb(f"state{k}", [P, W]) for k in range(RING)]
        seen = [s_.sb(f"seen{k}", [P, W]) for k in range(RING)]
        alog = s_.sb("alog", [P, DT, DS])
        neg_a = s_.sb("a", [P, DT, DS])
        dskip = s_.sb("dskip", [P, DT])
        ident = s_.sb("ident", [P, P])
        diag = s_.sb("diag", [P, DT, P])
        zero = s_.sb("zero", [P, NW], mybir.dt.bfloat16)
        y = [s_.ps(f"y{m}", [P, W]) for m in range(DT)]
        consts, set_up = s_.sem("consts"), s_.sem("set_up")
        steps_loaded = s_.sems("steps_loaded", 2)
        uz_loaded = s_.sem("uz_loaded")
        bc_loaded = s_.sems("bc_loaded", 4)
        decay_ready, drive_ready = s_.sem("decay_ready"), s_.sem("drive_ready")
        scanned, seen_ready, summed = s_.sem("scanned"), s_.sem("seen_ready"), s_.sem("summed")
        y_ready, gated, stored = s_.sem("y_ready"), s_.sem("gated"), s_.sem("stored")
        dve = s_.sem("dve")
        FREE = RING - 1

        def count(c, g, k, m):
            return (DS * c + 4 * g + k) * DT + m

        s_.start()
        with nc.Block() as block:
            @block.sync
            def _(sp):
                for dst, src in ((alog[:, :, :], alog_d), (dskip[:, :], dskip_d), (ident[:, :], ident_d)):
                    sp.dma_start(dst, src).then_inc(consts, 16)

                def load_bc(c, g, k):
                    row = bc.rearrange("c (k n) w -> c n k w", k=2)[c, bass.ds(4 * g + k, 1) if not isinstance(g, int) else slice(4 * g + k, 4 * g + k + 1)]
                    sp.dma_start(BC[k][:, :, :], row.broadcast_to([P, 2, W])).then_inc(bc_loaded[k], 16)

                def load_steps(c, s):
                    sp.dma_start(dt[s][:, :, :], dt_d[c]).then_inc(steps_loaded[s], 16)
                    sp.dma_start(dtu[s][:, :, :], dtu_d[c]).then_inc(steps_loaded[s], 16)

                def wait_bc(c, g, k):
                    sp.wait_ge(drive_ready, START + count(c, g, k, 0) - 3 * DT)
                    sp.wait_ge(seen_ready, START + count(c, g, k, 0) - 3 * DT)

                def sequence(c, s, more):
                    sp.wait_ge(stored, START + 16 * c)
                    sp.dma_start(u[:, :, :], u_d[c]).then_inc(uz_loaded, 16)
                    sp.dma_start(z[:, :, :], z_d[c]).then_inc(uz_loaded, 16)
                    if more:
                        load_steps(c + 1, 1 - s)
                    with sp.Fori(1, DS // 4) as g:
                        for k in range(4):
                            wait_bc(c, g, k)
                            load_bc(c, g, k)
                    if more:
                        for k in range(4):
                            wait_bc(c + 1, 0, k)
                            load_bc(c + 1, 0, k)
                    sp.wait_ge(gated, START + DT * c + DT)
                    sp.dma_start(gated_d[c], z[:, :, :]).then_inc(stored, 16)

                load_steps(0, 0)
                for k in range(4):
                    load_bc(0, 0, k)
                with sp.Fori(0, C // 2 - 1) as i:
                    for s in range(2):
                        sequence(2 * i + s, s, True)
                for s in range(2):
                    sequence(C - 2 + s, s, s == 0)
                sp.wait_ge(stored, START + 16 * C)

            def on_states(eng, before, state_step, after):
                with eng.Fori(0, C // 2) as i:
                    for s in range(2):
                        before(i, 2 * i + s, s)
                        with eng.Fori(0, DS // 4) as g:
                            for k in range(4):
                                state_step(i, 2 * i + s, s, g, k)
                        after(i, 2 * i + s, s)

            @block.scalar
            def _(act):
                act.wait_ge(consts, START + 48)
                nc.scalar.activation(neg_a[:, :, :], alog[:, :, :], ACT.Exp).then_inc(set_up, 1)
                act.wait_ge(set_up, START + 4)

                def before(i, c, s):
                    act.wait_ge(steps_loaded[s], START + 32 * i + 32)

                def step(i, c, s, g, k):
                    for m in range(DT):
                        act.wait_ge(scanned, START + count(c, g, k, m))
                        nc.scalar.activation(decay[m][:, :], dt[s][:, m], ACT.Exp,
                                             scale=neg_a[:, m, bass.ds(4 * g + k, 1)]).then_inc(decay_ready, 1)
                on_states(act, before, step, lambda i, c, s: None)

            @block.gpsimd
            def _(gp):
                nc.gpsimd.memset(zero[:, :], 0.0).then_inc(set_up, 1)

                def step(i, c, s, g, k):
                    if k == 0:
                        gp.wait_ge(steps_loaded[s], START + 32 * i + 32)
                    gp.wait_ge(bc_loaded[k], START + 16 * (4 * c + g + 1))
                    for m in range(DT):
                        gp.wait_ge(scanned, START + count(c, g, k, m))
                        nc.gpsimd.tensor_tensor(drive[m][:, :], dtu[s][:, m], BC[k][:, 0], ALU.mult).then_inc(drive_ready, 1)
                on_states(gp, lambda i, c, s: None, step, lambda i, c, s: None)

            @block.vector
            def _(v):
                v.wait_ge(consts, START + 48)
                v.wait_ge(set_up, START + 2)
                chain = Chain(v, dve)
                chain.link(nc.vector.tensor_scalar(neg_a[:, :, :], neg_a[:, :, :], -1.0, None, ALU.mult))
                v.sem_inc(set_up, 1)
                for m in range(DT):
                    chain.link(nc.vector.tensor_scalar(diag[:, m], ident[:, :], dskip[:, m:m + 1], None, ALU.mult))
                v.sem_inc(set_up, 1)
                v.sem_inc(scanned, FREE)

                def step(i, c, s, g, k):
                    v.wait_ge(bc_loaded[k], START + 16 * (4 * c + g + 1))

                    def scan(m):
                        n = count(c, g, k, m)
                        v.wait_ge(decay_ready, START + n + 1)
                        v.wait_ge(drive_ready, START + n + 1)
                        nc.vector.tensor_tensor_scan(state[m][:, :], decay[m][:, :], drive[m][:, :], 0.0, ALU.mult, ALU.add).then_inc(scanned, 1)

                    def see(m):
                        n = count(c, g, k, m)
                        v.wait_ge(summed, START + n)
                        v.wait_ge(scanned, START + n + 1 + FREE)
                        nc.vector.tensor_tensor(seen[m][:, :], state[m][:, :], BC[k][:, 1], ALU.mult).then_inc(seen_ready, 1)

                    scan(0)
                    for m in range(1, DT):
                        scan(m)
                        see(m - 1)
                    see(DT - 1)

                def after(i, c, s):
                    v.wait_ge(uz_loaded, START + 32 * c + 32)
                    for m in range(DT):
                        v.wait_ge(y_ready, START + DT * c + m + 1)
                        nc.vector.tensor_tensor(z[:, m], z[:, m], y[m][:, :], ALU.mult).then_inc(gated, 1)
                on_states(v, lambda i, c, s: None, step, after)

            @block.tensor
            def _(pe):
                pe.wait_ge(set_up, START + 4)
                pe.sem_inc(summed, FREE)

                def before(i, c, s):
                    pe.wait_ge(gated, START + DT * c)
                    for m in range(DT):
                        for half in range(HALVES):
                            nc.tensor.matmul(y[m][:, half * NW:(half + 1) * NW], zero[:, 0:P], zero[:, :], start=True, stop=False)

                def step(i, c, s, g, k):
                    for m in range(DT):
                        pe.wait_ge(seen_ready, START + count(c, g, k, m) + 1)
                        for half in range(HALVES):
                            last = nc.tensor.matmul(y[m][:, half * NW:(half + 1) * NW], ident[:, :], seen[m][:, half * NW:(half + 1) * NW],
                                                    start=False, stop=False)
                        last.then_inc(summed, 1)

                def after(i, c, s):
                    pe.wait_ge(uz_loaded, START + 32 * c + 32)
                    for m in range(DT):
                        for half in range(HALVES):
                            last = nc.tensor.matmul(y[m][:, half * NW:(half + 1) * NW], diag[:, m], u[:, m, half * NW:(half + 1) * NW],
                                                    start=False, stop=True)
                        last.then_inc(y_ready, 1)
                on_states(pe, before, step, after)


def stage_outer(nc, gated_d, x1, norm, avg_d, outw_d, lnp_d, res_d, h2_d):
    with ExitStack() as stack:
        s_ = Scope(nc, stack, "outer")
        avg = s_.sb("avg", [P, P])
        outw = s_.sb("outw", [P, DT, H])
        lnp = s_.sb("lnp", [P, HT, 2])
        gate = [s_.sb(f"gated{s}", [P, DT, W]) for s in range(2)]
        xc = [s_.sb(f"x{s}", [P, HT, W]) for s in range(2)]
        xg = s_.sb("xg", [P, HT, W])
        x2 = s_.sb("x2", [P, HT, W])
        res = s_.sb("res", [P, HT, W])
        cen = s_.sb("cen", [P, HT, W])
        sq = s_.sb("sq", [P, HT, W])
        var = s_.sb("var", [P, W])
        rstd = s_.sb("rstd", [P, W])
        eps = s_.sb("eps", [P, 1])
        hn = s_.sb("hn", [P, HT, W])
        acc = [s_.ps(f"acc{k}", [P, W]) for k in range(2)]
        mean_ps, var_ps = s_.ps("mean_acc", [P, W]), s_.ps("var_acc", [P, W])
        consts, set_up = s_.sem("consts"), s_.sem("set_up")
        loaded = s_.sems("loaded", 2)
        out_ready, xg_ready, x2_ready, res_ready = (s_.sem(k) for k in ("out_ready", "xg_ready", "x2_ready", "res_ready"))
        mean_ready, cen_ready, sq_ready, var_ready = (s_.sem(k) for k in ("mean_ready", "cen_ready", "sq_ready", "var_ready"))
        var_copied, rstd_ready, hn_ready, h_ready = (s_.sem(k) for k in ("var_copied", "rstd_ready", "hn_ready", "h_ready"))
        res_stored, h_stored = s_.sem("res_stored"), s_.sem("h_stored")

        s_.start()
        with nc.Block() as block:
            @block.sync
            def _(sp):
                for dst, src in ((avg[:, :], avg_d), (outw[:, :, :], outw_d), (lnp[:, :, :], lnp_d)):
                    sp.dma_start(dst, src).then_inc(consts, 16)

                def load(c, s):
                    sp.dma_start(gate[s][:, :, :], gated_d[c]).then_inc(loaded[s], 16)
                    sp.dma_start(xc[s][:, :, :], x1.rearrange("c (k p) w -> c p k w", p=P)[c]).then_inc(loaded[s], 16)

                def store(c, s):
                    view = lambda t: t.rearrange("c (k p) w -> c p k w", p=P)[c]
                    sp.wait_ge(res_ready, START + c + 1)
                    sp.dma_start(view(res_d), res[:, :, :]).then_inc(res_stored, 16)
                    sp.wait_ge(h_ready, START + HT * c + HT)
                    sp.dma_start(view(h2_d), hn[:, :, :]).then_inc(h_stored, 16)

                for s in range(2):
                    load(s, s)
                with sp.Fori(0, C // 2 - 1) as i:
                    for s in range(2):
                        store(2 * i + s, s)
                        load(2 * i + s + 2, s)
                for s in range(2):
                    store(C - 2 + s, s)
                sp.wait_ge(res_stored, START + 16 * C)
                sp.wait_ge(h_stored, START + 16 * C)

            @block.tensor
            def _(pe):
                pe.wait_ge(consts, START + 48)
                with pe.Fori(0, C // 2) as i:
                    for s in range(2):
                        c = 2 * i + s
                        pe.wait_ge(loaded[s], START + 32 * i + 32)
                        for g in range(HT):
                            pe.wait_ge(x2_ready, START + HT * c)
                            for half in range(HALVES):
                                for k in range(DT):
                                    last = nc.tensor.matmul(acc[g][:, half * NW:(half + 1) * NW], outw[:, k, g * P:(g + 1) * P],
                                                            gate[s][:, k, half * NW:(half + 1) * NW], start=k == 0, stop=k == DT - 1)
                            last.then_inc(out_ready, 1)
                        for src, ready, n, dst, done in ((x2, x2_ready, HT, mean_ps, mean_ready), (sq, sq_ready, 1, var_ps, var_ready)):
                            pe.wait_ge(ready, START + n * c + n)
                            for half in range(HALVES):
                                for k in range(HT):
                                    last = nc.tensor.matmul(dst[:, half * NW:(half + 1) * NW], avg[:, :], src[:, k, half * NW:(half + 1) * NW],
                                                            start=k == 0, stop=k == HT - 1)
                            last.then_inc(done, 1)

            @block.scalar
            def _(act):
                act.wait_ge(consts, START + 48)
                act.wait_ge(set_up, START + 1)
                with act.Fori(0, C) as c:
                    act.wait_ge(cen_ready, START + HT * c + HT)
                    nc.scalar.activation(sq[:, :, :], cen[:, :, :], ACT.Square).then_inc(sq_ready, 1)
                    act.wait_ge(var_ready, START + c + 1)
                    nc.scalar.activation(var[:, :], var_ps[:, :], ACT.Sqrt, bias=eps[:, :]).then_inc(var_copied, 1)
                    for k in range(HT):
                        act.wait_ge(hn_ready, START + HT * c + k + 1)
                        nc.scalar.activation(hn[:, k], hn[:, k], ACT.Identity, scale=lnp[:, k, 0:1], bias=lnp[:, k, 1:2]).then_inc(h_ready, 1)

            @block.gpsimd
            def _(gp):
                nc.gpsimd.memset(eps[:, :], EPS).then_inc(set_up, 1)
                with gp.Fori(0, C // 2) as i:
                    for s in range(2):
                        c = 2 * i + s
                        gp.wait_ge(x2_ready, START + HT * c + HT)
                        gp.wait_ge(res_stored, START + 16 * c)
                        nc.gpsimd.tensor_tensor(res[:, :, :], xc[s][:, :, :], x2[:, :, :], ALU.add).then_inc(res_ready, 1)

            @block.vector
            def _(v):
                with v.Fori(0, C // 2) as i:
                    for s in range(2):
                        c = 2 * i + s
                        v.wait_ge(loaded[s], START + 32 * i + 32)
                        nc.vector.tensor_scalar(xg[:, :, :], xc[s][:, :, :], norm[:, bass.ds(c, 1)], norm[:, bass.ds(C + c, 1)],
                                                ALU.mult, ALU.add).then_inc(xg_ready, 1)
                        v.wait_ge(xg_ready, START + c + 1)
                        v.wait_ge(res_ready, START + c)
                        for g in range(HT):
                            v.wait_ge(out_ready, START + HT * c + g + 1)
                            nc.vector.tensor_tensor(x2[:, g], acc[g][:, :], xg[:, g], ALU.add).then_inc(x2_ready, 1)
                        v.wait_ge(mean_ready, START + c + 1)
                        v.wait_ge(x2_ready, START + HT * c + HT)
                        for k in range(HT):
                            nc.vector.tensor_tensor(cen[:, k], x2[:, k], mean_ps[:, :], ALU.subtract).then_inc(cen_ready, 1)
                        v.wait_ge(var_copied, START + c + 1)
                        nc.vector.reciprocal(rstd[:, :], var[:, :]).then_inc(rstd_ready, 1)
                        v.wait_ge(rstd_ready, START + c + 1)
                        v.wait_ge(cen_ready, START + HT * c + HT)
                        v.wait_ge(h_stored, START + 16 * c)
                        for k in range(HT):
                            nc.vector.tensor_tensor(hn[:, k], cen[:, k], rstd[:, :], ALU.mult).then_inc(hn_ready, 1)


def stage_perceptron(nc, name, w_d, bias_d, src_d, kt, mt, cols, dst_d, add_d=None):
    with ExitStack() as stack:
        s_ = Scope(nc, stack, name)
        CK = KD
        CH = kt // CK
        N = mt * CH
        GROUPS = W // cols
        STAGING = 4 * W // cols
        src_hi, src_lo = s_.sb("src_hi", [P, kt, cols], F32R), s_.sb("src_lo", [P, kt, cols], F32R)
        staged = [s_.sb(f"staged{k}", [P, cols]) for k in range(STAGING)]
        raw = [s_.sb(f"raw{s}", [P, CK * P]) for s in range(2)]
        w_hi = [s_.sb(f"w_hi{s}", [P, CK * P], F32R) for s in range(2)]
        w_lo = [s_.sb(f"w_lo{s}", [P, CK * P], F32R) for s in range(2)]
        bias = s_.sb("bias", [P, mt])
        out = [s_.sb(f"out{t}", [P, cols]) for t in range(2)]
        add = [s_.sb(f"add{t}", [P, cols]) for t in range(2)] if add_d is not None else None
        acc = [s_.ps(f"acc{t}", [P, cols]) for t in range(2)]
        bias_loaded = s_.sem("bias_loaded")
        staged_loaded = s_.sems("staged_loaded", STAGING)
        raw_loaded = s_.sems("raw_loaded", 2)
        src_hi_ready, src_lo_ready = s_.sem("src_hi_ready"), s_.sem("src_lo_ready")
        w_hi_ready, w_lo_ready = s_.sem("w_hi_ready"), s_.sem("w_lo_ready")
        src_used = s_.sem("src_used")
        w_used = s_.sem("w_used")
        finished = s_.sem("finished")
        stored = s_.sems("stored", 2)
        add_loaded = s_.sems("add_loaded", 2)

        s_.start()
        with nc.Block() as block:
            @block.sync
            def _(sp):
                def load_source(g, tiles):
                    for k in tiles:
                        r = g * kt + k
                        if r >= STAGING:
                            sp.wait_ge(src_lo_ready, START + r - STAGING + 1)
                        sp.dma_start(staged[r % STAGING][:, :], src_d[k, :, g * cols:(g + 1) * cols]).then_inc(staged_loaded[r % STAGING], 16)

                def load_chunk(n, j, s):
                    if isinstance(n, int) and n < 2:
                        sp.dma_start(raw[s][:, :], w_d[j]).then_inc(raw_loaded[s], 16)
                    else:
                        sp.wait_ge(w_lo_ready, START + n - 1)
                        sp.dma_start(raw[s][:, :], w_d[j]).then_inc(raw_loaded[s], 16)

                load_chunk(0, 0, 0)
                sp.dma_start(bias[:, :], bias_d).then_inc(bias_loaded, 16)
                load_source(0, range(0, 4))
                load_chunk(1, 1, 1)
                for g in range(GROUPS):
                    load_source(g, range(0 if g else 4, kt // 2))
                    for s in range(2):
                        load_chunk(g * N + 2 + s, 2 + s, s)
                    load_source(g, range(kt // 2, kt))
                    with sp.Fori(2, N // 2) as i:
                        for s in range(2):
                            load_chunk(g * N + 2 * i + s, 2 * i + s, s)
                    if g + 1 < GROUPS:
                        for s in range(2):
                            load_chunk((g + 1) * N + s, s, s)

            @block.tensor
            def _(pe):
                def tile(g, i, t):
                    first, last_tile = isinstance(i, int) and i + t == 0, isinstance(i, int) and 2 * i + t == mt - 1
                    q = g * mt + 2 * i + t
                    if not (isinstance(q, int) and q < 2):
                        pe.wait_ge(finished, START + q - 1)
                    for c in range(CH):
                        s = (t * CH + c) % 2
                        pe.wait_ge(w_lo_ready, START + q * CH + c + 1)
                        for j in range(CK):
                            k = c * CK + j
                            if first:
                                pe.wait_ge(src_lo_ready, START + g * kt + k + 1)
                            for half in range(cols // NW):
                                h = slice(half * NW, (half + 1) * NW)
                                for wp, sr in ((w_hi, src_hi), (w_hi, src_lo), (w_lo, src_hi)):
                                    last = nc.tensor.matmul(acc[t][:, h], wp[s][:, j * P:(j + 1) * P], sr[:, k, h],
                                                            start=k == 0 and wp is w_hi and sr is src_hi,
                                                            stop=k == kt - 1 and wp is w_lo)
                            if last_tile and g + 1 < GROUPS and j < CK - 1:
                                last.then_inc(src_used, 1)
                        last.then_inc(w_used, 1)

                for g in range(GROUPS):
                    for t in range(2):
                        tile(g, 0, t)
                    with pe.Fori(1, mt // 2 - 1) as i:
                        for t in range(2):
                            tile(g, i, t)
                    for t in range(2):
                        tile(g, mt // 2 - 1, t)

            def on_tiles(eng, split_source, split_chunk, finish):
                for g in range(GROUPS):
                    def step(i, t, splits=CH):
                        for c in range(splits):
                            split_chunk(g * N + (2 * i + t) * CH + c + 2, (t * CH + c) % 2)
                        finish(g, i, t)

                    split_chunk(g * N, 0)
                    split_source(g, range(kt // 2))
                    split_chunk(g * N + 1, 1)
                    if g:
                        finish(g - 1, mt // 2 - 1, 1)
                    split_source(g, range(kt // 2, kt))
                    with eng.Fori(0, mt // 2 - 1) as i:
                        for t in range(2):
                            step(i, t)
                    step(mt // 2 - 1, 0, CH if CH > 1 else 0)
                finish(GROUPS - 1, mt // 2 - 1, 1)

            @block.scalar
            def _(act):
                def split_source(g, tiles):
                    for k in tiles:
                        r = g * kt + k
                        act.wait_ge(staged_loaded[r % STAGING], START + 16 * (r // STAGING + 1))
                        if g:
                            if k % CK < CK - 1:
                                act.wait_ge(src_used, START + (g - 1) * (kt - CH) + k // CK * (CK - 1) + k % CK + 1)
                            else:
                                act.wait_ge(w_used, START + (g - 1) * N + N - CH + k // CK + 1)
                        nc.scalar.activation(src_hi[:, k], staged[r % STAGING][:, :], ACT.Copy).then_inc(src_hi_ready, 1)

                def split_chunk(n, s):
                    if isinstance(n, int):
                        act.wait_ge(raw_loaded[s], START + 16 * (n // 2 + 1))
                    else:
                        act.wait_ge(raw_loaded[s], START + 8 * (n - s) + 16)
                    if not (isinstance(n, int) and n < 2):
                        act.wait_ge(w_used, START + n - 1)
                    nc.scalar.activation(w_hi[s][:, :], raw[s][:, :], ACT.Copy).then_inc(w_hi_ready, 1)

                def load_add(g, m, t):
                    act.dma_start(add[t][:, :], add_d[m][:, g * cols:(g + 1) * cols]).then_inc(add_loaded[t], 16)

                def finish(g, i, t):
                    q = g * mt + 2 * i + t
                    if add_d is None:
                        act.wait_ge(w_used, START + (q + 1) * CH)
                        act.wait_ge(stored[t], START + 8 * (q - t))
                        nc.scalar.activation(out[t][:, :], acc[t][:, :], ACT.Relu,
                                             bias=bias[:, bass.ds(2 * i + t, 1)]).then_inc(finished, 1)
                    act.wait_ge(finished, START + q + 1)
                    act.dma_start(dst_d[2 * i + t][:, g * cols:(g + 1) * cols], out[t][:, :]).then_inc(stored[t], 16)
                    if add_d is not None:
                        if not isinstance(i, int) or 2 * i + t + 2 < mt:
                            load_add(g, 2 * i + t + 2, t)
                        elif g + 1 < GROUPS:
                            load_add(g + 1, t, t)

                if add_d is not None:
                    for t in range(2):
                        load_add(0, t, t)
                act.wait_ge(bias_loaded, START + 16)
                on_tiles(act, split_source, split_chunk, finish)
                for t in range(2):
                    act.wait_ge(stored[t], START + 16 * (GROUPS * mt // 2))

            @block.vector
            def _(v):
                def split_source(g, tiles):
                    for k in tiles:
                        r = g * kt + k
                        v.wait_ge(src_hi_ready, START + r + 1)
                        nc.vector.tensor_tensor(src_lo[:, k], staged[r % STAGING][:, :], src_hi[:, k].bitcast(F32), ALU.subtract).then_inc(src_lo_ready, 1)

                def split_chunk(n, s):
                    v.wait_ge(w_hi_ready, START + n + 1)
                    nc.vector.tensor_tensor(w_lo[s][:, :], raw[s][:, :], w_hi[s][:, :].bitcast(F32), ALU.subtract).then_inc(w_lo_ready, 1)

                def finish(g, i, t):
                    if add_d is not None:
                        q = g * mt + 2 * i + t
                        v.wait_ge(w_used, START + (q + 1) * CH)
                        v.wait_ge(add_loaded[t], START + 8 * (q - t) + 16)
                        v.wait_ge(stored[t], START + 8 * (q - t))
                        nc.vector.scalar_tensor_tensor(out[t][:, :], acc[t][:, :], bias[:, bass.ds(2 * i + t, 1)], add[t][:, :],
                                                       ALU.add, ALU.add).then_inc(finished, 1)

                v.wait_ge(bias_loaded, START + 16)
                on_tiles(v, split_source, split_chunk, finish)


def build(nc, t, out):
    def scratch(name, shape):
        return nc.dram_tensor(f"scratch_{name}", shape, F32, kind="Internal").ap()

    y = scratch("y", [3, C, H, W])
    q_parts, k_parts = scratch("q", [2, C * H, W]), scratch("k", [2, C * H, W])
    v_heads = scratch("v", [NH, P, KT * D])
    att, den, rden = scratch("att", [NH, D, W]), scratch("den", [NH, W]), scratch("rden", [NH, W])
    mixed, x1 = scratch("mixed", [C, H, W]), scratch("x1", [C, H, W])
    u_d, z_d, dt_d, dtu_d, gated_d = (scratch(k, [C, P, DT, W]) for k in ("u", "z", "dt", "dtu", "gated"))
    bc = scratch("bc", [C, 2 * DS, W])
    res_d, h2_d = scratch("res", [C, H, W]), scratch("h2", [C, H, W])
    hid_d = scratch("hid", [MT, P, W])
    norm = nc.alloc_sbuf_tensor("norm", [P, 2 * C], F32)

    stage_project(nc, t["x"], t["w_qkv"], y)
    stage_convolve(nc, y, t["kron"], t["cbias"], t["vbias"], t["rot"], t["cos"], t["sin"], q_parts, k_parts, v_heads)
    stage_attend(nc, q_parts, k_parts, v_heads, t["ident"], t["mask"], att, den)
    stage_recombine(nc, att, den, rden, t["wo"], mixed)
    stage_mix(nc, mixed, t["kmix"], t["x"], t["gavg"], t["sel"], x1, norm)
    stage_inner(nc, x1, norm, t["avg"], t["inw"], t["ln1"], t["taps"], t["xpw"], t["dtw"], bc, u_d, z_d, dt_d, dtu_d)
    stage_scan(nc, dt_d, dtu_d, u_d, z_d, bc, t["alog"], t["dskip"], t["ident"], gated_d)
    stage_outer(nc, gated_d, x1, norm, t["avg"], t["outw"], t["ln2"], res_d, h2_d)
    tiles = lambda a: a.rearrange("c (k p) w -> (c k) p w", p=P)
    stage_perceptron(nc, "up", t["w1"], t["b1"], tiles(h2_d), KD, MT, W, hid_d)
    stage_perceptron(nc, "down", t["w2"], t["b2"], hid_d, MT, KD, NW, tiles(out[0]), tiles(res_d))


def constants():
    p = np.arange(P)
    out = {"ident": np.eye(P, dtype=np.float32)}
    rot = np.zeros((P, P), np.float32)
    rot[p ^ 1, p] = 1
    out["rot"] = rot
    inv = np.float32(1.0) / np.float32(10000.0) ** (np.arange(0, D, 2, dtype=np.float32) / np.float32(D))
    freqs = np.repeat(np.arange(W, dtype=np.float32)[:, None] * inv.astype(np.float32), 2, axis=-1)
    d = p[:, None] % HB + HB * np.arange(2)[None, :]
    sign = np.where(d % 2 == 0, -1.0, 1.0).astype(np.float32)
    out["cos"] = np.ascontiguousarray(np.cos(freqs).T[d])
    out["sin"] = np.ascontiguousarray(np.sin(freqs).T[d] * sign[:, :, None])
    mask = np.zeros((2 * KT, KT, P), np.float32)
    for t in range(KT):
        mask[t, t] = mask[KT + t, t] = 1
    out["mask"] = mask
    out["gavg"] = (p[:, None] // (GROUP * HB) == p[None, :] // (GROUP * HB)).astype(np.float32) / (GROUP * HB)
    out["sel"] = (p[:, None] // HB == np.arange(C)[None, :]).astype(np.float32) / HB
    out["avg"] = np.full((P, P), 1.0 / H, np.float32)
    return out


def spread_rows(m):
    k = np.zeros((C, HB, C, HB), np.float32)
    for r in range(HB):
        k[:, r, :, r] = m.T
    return k.reshape(P, P)


def cols(v, n):
    return v.reshape(n, P).T


def lay_out(i):
    t = constants()
    t["x"] = i["x"]
    L0, L1 = "L0_conv_", "L1_conv_"

    def contraction_first(w):
        w = np.swapaxes(w, -1, -2)
        w = w.reshape(*w.shape[:-2], w.shape[-2] // P, P, w.shape[-1])
        return np.swapaxes(w, -3, -2)

    parts = [contraction_first(i[f"{L0}W{n}_pw"]).reshape(C, P, HT * H) for n in "qkv"]
    parts += [np.swapaxes(i[f"{L0}b{n}_pw"].reshape(C, HT, P), 1, 2) for n in "qkv"]
    t["w_qkv"] = np.concatenate(parts, axis=2)
    t["kron"] = np.stack([np.stack([spread_rows(i[f"{L0}W{n}_conv"][:, :, 0, tap]) for tap in range(CT)], 1) for n in "qkv"], 1)
    t["cbias"] = np.stack([np.repeat(i[f"{L0}b{n}_conv"], HB) for n in "qk"], 1)
    t["vbias"] = np.broadcast_to(np.repeat(i[f"{L0}bv_conv"], HB), (P, P))
    t["wo"] = contraction_first(i[L0 + "Wo_pw"])
    t["kmix"] = spread_rows(i[L0 + "Wo_dw"])
    t["inw"] = contraction_first(i[L1 + "in_proj_w"])
    for n in "12":
        t["ln" + n] = np.stack([cols(i[f"{L1}n{n}_g"], HT), cols(i[f"{L1}n{n}_b"], HT)], 2)
    taps = [cols(i[L1 + "conv_w"][:, k], DT) for k in range(TAPS)] + [cols(i[L1 + "conv_b"], DT), cols(i[L1 + "dt_proj_b"], DT)]
    t["taps"] = np.stack(taps, 2)
    t["xpw"] = contraction_first(i[L1 + "x_proj_w"])
    t["dtw"] = i[L1 + "dt_proj_w"].T
    t["alog"] = np.swapaxes(i[L1 + "A_log"].reshape(DT, P, DS), 0, 1)
    t["dskip"] = cols(i[L1 + "D_skip"], DT)
    t["outw"] = contraction_first(i[L1 + "out_proj_w"])
    for n, kt, mt in (("1", KD, MT), ("2", MT, KD)):
        w = i[f"{L1}pw{n}_w"].reshape(mt, P, kt // KD, KD, P).transpose(0, 2, 4, 3, 1)
        t["w" + n] = w.reshape(mt * (kt // KD), P, KD * P)
        t["b" + n] = cols(i[f"{L1}pw{n}_b"], mt)
    return t


def kernel(**inputs):
    import concourse.bacc as bacc
    from concourse.bass_utils import run_bass_kernel_spmd

    nc = bacc.Bacc("TRN2", target_bir_lowering=False, num_devices=1)
    arrays, t = {}, {}
    for name, a in lay_out({k: np.asarray(v) for k, v in inputs.items()}).items():
        a = np.ascontiguousarray(a)
        arrays[f"in_{name}"] = a
        t[name] = nc.dram_tensor(f"in_{name}", a.shape, mybir.dt.from_np(a.dtype), kind="ExternalInput").ap()
    out = nc.dram_tensor("out", (1, C, H, W), F32, kind="ExternalOutput").ap()
    build(nc, t, out)
    r = run_bass_kernel_spmd(nc, [arrays], core_ids=[0])
    return r.results[0]["out"]
```

```python
import numpy as np

import concourse.bass as bass
from concourse import mybir
from contextlib import ExitStack

F32 = mybir.dt.float32
F32R = mybir.dt.float32r
ALU = mybir.AluOpType
ACT = mybir.ActivationFunctionType
AX = mybir.AxisListType

P = 128
C = 8
H = 256
W = 1024
HT = H // P
NW = 512
HALVES = W // NW
HB = P // C
NB = H // HB
GROUP = 2
NG = C // GROUP
HEADS = 8
D = H // HEADS
NH = C * HEADS
KT = W // P
DI = 512
DT = DI // P
DS = 16
RANK = 16
TAPS = 4
CT = 3
HID = 4096
MT = HID // P
CD = C * H
KD = CD // P
EPS = 1e-5
START = 1


class Scope:

    def __init__(self, nc, stack, name):
        self.nc, self.stack, self.name, self.own = nc, stack, name, []
        stack.callback(self.give_back)

    def give_back(self):
        self.nc.all_engine_barrier()
        self.nc.clear_and_free_semaphores(self.own)
        self.nc.all_engine_barrier()

    def start(self):
        for sem in self.own:
            self.nc.sync.sem_inc(sem, START)
        self.nc.all_engine_barrier()

    def sb(self, name, shape, dt=F32):
        return self.stack.enter_context(self.nc.sbuf_tensor(f"{self.name}_{name}", shape, dt))

    def ps(self, name, shape, dt=F32):
        return self.stack.enter_context(self.nc.psum_tensor(f"{self.name}_{name}", shape, dt))

    def sem(self, name):
        self.own.append(self.nc.alloc_semaphore(f"{self.name}_{name}"))
        return self.own[-1]

    def sems(self, name, n):
        return [self.sem(f"{name}{i}") for i in range(n)]


class Chain:

    def __init__(self, eng, sem, base=0):
        self.eng, self.sem, self.base, self.n = eng, sem, base, 0

    def link(self, ins):
        self.n += 1
        ins.then_inc(self.sem, 1)
        self.eng.wait_ge(self.sem, START + self.base + self.n)


def halves(t):
    return [slice(i * NW, (i + 1) * NW) for i in range(HALVES)]


def stage_project(nc, x, w_qkv, y):
    with ExitStack() as stack:
        s_ = Scope(nc, stack, "project")
        X = s_.sb("x", [P, C, HT, W])
        WB = HT * H
        NWT = 3 * WB + 3 * HT
        w = [s_.sb(f"w{s}", [P, NWT]) for s in range(2)]
        xn = [s_.sb(f"xn{s}", [P, HT, W]) for s in range(2)]
        x_hi, x_lo = ([s_.sb(f"{n}{s}", [P, HT, W], F32R) for s in range(2)] for n in ("x_hi", "x_lo"))
        w_hi, w_lo = ([s_.sb(f"{n}{s}", [P, 3 * WB], F32R) for s in range(2)] for n in ("w_hi", "w_lo"))
        ybuf = [s_.sb(f"y{s}", [P, W]) for s in range(4)]
        stats = s_.sb("stats", [P, C, 4, 6])
        mv = s_.sb("mv", [P, NG, 2])
        avg = s_.sb("avg", [P, P])
        mean = s_.sb("mean", [P, NG])
        dev = s_.sb("dev", [P, NG])
        var = s_.sb("var", [P, NG])
        rstd = s_.sb("rstd", [P, NG])
        shift = s_.sb("shift", [P, NG])
        epsc = s_.sb("eps", [P, 1])
        acc = [s_.ps(f"acc{k}", [P, W]) for k in range(4)]
        x_loaded = s_.sems("x_loaded", C)
        w_loaded = s_.sems("w_loaded", 2)
        dve = s_.sem("dve")
        stat_ready, stat_summed = s_.sem("stat_ready"), s_.sem("stat_summed")
        var_ready, sd_ready, norm_ready = s_.sem("var_ready"), s_.sem("sd_ready"), s_.sem("norm_ready")
        xn_ready = s_.sem("xn_ready")
        hi_ready, lo_ready = s_.sem("hi_ready"), s_.sem("lo_ready")
        multiplied = s_.sem("multiplied")
        biased = s_.sem("biased")
        stored = s_.sems("stored", 4)
        TILES = 3 * HT

        s_.start()
        with nc.Block() as block:
            @block.sync
            def _(sp):
                for c in range(C):
                    sp.dma_start(X[:, c], x[0, c].rearrange("(k p) w -> p k w", p=P)).then_inc(x_loaded[c], 16)
                for s in range(2):
                    sp.dma_start(w[s][:, :], w_qkv[s]).then_inc(w_loaded[s], 16)

                def store(c, i, s):
                    for n in range(TILES):
                        k = s * TILES + n
                        sp.wait_ge(biased, START + c * TILES + n + 1)
                        sp.dma_start(y[n // HT, c, (n % HT) * P:(n % HT + 1) * P, :],
                                     ybuf[k % 4][:, :]).then_inc(stored[k % 4], 16)

                with sp.Fori(0, C // 2 - 1) as i:
                    for s in range(2):
                        store(2 * i + s, i, s)
                        sp.dma_start(w[s][:, :], w_qkv[2 * i + 2 + s]).then_inc(w_loaded[s], 16)
                for s in range(2):
                    store(C - 2 + s, C // 2 - 1, s)
                for k in range(4):
                    sp.wait_ge(stored[k], START + 16 * (C * TILES // 4))

            @block.vector
            def _(v):
                nc.vector.memset(avg[:, :], 1.0 / P).then_inc(dve, 1)
                nc.vector.memset(epsc[:, :], EPS).then_inc(dve, 1)
                for c in range(C):
                    v.wait_ge(x_loaded[c], START + 16)
                    for q in range(4):
                        nc.vector.bn_stats(stats[:, c, q], X[:, c, q // 2, (q % 2) * NW:(q % 2 + 1) * NW]).then_inc(dve, 1)
                chain = Chain(v, dve, 2 + 4 * C)
                v.wait_ge(dve, START + 2 + 4 * C)
                for g in range(NG):
                    chain.link(nc.vector.bn_aggr(mv[:, g], stats[:, GROUP * g:GROUP * (g + 1)].rearrange("p c q s -> p (c q s)")))
                v.sem_inc(stat_ready, 1)
                v.wait_ge(stat_summed, START + 1)
                chain.link(nc.vector.tensor_copy(mean[:, :], acc[0][:, 0:NG]))
                chain.link(nc.vector.tensor_tensor(dev[:, :], mv[:, :, 0], mean[:, :], ALU.subtract))
                chain.link(nc.vector.tensor_tensor(dev[:, :], dev[:, :], dev[:, :], ALU.mult))
                nc.vector.tensor_tensor(var[:, :], dev[:, :], mv[:, :, 1], ALU.add).then_inc(var_ready, 1)
                v.wait_ge(sd_ready, START + 1)
                chain.link(nc.vector.reciprocal(rstd[:, :], dev[:, :]))
                nc.vector.scalar_tensor_tensor(shift[:, :], mean[:, :], -1.0, rstd[:, :], ALU.mult, ALU.mult).then_inc(norm_ready, 1)
                v.wait_ge(norm_ready, START + 1)
                with v.Fori(0, C // 2) as i:
                    for s in range(2):
                        v.wait_ge(lo_ready, START + 4 * i)
                        nc.vector.tensor_scalar(xn[s][:, :, :], X[:, bass.ds(2 * i + s, 1)].rearrange("p o k w -> p (o k) w"),
                                                rstd[:, bass.ds(i, 1)], shift[:, bass.ds(i, 1)],
                                                ALU.mult, ALU.add).then_inc(xn_ready, 1)
                        v.wait_ge(hi_ready, START + 2 * (2 * i + s) + 1)
                        nc.vector.tensor_tensor(x_lo[s][:, :, :], xn[s][:, :, :], x_hi[s][:, :, :].bitcast(F32), ALU.subtract).then_inc(lo_ready, 1)
                        v.wait_ge(hi_ready, START + 2 * (2 * i + s) + 2)
                        nc.vector.tensor_tensor(w_lo[s][:, :], w[s][:, 0:3 * WB], w_hi[s][:, :].bitcast(F32), ALU.subtract).then_inc(lo_ready, 1)

            @block.tensor
            def _(pe):
                pe.wait_ge(stat_ready, START + 1)
                nc.tensor.matmul(acc[0][:, 0:NG], avg[:, :], mv[:, :, 0], start=True, stop=True).then_inc(stat_summed, 1)
                pe.wait_ge(var_ready, START + 1)
                nc.tensor.matmul(acc[1][:, 0:NG], avg[:, :], var[:, :], start=True, stop=True).then_inc(stat_summed, 1)
                pe.wait_ge(norm_ready, START + 1)
                with pe.Fori(0, C // 2) as i:
                    for s in range(2):
                        pe.wait_ge(lo_ready, START + 2 * (2 * i + s) + 2)
                        for n in range(TILES):
                            k = s * TILES + n
                            if k >= 4:
                                pe.wait_ge(biased, START + i * 2 * TILES + k - 3)
                            else:
                                pe.wait_ge(biased, START + i * 2 * TILES)
                            a = acc[k % 4]
                            for h in halves(a):
                                for kt in range(HT):
                                    o = (n // HT) * WB + kt * H + (n % HT) * P
                                    for wp, xp in ((w_hi, x_hi), (w_hi, x_lo), (w_lo, x_hi)):
                                        last = nc.tensor.matmul(a[:, h], wp[s][:, o:o + P], xp[s][:, kt, h],
                                                                start=kt == 0 and wp is w_hi and xp is x_hi,
                                                                stop=kt == HT - 1 and wp is w_lo)
                            last.then_inc(multiplied, 1)

            @block.scalar
            def _(act):
                act.wait_ge(stat_summed, START + 2)
                nc.scalar.activation(dev[:, :], acc[1][:, 0:NG], ACT.Sqrt, bias=epsc[:, :]).then_inc(sd_ready, 1)

                def split(c, s):
                    act.wait_ge(xn_ready, START + c + 1)
                    if not isinstance(c, int) or c >= 2:
                        act.wait_ge(multiplied, START + (c - 1) * TILES)
                    nc.scalar.activation(x_hi[s][:, :, :], xn[s][:, :, :], ACT.Copy).then_inc(hi_ready, 1)
                    act.wait_ge(w_loaded[s], START + 8 * (c - s) + 16)
                    nc.scalar.activation(w_hi[s][:, :], w[s][:, 0:3 * WB], ACT.Copy).then_inc(hi_ready, 1)

                def add_bias(i, s):
                    for n in range(TILES):
                        k = s * TILES + n
                        act.wait_ge(multiplied, START + i * 2 * TILES + k + 1)
                        act.wait_ge(stored[k % 4], START + 16 * (i * (2 * TILES // 4) + k // 4))
                        nc.scalar.activation(ybuf[k % 4][:, :], acc[k % 4][:, :], ACT.Identity,
                                             bias=w[s][:, 3 * WB + n:3 * WB + n + 1]).then_inc(biased, 1)

                split(0, 0)
                split(1, 1)
                add_bias(0, 0)
                with act.Fori(1, C // 2) as i:
                    split(2 * i, 0)
                    add_bias(i - 1, 1)
                    split(2 * i + 1, 1)
                    add_bias(i, 0)
                add_bias(C // 2 - 1, 1)


def stage_convolve(nc, y, kron_d, cbias_d, vbias_d, rot_d, cos_d, sin_d, q_parts, k_parts, v_heads):
    with ExitStack() as stack:
        s_ = Scope(nc, stack, "conv")
        kron = s_.sb("kron", [P, 3, CT, P])
        cbias = s_.sb("cbias", [P, 2])
        vbias = s_.sb("vbias", [P, P])
        rot = s_.sb("rot", [P, P])
        cos = s_.sb("cos", [P, 2, W])
        sin = s_.sb("sin", [P, 2, W])
        yin = [[s_.sb(f"y{s}{n}", [P, W + 2]) for n in range(3)] for s in range(2)]
        qk = [s_.sb(f"qk{n}", [P, W]) for n in range(2)]
        turned = [s_.sb(f"turned{n}", [P, W]) for n in range(2)]
        kept = [s_.sb(f"kept{n}", [P, W]) for n in range(2)]
        hi = [s_.sb(f"hi{n}", [P, W], F32R) for n in range(2)]
        lo = [s_.sb(f"lo{n}", [P, W], F32R) for n in range(2)]
        vst = s_.sb("vst", [P, C, KT, 2 * HB])
        conv_ps = [s_.ps(f"conv{n}", [P, W]) for n in range(2)]
        rot_ps = s_.ps("turned", [P, W])
        v_ps = s_.ps("v", [P, W])
        consts = s_.sem("consts")
        padded = s_.sem("padded")
        y_loaded = [s_.sems(f"y_loaded{s}", 3) for s in range(2)]
        conv_done = s_.sem("conv_done")
        v_done = s_.sem("v_done")
        rot_done = s_.sem("rot_done")
        qk_ready = s_.sem("qk_ready")
        turn_taken = s_.sem("turn_taken")
        kept_ready = s_.sem("kept_ready")
        sum_ready = s_.sem("sum_ready")
        hi_ready = s_.sem("hi_ready")
        lo_ready = s_.sem("lo_ready")
        v_taken = s_.sem("v_taken")
        hi_stored, lo_stored = s_.sems("hi_stored", 2), s_.sems("lo_stored", 2)
        v_stored = s_.sem("v_stored")
        parts = [q_parts, k_parts]

        def rows(t, j):
            return t.rearrange("(c b r) w -> b c r w", c=C, r=HB)[j]

        s_.start()
        with nc.Block() as block:
            @block.sync
            def _(sp):
                for dst, src in ((kron[:, :, :, :], kron_d), (cbias[:, :], cbias_d), (vbias[:, :], vbias_d),
                                 (rot[:, :], rot_d), (cos[:, :, :], cos_d), (sin[:, :, :], sin_d)):
                    sp.dma_start(dst, src).then_inc(consts, 16)
                sp.wait_ge(padded, START + 12)

                def load(j, s):
                    for n in range(3):
                        sp.dma_start(yin[s][n][:, 1:W + 1], y[n].rearrange("c (b r) w -> b c r w", r=HB)[j]).then_inc(y_loaded[s][n], 16)

                for s in range(2):
                    load(s, s)
                with sp.Fori(1, NB // 2) as i:
                    for s in range(2):
                        sp.wait_ge(v_done, START + 2 * i + s - 1)
                        load(2 * i + s, s)

            @block.gpsimd
            def _(gp):
                for s in range(2):
                    for n in range(3):
                        nc.gpsimd.memset(yin[s][n][:, 0:1], 0.0).then_inc(padded, 1)
                        nc.gpsimd.memset(yin[s][n][:, W + 1:W + 2], 0.0).then_inc(padded, 1)
                gp.wait_ge(consts, START + 96)
                with gp.Fori(0, NB // 2) as i:
                    for s in range(2):
                        for n in range(2):
                            m = 2 * s + n
                            gp.wait_ge(qk_ready, START + 4 * i + m + 1)
                            gp.wait_ge(sum_ready, START + (4 * i + m - 1 if m >= 1 else 4 * i))
                            nc.gpsimd.tensor_tensor(kept[n][:, :], qk[n][:, :], cos[:, s], ALU.mult).then_inc(kept_ready, 1)

            @block.tensor
            def _(pe):
                pe.wait_ge(consts, START + 96)
                with pe.Fori(0, NB // 2) as i:
                    for s in range(2):
                        for n in range(2):
                            m = 2 * s + n
                            pe.wait_ge(y_loaded[s][n], START + 16 * i + 16)
                            pe.wait_ge(qk_ready, START + (4 * i + m - 1 if m >= 1 else 4 * i))
                            for h in range(HALVES):
                                for t in range(CT):
                                    last = nc.tensor.matmul(conv_ps[n][:, h * NW:(h + 1) * NW], kron[:, n, t],
                                                            yin[s][n][:, h * NW + t:h * NW + t + NW],
                                                            start=t == 0, stop=t == CT - 1)
                            last.then_inc(conv_done, 1)
                        pe.wait_ge(y_loaded[s][2], START + 16 * i + 16)
                        pe.wait_ge(v_taken, START + 2 * i + s)
                        for wt in range(KT):
                            for t in range(CT):
                                last = nc.tensor.matmul(v_ps[:, wt * P:(wt + 1) * P], yin[s][2][:, wt * P + t:wt * P + t + P],
                                                        kron[:, 2, t], start=t == 0, stop=t == CT - 1)
                        last.then_inc(v_done, 1)
                        for n in range(2):
                            m = 2 * s + n
                            pe.wait_ge(qk_ready, START + 4 * i + m + 1)
                            pe.wait_ge(turn_taken, START + 4 * i + m)
                            for h in range(HALVES):
                                last = nc.tensor.matmul(rot_ps[:, h * NW:(h + 1) * NW], rot[:, :], qk[n][:, h * NW:(h + 1) * NW],
                                                        start=True, stop=True)
                            last.then_inc(rot_done, 1)

            @block.scalar
            def _(act):
                act.wait_ge(consts, START + 96)

                def biases(i, s):
                    for n in range(2):
                        m = 2 * s + n
                        act.wait_ge(conv_done, START + 4 * i + m + 1)
                        if m >= 2:
                            act.wait_ge(rot_done, START + 4 * i + m - 1)
                            act.wait_ge(kept_ready, START + 4 * i + m - 1)
                        else:
                            act.wait_ge(rot_done, START + 4 * i)
                            act.wait_ge(kept_ready, START + 4 * i)
                        nc.scalar.activation(qk[n][:, :], conv_ps[n][:, :], ACT.Identity, bias=cbias[:, n:n + 1]).then_inc(qk_ready, 1)

                with act.Fori(0, NB // 2) as i:
                    for s in range(2):
                        biases(i, s)
                        for n in range(2):
                            m = 2 * s + n
                            act.wait_ge(sum_ready, START + 4 * i + m + 1)
                            act.wait_ge(hi_stored[n], START + 16 * (2 * i + s))
                            act.wait_ge(lo_ready, START + 4 * i + m)
                            nc.scalar.activation(hi[n][:, :], turned[n][:, :], ACT.Copy).then_inc(hi_ready, 1)
                            act.wait_ge(hi_ready, START + 4 * i + m + 1)
                            act.dma_start(rows(parts[n][0], 2 * i + s), hi[n][:, :].bitcast(F32)).then_inc(hi_stored[n], 16)
                            act.wait_ge(lo_ready, START + 4 * i + m + 1)
                            act.dma_start(rows(parts[n][1], 2 * i + s), lo[n][:, :].bitcast(F32)).then_inc(lo_stored[n], 16)
                    act.wait_ge(v_taken, START + 2 * i + 2)
                    for c in range(C):
                        act.dma_start(v_heads[HEADS * c + i], vst[:, c].rearrange("p t d -> p (t d)")).then_inc(v_stored, 16)
                for n in range(2):
                    act.wait_ge(hi_stored[n], START + 16 * NB)
                    act.wait_ge(lo_stored[n], START + 16 * NB)
                act.wait_ge(v_stored, START + 16 * C * (NB // 2))

            @block.vector
            def _(v):
                v.wait_ge(consts, START + 96)
                with v.Fori(0, NB // 2) as i:
                    for s in range(2):
                        v.wait_ge(v_done, START + 2 * i + s + 1)
                        v.wait_ge(v_stored, START + 16 * C * i)
                        nc.vector.tensor_tensor(
                            vst[:, :, :, s * HB:(s + 1) * HB].rearrange("p c t r -> p t c r"),
                            v_ps[:, :].rearrange("p (t c r) -> p t c r", t=KT, c=C),
                            vbias[:, :].rearrange("p (o c r) -> p o c r", o=1, c=C).broadcast_to([P, KT, C, HB]),
                            ALU.add).then_inc(v_taken, 1)
                        for n in range(2):
                            m = 2 * s + n
                            v.wait_ge(rot_done, START + 4 * i + m + 1)
                            v.wait_ge(hi_ready, START + (4 * i + m - 1 if m >= 1 else 4 * i))
                            nc.vector.tensor_tensor(turned[n][:, :], rot_ps[:, :], sin[:, s], ALU.mult).then_inc(turn_taken, 1)
                            v.wait_ge(turn_taken, START + 4 * i + m + 1)
                            v.wait_ge(kept_ready, START + 4 * i + m + 1)
                            nc.vector.tensor_tensor(turned[n][:, :], turned[n][:, :], kept[n][:, :], ALU.add).then_inc(sum_ready, 1)
                            v.wait_ge(hi_ready, START + 4 * i + m + 1)
                            v.wait_ge(lo_stored[n], START + 16 * (2 * i + s))
                            nc.vector.tensor_tensor(lo[n][:, :], turned[n][:, :], hi[n][:, :].bitcast(F32), ALU.subtract).then_inc(lo_ready, 1)


def stage_attend(nc, q_parts, k_parts, v_heads, ident_d, mask_d, att, den):
    with ExitStack() as stack:
        s_ = Scope(nc, stack, "attend")
        SLOTS = 4
        PARTS = 3 * D
        Q = [s_.sb(f"q{s}", [P, W], F32R) for s in range(SLOTS)]
        K = [s_.sb(f"k{s}", [P, W], F32R) for s in range(SLOTS)]
        V = [s_.sb(f"v{s}", [P, KT * D]) for s in range(SLOTS)]
        PT = [s_.sb(f"probs{t}", [P, W]) for t in range(2)]
        osb = [s_.sb(f"o{s}", [P, NW]) for s in range(SLOTS)]
        nm2 = s_.sb("negmax_halves", [P, KT, HALVES])
        nm = s_.sb("negmax", [P, KT])
        m16 = s_.sb("maxparts", [P, 2 * KT], F32R)
        ident = s_.sb("ident", [P, P])
        mask = s_.sb("mask", [2 * KT, KT, P])
        ones = s_.sb("ones", [P, D])
        onesf = s_.sb("onesf", [P, W])
        zeros = s_.sb("zeros", [P, W])
        row_ps = [s_.ps(f"rows{half}", [P, NW]) for half in range(HALVES)]
        st_ps = [s_.ps(f"cols{t}", [P, W]) for t in range(2)]
        o_ps = [s_.ps(f"out{t}", [P, NW]) for t in range(2)]
        consts = s_.sem("consts")
        set_up = s_.sem("set_up")
        loaded = s_.sems("loaded", SLOTS)
        cleared = s_.sem("cleared")
        row_ready = s_.sem("row_ready")
        row_taken = s_.sem("row_taken")
        max_split = s_.sem("max_split")
        dve = s_.sem("dve")
        st_ready = s_.sem("st_ready")
        exp_done = s_.sem("exp_done")
        pv_done = s_.sem("pv_done")
        o_copied = s_.sem("o_copied")
        stored = s_.sems("stored", SLOTS)
        PER = HALVES * KT + 1

        s_.start()
        with nc.Block() as block:
            def on_heads(eng, head):
                with eng.Fori(0, NH // SLOTS - 1) as i:
                    for s in range(SLOTS):
                        head(SLOTS * i + s, i, s, True)
                for s in range(SLOTS):
                    head(NH - SLOTS + s, NH // SLOTS - 1, s, s < SLOTS - 1)

            @block.sync
            def _(sp):
                sp.dma_start(ident[:, :], ident_d).then_inc(consts, 16)
                sp.dma_start(mask[:, :, :], mask_d).then_inc(consts, 16)

                def load(h, s):
                    q = Q[s][:, :].bitcast(F32)
                    k = K[s][:, :].bitcast(F32)
                    qs = q_parts.rearrange("a (h d) w -> h a d w", d=D)[h]
                    ks = k_parts.rearrange("a (h d) w -> h a d w", d=D)[h]
                    sp.dma_start(q[0:2 * D, :], qs).then_inc(loaded[s], 16)
                    sp.dma_start(q[2 * D:3 * D, :], qs[0]).then_inc(loaded[s], 16)
                    sp.dma_start(k[0:D, :], ks[0]).then_inc(loaded[s], 16)
                    sp.dma_start(k[D:3 * D, :], ks).then_inc(loaded[s], 16)
                    sp.dma_start(V[s][:, :], v_heads[h]).then_inc(loaded[s], 16)

                def store(h, s):
                    sp.wait_ge(o_copied, START + h + 3)
                    for half in range(HALVES):
                        r = 2 * D * half
                        sp.dma_start(att[h, :, half * NW:(half + 1) * NW], osb[s][r:r + D, :]).then_inc(stored[s], 16)
                        sp.dma_start(den[bass.ds(h, 1) if not isinstance(h, int) else slice(h, h + 1), half * NW:(half + 1) * NW],
                                     osb[s][r + D:r + D + 1, :]).then_inc(stored[s], 16)

                for s in range(SLOTS):
                    load(s, s)
                with sp.Fori(0, NH // SLOTS - 1) as i:
                    for s in range(SLOTS):
                        h = SLOTS * i + s
                        sp.wait_ge(pv_done, START + KT * (h + 1))
                        load(h + SLOTS, s)
                        store(h, s)
                for s in range(SLOTS):
                    store(NH - SLOTS + s, s)
                for s in range(SLOTS):
                    sp.wait_ge(stored[s], START + 64 * (NH // SLOTS))

            @block.gpsimd
            def _(gp):
                nc.gpsimd.memset(ones[:, :], 1.0).then_inc(set_up, 1)
                gp.wait_ge(set_up, START + 2 + SLOTS)

                def clear(s):
                    nc.gpsimd.tensor_tensor(Q[s][PARTS:, :], zeros[PARTS:, :], zeros[PARTS:, :], ALU.mult).then_inc(cleared, 1)

                for s in range(SLOTS):
                    clear(s)

                def head(h, i, s, following):
                    gp.wait_ge(st_ready, START + KT * (h + 1))
                    clear(s)
                on_heads(gp, head)

            @block.tensor
            def _(pe):
                pe.wait_ge(consts, START + 32)
                pe.wait_ge(set_up, START + 2 + SLOTS)

                def row_scores(h, s, n):
                    pe.wait_ge(row_taken, START + PER * h + max(n - 1, 0))
                    if n == 0:
                        pe.wait_ge(cleared, START + h + 1)
                    j, half = n // HALVES, n % HALVES
                    nc.tensor.matmul(row_ps[half][:, :], Q[s][:, j * P:(j + 1) * P], K[s][:, half * NW:(half + 1) * NW],
                                     start=True, stop=True).then_inc(row_ready, 1)

                def maxima_as_rows(h):
                    pe.wait_ge(max_split, START + h + 1)
                    nc.tensor.matmul(row_ps[0][0:2 * KT, 0:P], m16[:, :].bitcast(F32), ident[:, :], start=True, stop=True).then_inc(row_ready, 1)

                def column_scores(h, s, t, half):
                    cut = slice(half * NW, (half + 1) * NW)
                    last = nc.tensor.matmul(st_ps[t % 2][:, cut], K[s][:, t * P:(t + 1) * P], Q[s][:, cut], start=True, stop=True)
                    if half == HALVES - 1:
                        last.then_inc(st_ready, 1)

                def values(h, s, t, half):
                    if half == 0:
                        pe.wait_ge(exp_done, START + KT * h + t + 1)
                    for sums in range(2):
                        g = D * (2 * half + sums)
                        lhs = ones[:, :] if sums else V[s][:, t * D:(t + 1) * D]
                        last = nc.tensor.matmul(o_ps[s % 2][g:g + D, :], lhs, PT[t % 2][:, half * NW:(half + 1) * NW],
                                                start=t == 0, stop=t == KT - 1)
                    if half == HALVES - 1:
                        last.then_inc(pv_done, 1)

                PLACES = {0: (1, 2, 3), 1: (0, 2, 3), 2: (0, 2, 3), 3: (0, 2, 3), 4: (0, 2, 3), 5: (0,)}
                ROWS_AT = (6, 0)

                def head(h, i, s, following):
                    nh, ns, ni = h + 1, (s + 1) % SLOTS, i + (s + 1) // SLOTS
                    ahead = {}
                    if following:
                        pe.wait_ge(loaded[ns], START + 80 * (ni + 1))
                        for t, places in PLACES.items():
                            for place in places:
                                ahead[t, place] = len(ahead)

                    def place(t, k):
                        if (t, k) in ahead:
                            row_scores(nh, ns, ahead[t, k])
                        elif following and (t, k) == ROWS_AT:
                            maxima_as_rows(nh)

                    for t in range(KT):
                        for half in range(HALVES):
                            place(t, half)
                            if t + 1 < KT:
                                column_scores(h, s, t + 1, half)
                            elif following:
                                if half == 0:
                                    pe.wait_ge(row_taken, START + PER * (nh + 1))
                                column_scores(nh, ns, 0, half)
                        place(t, 2)
                        if t == 0:
                            pe.wait_ge(o_copied, START + h + 1)
                        values(h, s, t, 0)
                        place(t, 3)
                        values(h, s, t, 1)

                pe.wait_ge(loaded[0], START + 80)
                for n in range(HALVES * KT):
                    row_scores(0, 0, n)
                maxima_as_rows(0)
                pe.wait_ge(row_taken, START + PER)
                for half in range(HALVES):
                    column_scores(0, 0, 0, half)
                on_heads(pe, head)

            @block.scalar
            def _(act):
                def head(h, i, s, following):
                    for t in range(KT):
                        act.wait_ge(st_ready, START + KT * h + t + 1)
                        nc.scalar.activation(PT[t % 2][:, :], st_ps[t % 2][:, :], ACT.Exp,
                                             scale=float(H) ** -0.5).then_inc(exp_done, 1)
                on_heads(act, head)

            @block.vector
            def _(v):
                nc.vector.memset(onesf[:, :], 1.0).then_inc(dve, 1)
                v.wait_ge(dve, START + 1)
                nc.vector.memset(zeros[:, :], 0.0).then_inc(set_up, 1)
                for s in range(SLOTS):
                    nc.vector.tensor_copy(K[s][PARTS:, :], onesf[PARTS:, :]).then_inc(set_up, 1)
                v.sem_inc(o_copied, 2)
                v.wait_ge(consts, START + 32)

                def maximum(h, s):
                    for n in range(HALVES * KT):
                        v.wait_ge(row_ready, START + PER * h + n + 1)
                        nc.vector.tensor_reduce(nm2[:, n // HALVES, n % HALVES:n % HALVES + 1], row_ps[n % HALVES][:, :],
                                                AX.X, ALU.max, negate=True).then_inc(row_taken, 1)
                    v.wait_ge(row_taken, START + PER * h + HALVES * KT)
                    nc.vector.tensor_reduce(nm[:, :], nm2[:, :, :], AX.X, ALU.min).then_inc(dve, 1)
                    v.wait_ge(dve, START + 2 * h + 2)
                    nc.vector.tensor_copy(m16[:, 0:KT], nm[:, :]).then_inc(dve, 1)
                    v.wait_ge(dve, START + 2 * h + 3)
                    nc.vector.tensor_tensor(m16[:, KT:2 * KT], nm[:, :], m16[:, 0:KT].bitcast(F32), ALU.subtract).then_inc(max_split, 1)
                    v.wait_ge(row_ready, START + PER * (h + 1))
                    nc.vector.tensor_tensor(Q[s][PARTS:PARTS + 2 * KT, :].rearrange("r (t q) -> r t q", t=KT),
                                            row_ps[0][0:2 * KT, 0:P].rearrange("r (o q) -> r o q", o=1).broadcast_to([2 * KT, KT, P]),
                                            mask[:, :, :], ALU.mult).then_inc(row_taken, 1)

                def head(h, i, s, following):
                    if following:
                        maximum(h + 1, (s + 1) % SLOTS)
                    v.wait_ge(pv_done, START + KT * (h + 1))
                    v.wait_ge(stored[s], START + 64 * i)
                    nc.vector.tensor_copy(osb[s][:, :], o_ps[s % 2][:, :]).then_inc(o_copied, 1)

                maximum(0, 0)
                on_heads(v, head)


def stage_recombine(nc, att, den, rden, wo_d, mixed):
    with ExitStack() as stack:
        s_ = Scope(nc, stack, "recombine")
        dsb = s_.sb("den", [P, NW])
        rsb = s_.sb("rden", [P, NW])
        a = [s_.sb(f"a{s}", [P, HT, W]) for s in range(2)]
        r = [s_.sb(f"r{s}", [P, HT, W]) for s in range(2)]
        w = [s_.sb(f"w{s}", [P, HT, H]) for s in range(2)]
        out = [s_.sb(f"out{k}", [P, W]) for k in range(4)]
        acc = [s_.ps(f"acc{k}", [P, W]) for k in range(4)]
        den_loaded, inverted, inverse_stored = s_.sem("den_loaded"), s_.sem("inverted"), s_.sem("inverse_stored")
        loaded = s_.sems("loaded", 2)
        divided, multiplied, copied = s_.sem("divided"), s_.sem("multiplied"), s_.sem("copied")
        stored = s_.sems("stored", 4)
        N4 = P // D

        s_.start()
        with nc.Block() as block:
            @block.sync
            def _(sp):
                view = lambda t: t.rearrange("h (a w) -> (h a) w", a=HALVES)
                sp.dma_start(dsb[:, :], view(den)).then_inc(den_loaded, 16)
                sp.wait_ge(inverted, START + 1)
                sp.dma_start(view(rden), rsb[:, :]).then_inc(inverse_stored, 16)
                sp.wait_ge(inverse_stored, START + 16)

                def load(c, s):
                    sp.dma_start(a[s][:, :, :], att.rearrange("(c k n) d w -> c (n d) k w", c=C, k=HT)[c]).then_inc(loaded[s], 16)
                    sp.dma_start(w[s][:, :, :], wo_d[c]).then_inc(loaded[s], 16)
                    for k in range(HT):
                        src = rden.rearrange("(c k n o) w -> c k n o w", c=C, k=HT, o=1)[c, k]
                        sp.dma_start(r[s][:, k, :], src.broadcast_to([N4, D, W])).then_inc(loaded[s], 16)

                def store(c, s):
                    for g in range(HT):
                        k = HT * s + g
                        sp.wait_ge(copied, START + HT * c + g + 1)
                        sp.dma_start(mixed[c, g * P:(g + 1) * P, :], out[k][:, :]).then_inc(stored[k], 16)

                for s in range(2):
                    load(s, s)
                with sp.Fori(0, C // 2 - 1) as i:
                    for s in range(2):
                        store(2 * i + s, s)
                        load(2 * i + s + 2, s)
                for s in range(2):
                    store(C - 2 + s, s)
                for k in range(4):
                    sp.wait_ge(stored[k], START + 16 * (C // 2))

            @block.vector
            def _(v):
                v.wait_ge(den_loaded, START + 16)
                nc.vector.reciprocal(rsb[:, :], dsb[:, :]).then_inc(inverted, 1)
                with v.Fori(0, C // 2) as i:
                    for s in range(2):
                        v.wait_ge(loaded[s], START + 64 * i + 64)
                        nc.vector.tensor_tensor(a[s][:, :, :], a[s][:, :, :], r[s][:, :, :], ALU.mult).then_inc(divided, 1)

            @block.tensor
            def _(pe):
                with pe.Fori(0, C // 2) as i:
                    for s in range(2):
                        pe.wait_ge(divided, START + 2 * i + s + 1)
                        pe.wait_ge(copied, START + 4 * i)
                        for g in range(HT):
                            for half in range(HALVES):
                                for k in range(HT):
                                    last = nc.tensor.matmul(acc[HT * s + g][:, half * NW:(half + 1) * NW], w[s][:, k, g * P:(g + 1) * P],
                                                            a[s][:, k, half * NW:(half + 1) * NW], start=k == 0, stop=k == HT - 1)
                            last.then_inc(multiplied, 1)

            @block.scalar
            def _(act):
                with act.Fori(0, C // 2) as i:
                    for k in range(4):
                        act.wait_ge(multiplied, START + 4 * i + k + 1)
                        act.wait_ge(stored[k], START + 16 * i)
                        nc.scalar.activation(out[k][:, :], acc[k][:, :], ACT.Copy).then_inc(copied, 1)


def stage_mix(nc, mixed, kmix_d, x, gavg_d, sel_d, x1, norm):
    with ExitStack() as stack:
        s_ = Scope(nc, stack, "mix")
        kmix = s_.sb("kmix", [P, P])
        gavg = s_.sb("gavg", [P, P])
        sel = s_.sb("sel", [P, C])
        ones = s_.sb("ones", [P, P])
        eps = s_.sb("eps", [P, 1])
        a = [s_.sb(f"a{s}", [P, W]) for s in range(2)]
        xb = [s_.sb(f"x{s}", [P, W]) for s in range(2)]
        out = [s_.sb(f"out{s}", [P, W]) for s in range(2)]
        stats = s_.sb("stats", [P, NB * HALVES, 6])
        mv = s_.sb("mv", [P, 2])
        dev = s_.sb("dev", [P, 1])
        var = s_.sb("var", [P, 1])
        both = s_.sb("both", [P, 2])
        spread = s_.sb("spread", [P, 2, C])
        acc = [s_.ps(f"acc{s}", [P, W]) for s in range(2)]
        small = [s_.ps(f"small{k}", [P, NW]) for k in range(3)]
        consts = s_.sem("consts")
        loaded = s_.sems("loaded", 2)
        multiplied, added, measured = s_.sem("multiplied"), s_.sem("added"), s_.sem("measured")
        stored = s_.sems("stored", 2)
        dve, stat_ready, summed, sd_ready = s_.sem("dve"), s_.sem("stat_ready"), s_.sem("summed"), s_.sem("sd_ready")

        s_.start()
        with nc.Block() as block:
            @block.sync
            def _(sp):
                for dst, src in ((kmix[:, :], kmix_d), (gavg[:, :], gavg_d), (sel[:, :], sel_d)):
                    sp.dma_start(dst, src).then_inc(consts, 16)

                def load(j, s):
                    sp.dma_start(a[s][:, :], mixed.rearrange("c (b r) w -> b c r w", r=HB)[j]).then_inc(loaded[s], 16)
                    sp.dma_start(xb[s][:, :], x[0].rearrange("c (b r) w -> b c r w", r=HB)[j]).then_inc(loaded[s], 16)

                def store(j, s):
                    sp.wait_ge(added, START + j + 1)
                    sp.dma_start(x1.rearrange("c (b r) w -> b c r w", r=HB)[j], out[s][:, :]).then_inc(stored[s], 16)

                for s in range(2):
                    load(s, s)
                with sp.Fori(0, NB // 2 - 1) as i:
                    for s in range(2):
                        store(2 * i + s, s)
                        load(2 * i + s + 2, s)
                for s in range(2):
                    store(NB - 2 + s, s)
                for s in range(2):
                    sp.wait_ge(stored[s], START + 16 * (NB // 2))

            @block.tensor
            def _(pe):
                pe.wait_ge(consts, START + 48)
                with pe.Fori(0, NB // 2) as i:
                    for s in range(2):
                        pe.wait_ge(loaded[s], START + 32 * i + 32)
                        pe.wait_ge(added, START + 2 * i)
                        for half in range(HALVES):
                            last = nc.tensor.matmul(acc[s][:, half * NW:(half + 1) * NW], kmix[:, :], a[s][:, half * NW:(half + 1) * NW],
                                                    start=True, stop=True)
                        last.then_inc(multiplied, 1)
                pe.wait_ge(stat_ready, START + 1)
                nc.tensor.matmul(small[0][:, 0:1], gavg[:, :], mv[:, 0:1], start=True, stop=True).then_inc(summed, 1)
                pe.wait_ge(stat_ready, START + 2)
                nc.tensor.matmul(small[1][:, 0:1], gavg[:, :], var[:, :], start=True, stop=True).then_inc(summed, 1)
                pe.wait_ge(stat_ready, START + 3)
                nc.tensor.matmul(small[2][:, 0:2 * C], ones[:, :], spread[:, :, :].rearrange("p a c -> p (a c)"),
                                 start=True, stop=True).then_inc(summed, 1)

            @block.scalar
            def _(act):
                act.wait_ge(summed, START + 2)
                nc.scalar.activation(dev[:, :], small[1][:, 0:1], ACT.Sqrt, bias=eps[:, :]).then_inc(sd_ready, 1)

            @block.vector
            def _(v):
                nc.vector.memset(ones[:, :], 1.0)
                nc.vector.memset(eps[:, :], EPS)
                with v.Fori(0, NB // 2) as i:
                    for s in range(2):
                        v.wait_ge(multiplied, START + 2 * i + s + 1)
                        v.wait_ge(stored[s], START + 16 * i)
                        nc.vector.tensor_tensor(out[s][:, :], acc[s][:, :], xb[s][:, :], ALU.add).then_inc(added, 1)
                        v.wait_ge(added, START + 2 * i + s + 1)
                        for half in range(HALVES):
                            nc.vector.bn_stats(stats[:, bass.ds(4 * i + 2 * s + half, 1)].rearrange("p o k -> p (o k)"),
                                               out[s][:, half * NW:(half + 1) * NW]).then_inc(measured, 1)
                v.wait_ge(measured, START + 2 * NB)
                v.wait_ge(consts, START + 48)
                chain = Chain(v, dve)
                chain.link(nc.vector.bn_aggr(mv[:, :], stats[:, :, :].rearrange("p q k -> p (q k)")))
                v.sem_inc(stat_ready, 1)
                v.wait_ge(summed, START + 1)
                chain.link(nc.vector.tensor_copy(both[:, 1:2], small[0][:, 0:1]))
                chain.link(nc.vector.tensor_tensor(dev[:, :], mv[:, 0:1], both[:, 1:2], ALU.subtract))
                chain.link(nc.vector.tensor_tensor(dev[:, :], dev[:, :], dev[:, :], ALU.mult))
                chain.link(nc.vector.tensor_tensor(var[:, :], dev[:, :], mv[:, 1:2], ALU.add))
                v.sem_inc(stat_ready, 1)
                v.wait_ge(sd_ready, START + 1)
                chain.link(nc.vector.reciprocal(both[:, 0:1], dev[:, :]))
                chain.link(nc.vector.scalar_tensor_tensor(both[:, 1:2], both[:, 1:2], -1.0, both[:, 0:1], ALU.mult, ALU.mult))
                for k in range(2):
                    chain.link(nc.vector.tensor_scalar(spread[:, k], sel[:, :], both[:, k:k + 1], None, ALU.mult))
                v.sem_inc(stat_ready, 1)
                v.wait_ge(summed, START + 3)
                chain.link(nc.vector.tensor_copy(norm[:, :], small[2][:, 0:2 * C]))


def stage_inner(nc, x1, norm, avg_d, inw_d, lnp_d, taps_d, xpw_d, dtw_d, bc, u_d, z_d, dt_d, dtu_d):
    with ExitStack() as stack:
        s_ = Scope(nc, stack, "inner")
        MI = 2 * DT
        avg = s_.sb("avg", [P, P])
        inw = s_.sb("inw", [P, HT, 2 * DI])
        lnp = s_.sb("lnp", [P, HT, 2])
        taps = s_.sb("taps", [P, DT, TAPS + 2])
        xpw = s_.sb("xpw", [P, DT, RANK + 2 * DS])
        dtw = s_.sb("dtw", [RANK, DI])
        xc = s_.sb("x", [P, HT, W])
        xg = s_.sb("xg", [P, HT, W])
        cen = s_.sb("cen", [P, HT, W])
        sq = s_.sb("sq", [P, HT, W])
        var = s_.sb("var", [P, W])
        rstd = s_.sb("rstd", [P, W])
        eps = s_.sb("eps", [P, 1])
        hn = [s_.sb(f"hn{p}", [P, HT, W]) for p in range(2)]
        xi = s_.sb("xi", [P, DT, TAPS - 1 + W])
        pre = [s_.sb(f"pre{k}", [P, W]) for k in range(2)]
        sigu = [s_.sb(f"sigu{k}", [P, W]) for k in range(2)]
        sigz = [s_.sb(f"sigz{k}", [P, W]) for k in range(2)]
        z = [s_.sb(f"z{k}", [P, W]) for k in range(2)]
        u = [s_.sb(f"u{p}", [P, DT, W]) for p in range(2)]
        xd = s_.sb("xd", [RANK + 2 * DS, W])
        above = [s_.sb(f"above{m}", [P, W]) for m in range(DT)]
        soft = [s_.sb(f"soft{m}", [P, W]) for m in range(DT)]
        dt = [s_.sb(f"dt{k}", [P, W]) for k in range(2)]
        dtu = [s_.sb(f"dtu{k}", [P, W]) for k in range(2)]
        in_acc = [s_.ps(f"in{k}", [P, W]) for k in range(2)]
        stat_acc, back_acc = s_.ps("stat", [P, W]), s_.ps("back", [P, W])
        consts, padded = s_.sem("consts"), s_.sem("padded")
        x_loaded = s_.sem("x_loaded")
        xg_ready, mean_ready, cen_ready = s_.sem("xg_ready"), s_.sem("mean_ready"), s_.sem("cen_ready")
        sq_ready, var_ready, var_copied = s_.sem("sq_ready"), s_.sem("var_ready"), s_.sem("var_copied")
        rstd_ready, hn_ready, h_ready = s_.sem("rstd_ready"), s_.sem("hn_ready"), s_.sem("h_ready")
        in_ready = s_.sem("in_ready")
        xi_ready, tap_done, pre_ready, sigu_ready, u_ready = (s_.sem(k) for k in ("xi_ready", "tap_done", "pre_ready", "sigu_ready", "u_ready"))
        sigz_ready, z_ready = s_.sem("sigz_ready"), s_.sem("z_ready")
        xd_ready, xd_copied = s_.sem("xd_ready"), s_.sem("xd_copied")
        dtp_ready, above_ready, abs_ready, exp_ready, soft_ready = (s_.sem(k) for k in ("dtp_ready", "above_ready", "abs_ready", "exp_ready", "soft_ready"))
        dt_ready, dtu_ready = s_.sem("dt_ready"), s_.sem("dtu_ready")
        u_stored, z_stored = s_.sems("u_stored", DT), s_.sems("z_stored", 2)
        dt_stored, dtu_stored, bc_stored = s_.sems("dt_stored", 2), s_.sems("dtu_stored", 2), s_.sem("bc_stored")

        def known(c, n):
            return isinstance(c, int) and c < n

        def on_sequences(eng, body):
            body((0, 0), None, None)
            body((1, 1), (0, 0), None)
            for p in range(2):
                body((p + 2, p), (p + 1, 1 - p), (p, p))
            with eng.Fori(2, C // 2) as i:
                for p in range(2):
                    body((2 * i + p, p), (2 * i + p - 1, 1 - p), (2 * i + p - 2, p))
            body(None, (C - 1, 1), (C - 2, 0))
            body(None, None, (C - 1, 1))

        s_.start()
        with nc.Block() as block:
            @block.sync
            def _(sp):
                for dst, src in ((avg[:, :], avg_d), (inw[:, :, :], inw_d), (lnp[:, :, :], lnp_d), (taps[:, :, :], taps_d),
                                 (xpw[:, :, :], xpw_d), (dtw[:, :], dtw_d)):
                    sp.dma_start(dst, src).then_inc(consts, 16)

                def body(front, middle, back):
                    if middle:
                        c, p = middle
                        for m in range(DT):
                            sp.wait_ge(u_ready, START + DT * c + m + 1)
                            sp.dma_start(u_d[c, :, m], u[p][:, m]).then_inc(u_stored[m], 16)
                            sp.wait_ge(z_ready, START + DT * c + m + 1)
                            sp.dma_start(z_d[c, :, m], z[m % 2][:, :]).then_inc(z_stored[m % 2], 16)
                    if back:
                        c, p = back
                        sp.wait_ge(xd_copied, START + c + 1)
                        sp.dma_start(bc[c], xd[RANK:, :]).then_inc(bc_stored, 16)
                        for m in range(DT):
                            sp.wait_ge(dt_ready, START + DT * c + m + 1)
                            sp.dma_start(dt_d[c, :, m], dt[m % 2][:, :]).then_inc(dt_stored[m % 2], 16)
                            sp.wait_ge(dtu_ready, START + DT * c + m + 1)
                            sp.dma_start(dtu_d[c, :, m], dtu[m % 2][:, :]).then_inc(dtu_stored[m % 2], 16)

                on_sequences(sp, body)
                for m in range(DT):
                    sp.wait_ge(u_stored[m], START + 16 * C)
                for k in range(2):
                    for t in (z_stored, dt_stored, dtu_stored):
                        sp.wait_ge(t[k], START + 16 * C * DT // 2)
                sp.wait_ge(bc_stored, START + 16 * C)

            @block.tensor
            def _(pe):
                pe.wait_ge(consts, START + 96)

                def product(a, rows, lhs, rhs, n):
                    for half in range(HALVES):
                        for k in range(n):
                            last = nc.tensor.matmul(a[0:rows, half * NW:(half + 1) * NW], lhs(k), rhs(k, slice(half * NW, (half + 1) * NW)),
                                                    start=k == 0, stop=k == n - 1)
                    return last

                def mean(c, p):
                    pe.wait_ge(xg_ready, START + c + 1)
                    if not known(c, 1):
                        pe.wait_ge(var_copied, START + c)
                    product(stat_acc, P, lambda k: avg[:, :], lambda k, h: xg[:, k, h], HT).then_inc(mean_ready, 1)

                def variance(c, p):
                    pe.wait_ge(sq_ready, START + c + 1)
                    product(stat_acc, P, lambda k: avg[:, :], lambda k, h: sq[:, k, h], HT).then_inc(var_ready, 1)

                def project(c, p, m):
                    if m == 0:
                        pe.wait_ge(h_ready, START + HT * c + HT)
                    if m < 2:
                        if not known(c, 1):
                            pe.wait_ge(z_ready, START + DT * c + m - 1)
                    elif m < DT + 2:
                        pe.wait_ge(xi_ready, START + DT * c + m - 1)
                    else:
                        pe.wait_ge(z_ready, START + DT * c + m - DT - 1)
                    product(in_acc[m % 2], P, lambda k: inw[:, k, m * P:(m + 1) * P], lambda k, h: hn[p][:, k, h], HT).then_inc(in_ready, 1)

                def bc_product(c, p):
                    pe.wait_ge(u_ready, START + DT * c + DT)
                    if not known(c, 1):
                        pe.wait_ge(abs_ready, START + DT * c)
                    product(back_acc, RANK + 2 * DS, lambda k: xpw[:, k], lambda k, h: u[p][:, k, h], DT).then_inc(xd_ready, 1)

                def step_product(c, p, m):
                    if m == 0:
                        pe.wait_ge(xd_copied, START + c + 1)
                    else:
                        pe.wait_ge(abs_ready, START + DT * c + m)
                    product(back_acc, P, lambda k: dtw[:, m * P:(m + 1) * P], lambda k, h: xd[0:RANK, h], 1).then_inc(dtp_ready, 1)

                def body(front, middle, back):
                    for m in range(MI):
                        if middle:
                            project(*middle, m)
                        if m == 1 and front:
                            mean(*front)
                        if m == 2 and back:
                            bc_product(*back)
                        if m == 4 and front:
                            variance(*front)
                        if 3 <= m < 3 + DT and back:
                            step_product(*back, m - 3)

                on_sequences(pe, body)

            @block.scalar
            def _(act):
                def load(c, p):
                    if not known(c, 1):
                        act.wait_ge(xg_ready, START + c)
                    act.dma_start(xc[:, :, :], x1.rearrange("c (k p) w -> c p k w", p=P)[c]).then_inc(x_loaded, 16)

                act.wait_ge(padded, START + 2)

                def square(c, p):
                    act.wait_ge(cen_ready, START + HT * c + HT)
                    if not known(c, 1):
                        act.wait_ge(var_ready, START + c)
                    nc.scalar.activation(sq[:, :, :], cen[:, :, :], ACT.Square).then_inc(sq_ready, 1)

                def root(c, p):
                    act.wait_ge(var_ready, START + c + 1)
                    if not known(c, 1):
                        act.wait_ge(rstd_ready, START + c)
                    nc.scalar.activation(var[:, :], stat_acc[:, :], ACT.Sqrt, bias=eps[:, :]).then_inc(var_copied, 1)

                def gains(c, p):
                    for k in range(HT):
                        act.wait_ge(hn_ready, START + HT * c + k + 1)
                        if not known(c, 2):
                            act.wait_ge(in_ready, START + MI * (c - 1))
                        nc.scalar.activation(hn[p][:, k], cen[:, k], ACT.Identity, scale=lnp[:, k, 0:1], bias=lnp[:, k, 1:2]).then_inc(h_ready, 1)

                def to_conv(c, p, m):
                    act.wait_ge(in_ready, START + MI * c + m + 1)
                    if not known(c, 1):
                        act.wait_ge(pre_ready, START + DT * (c - 1) + m + 1)
                    nc.scalar.activation(xi[:, m, TAPS - 1:], in_acc[m % 2][:, :], ACT.Copy).then_inc(xi_ready, 1)

                def sigmoid_u(c, p, m):
                    act.wait_ge(pre_ready, START + DT * c + m + 1)
                    if not known(c, 1) or m >= 2:
                        act.wait_ge(u_ready, START + DT * c + m - 1)
                    nc.scalar.activation(sigu[m % 2][:, :], pre[m % 2][:, :], ACT.Sigmoid).then_inc(sigu_ready, 1)

                def sigmoid_z(c, p, m):
                    act.wait_ge(in_ready, START + MI * c + DT + m + 1)
                    if not known(c, 1) or m >= 2:
                        act.wait_ge(z_ready, START + DT * c + m - 1)
                    nc.scalar.activation(sigz[m % 2][:, :], in_acc[m % 2][:, :], ACT.Sigmoid).then_inc(sigz_ready, 1)

                def copy_xd(c, p):
                    act.wait_ge(xd_ready, START + c + 1)
                    if not known(c, 1):
                        act.wait_ge(dtp_ready, START + DT * c)
                        act.wait_ge(bc_stored, START + 16 * c)
                    nc.scalar.activation(xd[:, :], back_acc[0:RANK + 2 * DS, :], ACT.Copy).then_inc(xd_copied, 1)

                def absolute(c, p, m):
                    act.wait_ge(above_ready, START + DT * c + m + 1)
                    if not known(c, 1):
                        act.wait_ge(dt_ready, START + DT * (c - 1) + m + 1)
                    nc.scalar.activation(soft[m][:, :], back_acc[:, :], ACT.Abs, bias=taps[:, m, TAPS + 1:TAPS + 2]).then_inc(abs_ready, 1)

                def exp_ln(c, p):
                    act.wait_ge(abs_ready, START + DT * c + DT)
                    for m in range(DT):
                        nc.scalar.activation(soft[m][:, :], soft[m][:, :], ACT.Exp, scale=-1.0).then_inc(exp_ready, 1)
                    for m in range(DT):
                        act.wait_ge(exp_ready, START + DT * c + m + 1)
                        nc.scalar.activation(soft[m][:, :], soft[m][:, :], ACT.Ln, bias=1.0).then_inc(soft_ready, 1)

                def body(front, middle, back):
                    if front:
                        load(*front)
                        if known(front[0], 1):
                            act.wait_ge(consts, START + 96)
                    if middle:
                        to_conv(*middle, 0)
                        to_conv(*middle, 1)
                        to_conv(*middle, 2)
                        sigmoid_u(*middle, 0)
                    if front:
                        square(*front)
                    if middle:
                        sigmoid_u(*middle, 1)
                    if back:
                        copy_xd(*back)
                    if middle:
                        to_conv(*middle, 3)
                        sigmoid_u(*middle, 2)
                    if back:
                        absolute(*back, 0)
                    if middle:
                        sigmoid_z(*middle, 0)
                    if back:
                        absolute(*back, 1)
                    if middle:
                        sigmoid_u(*middle, 3)
                    if front:
                        root(*front)
                    if middle:
                        sigmoid_z(*middle, 1)
                    if back:
                        absolute(*back, 2)
                    if middle:
                        sigmoid_z(*middle, 2)
                    if back:
                        absolute(*back, 3)
                    if front:
                        gains(*front)
                    if middle:
                        sigmoid_z(*middle, 3)
                    if back:
                        exp_ln(*back)

                on_sequences(act, body)

            @block.gpsimd
            def _(gp):
                nc.gpsimd.memset(xi[:, :, 0:TAPS - 1], 0.0).then_inc(padded, 1)
                nc.gpsimd.memset(eps[:, :], EPS).then_inc(padded, 1)

                def body(front, middle, back):
                    if back:
                        c, p = back
                        for m in range(DT):
                            gp.wait_ge(soft_ready, START + DT * c + m + 1)
                            if not known(c, 1) or m >= 2:
                                gp.wait_ge(dt_stored[m % 2], START + 16 * (2 * c + m // 2))
                                gp.wait_ge(dtu_stored[m % 2], START + 16 * (2 * c + m // 2))
                            nc.gpsimd.tensor_tensor(dt[m % 2][:, :], above[m][:, :], soft[m][:, :], ALU.add).then_inc(dt_ready, 1)
                            gp.wait_ge(dt_ready, START + DT * c + m + 1)
                            nc.gpsimd.tensor_tensor(dtu[m % 2][:, :], dt[m % 2][:, :], u[p][:, m], ALU.mult).then_inc(dtu_ready, 1)

                on_sequences(gp, body)

            @block.vector
            def _(v):
                v.wait_ge(consts, START + 96)

                def group_norm(c, p):
                    v.wait_ge(x_loaded, START + 16 * c + 16)
                    if not known(c, 1):
                        v.wait_ge(mean_ready, START + c)
                    nc.vector.tensor_scalar(xg[:, :, :], xc[:, :, :], norm[:, bass.ds(c, 1)], norm[:, bass.ds(C + c, 1)],
                                            ALU.mult, ALU.add).then_inc(xg_ready, 1)

                def centre(c, p):
                    v.wait_ge(mean_ready, START + c + 1)
                    v.wait_ge(xg_ready, START + c + 1)
                    if not known(c, 1):
                        v.wait_ge(h_ready, START + HT * c)
                    for k in range(HT):
                        nc.vector.tensor_tensor(cen[:, k], xg[:, k], stat_acc[:, :], ALU.subtract).then_inc(cen_ready, 1)

                def normalise(c, p):
                    v.wait_ge(var_copied, START + c + 1)
                    nc.vector.reciprocal(rstd[:, :], var[:, :]).then_inc(rstd_ready, 1)
                    v.wait_ge(rstd_ready, START + c + 1)
                    v.wait_ge(sq_ready, START + c + 1)
                    for k in range(HT):
                        nc.vector.tensor_tensor(cen[:, k], cen[:, k], rstd[:, :], ALU.mult).then_inc(hn_ready, 1)

                def convolve(c, p, m):
                    chain = Chain(v, tap_done, (TAPS - 1) * (DT * c + m))
                    to = pre[m % 2][:, :]
                    v.wait_ge(xi_ready, START + DT * c + m + 1)
                    if not known(c, 1) or m >= 2:
                        v.wait_ge(u_ready, START + DT * c + m - 1)
                    chain.link(nc.vector.tensor_scalar(to, xi[:, m, 0:W], taps[:, m, 0:1], taps[:, m, TAPS:TAPS + 1], ALU.mult, ALU.add))
                    for t in range(1, TAPS):
                        step = nc.vector.scalar_tensor_tensor(to, xi[:, m, t:t + W], taps[:, m, t:t + 1], to, ALU.mult, ALU.add)
                        if t < TAPS - 1:
                            chain.link(step)
                        else:
                            step.then_inc(pre_ready, 1)

                def silu_u(c, p, m):
                    v.wait_ge(sigu_ready, START + DT * c + m + 1)
                    if not known(c, 2):
                        v.wait_ge(u_stored[m], START + 16 * (c - 1))
                        v.wait_ge(dtu_ready, START + DT * (c - 1))
                        v.wait_ge(xd_ready, START + c - 1)
                    nc.vector.tensor_tensor(u[p][:, m], pre[m % 2][:, :], sigu[m % 2][:, :], ALU.mult).then_inc(u_ready, 1)

                def silu_z(c, p, m):
                    v.wait_ge(sigz_ready, START + DT * c + m + 1)
                    if not known(c, 1) or m >= 2:
                        v.wait_ge(z_stored[m % 2], START + 16 * (2 * c + m // 2))
                    nc.vector.tensor_tensor(z[m % 2][:, :], in_acc[m % 2][:, :], sigz[m % 2][:, :], ALU.mult).then_inc(z_ready, 1)

                def maximum(c, p, m):
                    v.wait_ge(dtp_ready, START + DT * c + m + 1)
                    if not known(c, 1):
                        v.wait_ge(dt_ready, START + DT * (c - 1) + m + 1)
                    nc.vector.tensor_scalar(above[m][:, :], back_acc[:, :], taps[:, m, TAPS + 1:TAPS + 2], 0.0, ALU.add, ALU.max).then_inc(above_ready, 1)

                def body(front, middle, back):
                    if front:
                        group_norm(*front)
                    if middle:
                        convolve(*middle, 0)
                        convolve(*middle, 1)
                    if front:
                        centre(*front)
                    if middle:
                        silu_u(*middle, 0)
                        convolve(*middle, 2)
                        silu_u(*middle, 1)
                    if back:
                        maximum(*back, 0)
                    if middle:
                        convolve(*middle, 3)
                        silu_u(*middle, 2)
                        silu_z(*middle, 0)
                    if back:
                        maximum(*back, 1)
                    if front:
                        normalise(*front)
                    if middle:
                        silu_u(*middle, 3)
                        silu_z(*middle, 1)
                    if back:
                        maximum(*back, 2)
                    if middle:
                        silu_z(*middle, 2)
                    if back:
                        maximum(*back, 3)
                    if middle:
                        silu_z(*middle, 3)

                on_sequences(v, body)


def stage_scan(nc, dt_d, dtu_d, u_d, z_d, bc, alog_d, dskip_d, ident_d, pick_d, gated_d):
    with ExitStack() as stack:
        s_ = Scope(nc, stack, "scan")
        RING = DT
        LO = 32
        dt = [s_.sb(f"dt{s}", [P, DT, W]) for s in range(2)]
        dtu = [s_.sb(f"dtu{s}", [P, DT, W]) for s in range(2)]
        u = s_.sb("u", [P, DT, W])
        z = s_.sb("z", [P, DT, W])
        B = [s_.sb(f"b{k}", [P, NW]) for k in range(4)]
        c_raw = s_.sb("c_raw", [LO + DS, W])
        c_high = s_.sb("c_high", [LO + DS, W], F32R)
        c_parts = s_.sb("c_parts", [P, W], F32R)
        pick_raw = s_.sb("pick_raw", [P, DS, P])
        pick = s_.sb("pick", [P, DS, P], F32R)
        drive = [s_.sb(f"drive{k}", [P, NW]) for k in range(2 * RING)]
        state = [s_.sb(f"state{k}", [P, NW]) for k in range(RING)]
        seen = [s_.sb(f"seen{k}", [P, NW]) for k in range(RING)]
        carry = s_.sb("carry", [P, DS * DT])
        alog = s_.sb("alog", [P, DT, DS])
        neg_a = s_.sb("a", [P, DT, DS])
        dskip = s_.sb("dskip", [P, DT])
        ident = s_.sb("ident", [P, P])
        diag = s_.sb("diag", [P, DT, P])
        zero = s_.sb("zero", [P, NW], mybir.dt.bfloat16)
        y = [s_.ps(f"y{m}", [P, NW]) for m in range(DT)]
        decay = [s_.ps(f"decay{k}", [P, NW]) for k in range(2)]
        c_all = [s_.ps(f"c_all{k}", [P, NW]) for k in range(2)]
        consts, set_up = s_.sem("consts"), s_.sem("set_up")
        pick_loaded, neg_a_ready = s_.sem("pick_loaded"), s_.sem("neg_a_ready")
        steps_loaded = s_.sems("steps_loaded", 2)
        u_loaded, z_loaded, c_loaded = s_.sem("u_loaded"), s_.sem("z_loaded"), s_.sem("c_loaded")
        b_loaded = s_.sems("b_loaded", 4)
        c_high_ready, c_parts_ready = s_.sem("c_high_ready"), s_.sem("c_parts_ready")
        decay_ready, drive_ready, c_ready = s_.sem("decay_ready"), s_.sem("drive_ready"), s_.sem("c_ready")
        scanned, carried, seen_ready, summed = s_.sem("scanned"), s_.sem("carried"), s_.sem("seen_ready"), s_.sem("summed")
        skip_ready, y_ready, gated, stored = s_.sem("skip_ready"), s_.sem("y_ready"), s_.sem("gated"), s_.sem("stored")
        dve = s_.sem("dve")
        FREE = RING - 1
        AHEAD = 2 * RING - 1

        def count(r, n, m):
            return (DS * r + n) * DT + m

        s_.start()
        with nc.Block() as block:
            @block.sync
            def _(sp):
                for dst, src in ((alog[:, :, :], alog_d), (dskip[:, :], dskip_d), (ident[:, :], ident_d)):
                    sp.dma_start(dst, src).then_inc(consts, 16)

                def load_b(c, half, at, k):
                    pieces = bc.rearrange("c n (q w) -> c (n q) w", q=DT)
                    at += half * (DT // HALVES)
                    row = pieces[c, bass.ds(at, DT // HALVES) if not isinstance(at, int) else slice(at, at + DT // HALVES)]
                    sp.dma_start(B[k][:, :].rearrange("p (q w) -> p q w", q=DT // HALVES),
                                 row.rearrange("(o q) w -> o q w", o=1).broadcast_to([P, DT // HALVES, W // DT])).then_inc(b_loaded[k], 16)

                def load_c(c):
                    for r in (0, LO):
                        sp.dma_start(c_raw[r:r + DS, :], bc[c, DS:]).then_inc(c_loaded, 16)

                def load_steps(c, s):
                    sp.dma_start(dt[s][:, :, :], dt_d[c]).then_inc(steps_loaded[s], 16)
                    sp.dma_start(dtu[s][:, :, :], dtu_d[c]).then_inc(steps_loaded[s], 16)

                def load_first(c, half, states=range(4)):
                    for k in states:
                        sp.wait_ge(drive_ready, START + count(HALVES * c + half, k, 0) - 3 * DT)
                        load_b(c, half, k * DT, k)

                def sequence(c, s, first, more):
                    for half in range(HALVES):
                        with sp.Fori(1, DS // 4) as g:
                            for k in range(4):
                                at = 4 * DT * g + k * DT
                                sp.wait_ge(drive_ready, START + DS * DT * HALVES * c + 4 * DT * g + (DS * half + k - 3) * DT)
                                load_b(c, half, at, k)
                        if half == 0:
                            if not first:
                                sp.wait_ge(gated, START + HALVES * DT * c + DT)
                                sp.dma_start(gated_d[c - 1], z[:, :, :]).then_inc(stored, 16)
                            if more:
                                load_steps(c + 1, 1 - s)
                            if not first:
                                sp.wait_ge(stored, START + 16 * c)
                            sp.dma_start(z[:, :, :], z_d[c]).then_inc(z_loaded, 16)
                            load_first(c, 1)
                        elif more:
                            load_first(c + 1, 0, range(1))
                            sp.wait_ge(skip_ready, START + HALVES * DT * (c + 1))
                            sp.dma_start(u[:, :, :], u_d[c + 1]).then_inc(u_loaded, 16)
                            load_c(c + 1)
                            load_first(c + 1, 0, range(1, 4))

                for k in range(2):
                    load_b(0, 0, k * DT, k)
                load_steps(0, 0)
                load_c(0)
                sp.dma_start(pick_raw[:, :, :], pick_d).then_inc(pick_loaded, 16)
                for k in range(2, 4):
                    load_b(0, 0, k * DT, k)
                sp.dma_start(u[:, :, :], u_d[0]).then_inc(u_loaded, 16)
                sequence(0, 0, True, True)
                with sp.Fori(0, C // 2 - 1) as i:
                    for s in range(2):
                        sequence(2 * i + 1 + s, 1 - s, False, True)
                sequence(C - 1, 1, False, False)
                sp.wait_ge(gated, START + HALVES * DT * C + DT)
                sp.dma_start(gated_d[C - 1], z[:, :, :]).then_inc(stored, 16)
                sp.wait_ge(stored, START + 16 * C)

            def on_states(eng, before, state_step, after, apart=4):
                with eng.Fori(0, C // 2) as i:
                    for s in range(2):
                        c = 2 * i + s
                        for half in range(HALVES):
                            before(i, c, s, half)
                            for n in range(apart):
                                state_step(c, s, half, n, n % 4)
                            if apart < DS:
                                with eng.Fori(apart // 4, DS // 4) as g:
                                    for k in range(4):
                                        state_step(c, s, half, 4 * g + k, k)
                            after(c, half)

            @block.scalar
            def _(act):
                act.wait_ge(consts, START + 48)
                nc.scalar.activation(neg_a[:, :, :], alog[:, :, :], ACT.Exp).then_inc(set_up, 1)
                act.wait_ge(neg_a_ready, START + 1)

                def before(i, c, s, half):
                    if half == 0:
                        act.wait_ge(c_loaded, START + 32 * c + 32)
                        act.wait_ge(c_ready, START + HALVES * DS * c)
                        act.wait_ge(c_parts_ready, START + c)
                        nc.scalar.activation(c_high[LO:LO + DS, :], c_raw[LO:LO + DS, :], ACT.Copy).then_inc(c_high_ready, 1)
                        nc.scalar.activation(c_parts[0:DS, :], c_raw[0:DS, :], ACT.Copy).then_inc(c_high_ready, 1)
                        act.wait_ge(steps_loaded[s], START + 32 * i + 32)

                def step(c, s, half, n, k):
                    r = HALVES * c + half
                    for m in range(DT):
                        act.wait_ge(scanned, START + AHEAD + count(r, n, m) - 1)
                        nc.scalar.activation(decay[m % 2][:, :], dt[s][:, m, half * NW:(half + 1) * NW], ACT.Exp,
                                             scale=neg_a[:, m, bass.ds(n, 1) if not isinstance(n, int) else slice(n, n + 1)]).then_inc(decay_ready, 1)
                        if half == 0 and m >= 2:
                            keep(c, n, m - 2)
                    if half == 0:
                        for m in (DT - 2, DT - 1):
                            act.wait_ge(scanned, START + AHEAD + count(r, n, m) + 1)
                            keep(c, n, m)

                def keep(c, n, m):
                    at = n * DT + m
                    nc.scalar.activation(carry[:, bass.ds(at, 1) if not isinstance(at, int) else slice(at, at + 1)],
                                         state[m][:, NW - 1:NW], ACT.Copy).then_inc(carried, 1)
                on_states(act, before, step, lambda c, half: None)

            @block.gpsimd
            def _(gp):
                nc.gpsimd.memset(zero[:, :], 0.0).then_inc(set_up, 1)

                def before(i, c, s, half):
                    if half == 0:
                        gp.wait_ge(steps_loaded[s], START + 32 * i + 32)

                def step(c, s, half, n, k):
                    r = HALVES * c + half
                    gp.wait_ge(b_loaded[k], START + 64 * r + 4 * (n - k) + 16)
                    for m in range(DT):
                        gp.wait_ge(scanned, START + count(r, n, m))
                        nc.gpsimd.tensor_tensor(drive[RING * (k % 2) + m][:, :], dtu[s][:, m, half * NW:(half + 1) * NW], B[k][:, :], ALU.mult).then_inc(drive_ready, 1)
                on_states(gp, before, step, lambda c, half: None)

            @block.vector
            def _(v):
                nc.vector.memset(c_parts[:, :].bitcast(mybir.dt.uint32), 0).then_inc(dve, 1)
                v.wait_ge(consts, START + 48)
                v.wait_ge(set_up, START + 2)
                chain = Chain(v, dve, 1)
                chain.link(nc.vector.tensor_scalar(neg_a[:, :, :], neg_a[:, :, :], -1.0, None, ALU.mult))
                v.sem_inc(neg_a_ready, 1)
                v.wait_ge(pick_loaded, START + 16)
                chain.link(nc.vector.tensor_copy(pick[:, :, :], pick_raw[:, :, :]))
                for m in range(DT):
                    chain.link(nc.vector.tensor_scalar(diag[:, m], ident[:, :], dskip[:, m:m + 1], None, ALU.mult))
                v.sem_inc(set_up, 1)
                v.sem_inc(scanned, AHEAD)
                v.sem_inc(gated, DT)

                def before(i, c, s, half):
                    if half == 0:
                        v.wait_ge(c_high_ready, START + 2 * c + 2)
                        nc.vector.tensor_tensor(c_parts[LO:LO + DS, :], c_raw[LO:LO + DS, :], c_high[LO:LO + DS, :].bitcast(F32),
                                                ALU.subtract).then_inc(c_parts_ready, 1)

                def step(c, s, half, n, k):
                    r = HALVES * c + half

                    def scan(m):
                        at = n * DT + m
                        first = carry[:, bass.ds(at, 1) if not isinstance(at, int) else slice(at, at + 1)] if half else 0.0
                        v.wait_ge(decay_ready, START + count(r, n, m) + 1)
                        v.wait_ge(drive_ready, START + count(r, n, m) + 1)
                        if half:
                            v.wait_ge(carried, START + DS * DT * (c + 1))
                        nc.vector.tensor_tensor_scan(state[m][:, :], decay[m % 2][:, :], drive[RING * (k % 2) + m][:, :], first, ALU.mult, ALU.add).then_inc(scanned, 1)

                    def see(m):
                        if m == 0:
                            v.wait_ge(c_ready, START + DS * r + n + 1)
                        v.wait_ge(summed, START + count(r, n, m))
                        v.wait_ge(scanned, START + count(r, n, m) + 1 + AHEAD)
                        nc.vector.tensor_tensor(seen[m][:, :], c_all[k % 2][:, :], state[m][:, :], ALU.mult).then_inc(seen_ready, 1)

                    scan(0)
                    for m in range(1, DT):
                        scan(m)
                        see(m - 1)
                    see(DT - 1)

                def after(c, half):
                    if half == 0:
                        v.wait_ge(z_loaded, START + 16 * c + 16)
                    for m in range(DT):
                        v.wait_ge(y_ready, START + DT * (HALVES * c + half) + m + 1)
                        zh = z[:, m, half * NW:(half + 1) * NW]
                        nc.vector.tensor_tensor(zh, zh, y[m][:, :], ALU.mult).then_inc(gated, 1)
                on_states(v, before, step, after)

            @block.tensor
            def _(pe):
                pe.wait_ge(set_up, START + 3)
                pe.sem_inc(summed, FREE)

                def add_up(r, n, m):
                    pe.wait_ge(seen_ready, START + count(r, n, m) + 1)
                    nc.tensor.matmul(y[m][:, :], ident[:, :], seen[m][:, :], start=False, stop=False).then_inc(summed, 1)

                def before(i, c, s, half):
                    if half == 0:
                        pe.wait_ge(c_parts_ready, START + c + 1)
                        pe.wait_ge(u_loaded, START + 16 * c + 16)

                def step(c, s, half, n, k):
                    r, h = HALVES * c + half, slice(half * NW, (half + 1) * NW)
                    at = bass.ds(n, 1) if not isinstance(n, int) else slice(n, n + 1)
                    nc.tensor.matmul(c_all[k % 2][:, :], pick[:, at].rearrange("p o q -> p (o q)"), c_parts[:, h],
                                     start=True, stop=True).then_inc(c_ready, 1)
                    if n > 0:
                        add_up(r, n - 1, DT - 1)
                    for m in range(DT - 1):
                        if n == 0:
                            begin(r, h, m)
                        add_up(r, n, m)
                        if n == DS - 1:
                            close(m)
                    if n == 0:
                        begin(r, h, DT - 1)

                def begin(r, h, m):
                    pe.wait_ge(gated, START + DT * r + m + 1)
                    nc.tensor.matmul(y[m][:, :], diag[:, m], u[:, m, h], start=True, stop=False).then_inc(skip_ready, 1)

                def close(m):
                    nc.tensor.matmul(y[m][:, :], zero[:, 0:P], zero[:, :], start=False, stop=True).then_inc(y_ready, 1)

                def after(c, half):
                    add_up(HALVES * c + half, DS - 1, DT - 1)
                    close(DT - 1)
                on_states(pe, before, step, after, apart=DS)


def stage_outer(nc, gated_d, x1, norm, avg_d, outw_d, lnp_d, res_d, h2_d):
    with ExitStack() as stack:
        s_ = Scope(nc, stack, "outer")
        avg = s_.sb("avg", [P, P])
        outw = s_.sb("outw", [P, DT, H])
        lnp = s_.sb("lnp", [P, HT, 2])
        gate = [s_.sb(f"gated{s}", [P, DT, W]) for s in range(2)]
        xc = [s_.sb(f"x{s}", [P, HT, W]) for s in range(2)]
        xg = s_.sb("xg", [P, HT, W])
        x2 = [s_.sb(f"x2{p}", [P, HT, W]) for p in range(2)]
        res = s_.sb("res", [P, HT, W])
        cen = s_.sb("cen", [P, HT, W])
        sq = s_.sb("sq", [P, HT, W])
        var = s_.sb("var", [P, W])
        rstd = s_.sb("rstd", [P, W])
        eps = s_.sb("eps", [P, 1])
        hn = s_.sb("hn", [P, HT, W])
        acc = [s_.ps(f"acc{k}", [P, W]) for k in range(2)]
        mean_ps, var_ps = s_.ps("mean_acc", [P, W]), s_.ps("var_acc", [P, W])
        consts, set_up = s_.sem("consts"), s_.sem("set_up")
        loaded = s_.sems("loaded", 2)
        out_ready, xg_ready, x2_ready, res_ready = (s_.sem(k) for k in ("out_ready", "xg_ready", "x2_ready", "res_ready"))
        mean_ready, cen_ready, sq_ready, var_ready = (s_.sem(k) for k in ("mean_ready", "cen_ready", "sq_ready", "var_ready"))
        var_copied, rstd_ready, hn_ready, h_ready = (s_.sem(k) for k in ("var_copied", "rstd_ready", "hn_ready", "h_ready"))
        res_stored, h_stored = s_.sem("res_stored"), s_.sem("h_stored")

        def on_sequences(eng, body):
            body((0, 0), None)
            with eng.Fori(0, C // 2 - 1) as i:
                for p in range(2):
                    body((2 * i + p + 1, 1 - p), (2 * i + p, p))
            body((C - 1, 1), (C - 2, 0))
            body(None, (C - 1, 1))

        s_.start()
        with nc.Block() as block:
            @block.sync
            def _(sp):
                for dst, src in ((avg[:, :], avg_d), (outw[:, :, :], outw_d), (lnp[:, :, :], lnp_d)):
                    sp.dma_start(dst, src).then_inc(consts, 16)

                view = lambda t: t.rearrange("c (k p) w -> c p k w", p=P)

                def load(c, s):
                    sp.dma_start(gate[s][:, :, :], gated_d[c]).then_inc(loaded[s], 16)
                    sp.dma_start(xc[s][:, :, :], view(x1)[c]).then_inc(loaded[s], 16)

                def sequence(c, s, more):
                    sp.wait_ge(res_ready, START + c + 1)
                    sp.dma_start(view(res_d)[c], res[:, :, :]).then_inc(res_stored, 16)
                    if more:
                        load(c + 2, s)
                    sp.wait_ge(h_ready, START + HT * c + HT)
                    sp.dma_start(view(h2_d)[c], hn[:, :, :]).then_inc(h_stored, 16)

                for s in range(2):
                    load(s, s)
                with sp.Fori(0, C // 2 - 1) as i:
                    for s in range(2):
                        sequence(2 * i + s, s, True)
                for s in range(2):
                    sequence(C - 2 + s, s, False)
                sp.wait_ge(res_stored, START + 16 * C)
                sp.wait_ge(h_stored, START + 16 * C)

            @block.tensor
            def _(pe):
                pe.wait_ge(consts, START + 48)

                def project(c, p, g):
                    if g == 0:
                        pe.wait_ge(loaded[p], START + 16 * (c - p) + 32)
                    if not (isinstance(c, int) and c == 0):
                        pe.wait_ge(x2_ready, START + HT * c)
                    for half in range(HALVES):
                        for k in range(DT):
                            last = nc.tensor.matmul(acc[g][:, half * NW:(half + 1) * NW], outw[:, k, g * P:(g + 1) * P],
                                                    gate[p][:, k, half * NW:(half + 1) * NW], start=k == 0, stop=k == DT - 1)
                    last.then_inc(out_ready, 1)

                def average(src, dst, done):
                    for half in range(HALVES):
                        for k in range(HT):
                            last = nc.tensor.matmul(dst[:, half * NW:(half + 1) * NW], avg[:, :], src[:, k, half * NW:(half + 1) * NW],
                                                    start=k == 0, stop=k == HT - 1)
                    last.then_inc(done, 1)

                def body(front, back):
                    if front:
                        project(*front, 0)
                    if back:
                        c, p = back
                        pe.wait_ge(x2_ready, START + HT * c + HT)
                        pe.wait_ge(cen_ready, START + HT * c)
                        average(x2[p], mean_ps, mean_ready)
                    if front:
                        project(*front, 1)
                    if back:
                        pe.wait_ge(sq_ready, START + c + 1)
                        pe.wait_ge(var_copied, START + c)
                        average(sq, var_ps, var_ready)

                on_sequences(pe, body)

            @block.scalar
            def _(act):
                act.wait_ge(consts, START + 48)
                act.wait_ge(set_up, START + 1)

                def body(front, back):
                    if back:
                        c, p = back
                        act.wait_ge(cen_ready, START + HT * c + HT)
                        nc.scalar.activation(sq[:, :, :], cen[:, :, :], ACT.Square).then_inc(sq_ready, 1)
                        act.wait_ge(var_ready, START + c + 1)
                        act.wait_ge(rstd_ready, START + c)
                        nc.scalar.activation(var[:, :], var_ps[:, :], ACT.Sqrt, bias=eps[:, :]).then_inc(var_copied, 1)
                        for k in range(HT):
                            act.wait_ge(hn_ready, START + HT * c + k + 1)
                            nc.scalar.activation(hn[:, k], hn[:, k], ACT.Identity, scale=lnp[:, k, 0:1], bias=lnp[:, k, 1:2]).then_inc(h_ready, 1)

                on_sequences(act, body)

            @block.gpsimd
            def _(gp):
                nc.gpsimd.memset(eps[:, :], EPS).then_inc(set_up, 1)

                def body(front, back):
                    if front:
                        c, p = front
                        gp.wait_ge(x2_ready, START + HT * c + HT)
                        gp.wait_ge(res_stored, START + 16 * c)
                        nc.gpsimd.tensor_tensor(res[:, :, :], xc[p][:, :, :], x2[p][:, :, :], ALU.add).then_inc(res_ready, 1)

                on_sequences(gp, body)

            @block.vector
            def _(v):
                def residual(c, p, g):
                    if g == 0:
                        v.wait_ge(loaded[p], START + 16 * (c - p) + 32)
                        v.wait_ge(x2_ready, START + HT * c)
                        nc.vector.tensor_scalar(xg[:, :, :], xc[p][:, :, :], norm[:, bass.ds(c, 1)], norm[:, bass.ds(C + c, 1)],
                                                ALU.mult, ALU.add).then_inc(xg_ready, 1)
                        v.wait_ge(xg_ready, START + c + 1)
                        if not (isinstance(c, int) and c < 2):
                            v.wait_ge(res_ready, START + c - 1)
                            v.wait_ge(mean_ready, START + c - 1)
                    v.wait_ge(out_ready, START + HT * c + g + 1)
                    nc.vector.tensor_tensor(x2[p][:, g], acc[g][:, :], xg[:, g], ALU.add).then_inc(x2_ready, 1)

                def body(front, back):
                    if front:
                        residual(*front, 0)
                    if back:
                        c, p = back
                        v.wait_ge(mean_ready, START + c + 1)
                        v.wait_ge(sq_ready, START + c)
                        v.wait_ge(hn_ready, START + HT * c)
                        for k in range(HT):
                            nc.vector.tensor_tensor(cen[:, k], x2[p][:, k], mean_ps[:, :], ALU.subtract).then_inc(cen_ready, 1)
                    if front:
                        residual(*front, 1)
                    if back:
                        v.wait_ge(var_copied, START + c + 1)
                        nc.vector.reciprocal(rstd[:, :], var[:, :]).then_inc(rstd_ready, 1)
                        v.wait_ge(rstd_ready, START + c + 1)
                        v.wait_ge(cen_ready, START + HT * c + HT)
                        v.wait_ge(h_stored, START + 16 * c)
                        for k in range(HT):
                            nc.vector.tensor_tensor(hn[:, k], cen[:, k], rstd[:, :], ALU.mult).then_inc(hn_ready, 1)

                on_sequences(v, body)


def stage_perceptron(nc, name, w_d, bias_d, src_d, kt, mt, cols, dst_d, add_d=None):
    with ExitStack() as stack:
        s_ = Scope(nc, stack, name)
        CK = KD
        CH = kt // CK
        N = mt * CH
        GROUPS = W // cols
        STAGING = 4 * W // cols
        src_hi, src_lo = s_.sb("src_hi", [P, kt, cols], F32R), s_.sb("src_lo", [P, kt, cols], F32R)
        staged = [s_.sb(f"staged{k}", [P, cols]) for k in range(STAGING)]
        raw = [s_.sb(f"raw{s}", [P, CK * P]) for s in range(2)]
        w_hi = [s_.sb(f"w_hi{s}", [P, CK * P], F32R) for s in range(2)]
        w_lo = [s_.sb(f"w_lo{s}", [P, CK * P], F32R) for s in range(2)]
        bias = s_.sb("bias", [P, mt])
        out = [s_.sb(f"out{t}", [P, cols]) for t in range(2)]
        add = [s_.sb(f"add{t}", [P, cols]) for t in range(2)] if add_d is not None else None
        acc = [s_.ps(f"acc{t}", [P, cols]) for t in range(2)]
        bias_loaded = s_.sem("bias_loaded")
        staged_loaded = s_.sems("staged_loaded", STAGING)
        raw_loaded = s_.sems("raw_loaded", 2)
        src_hi_ready, src_lo_ready = s_.sem("src_hi_ready"), s_.sem("src_lo_ready")
        w_hi_ready, w_lo_ready = s_.sem("w_hi_ready"), s_.sem("w_lo_ready")
        src_used = s_.sem("src_used")
        w_used = s_.sem("w_used")
        finished = s_.sem("finished")
        stored = s_.sems("stored", 2)
        add_loaded = s_.sems("add_loaded", 2)

        s_.start()
        with nc.Block() as block:
            @block.sync
            def _(sp):
                def load_source(g, tiles):
                    for k in tiles:
                        r = g * kt + k
                        if r >= STAGING:
                            sp.wait_ge(src_lo_ready, START + r - STAGING + 1)
                        sp.dma_start(staged[r % STAGING][:, :], src_d[k, :, g * cols:(g + 1) * cols]).then_inc(staged_loaded[r % STAGING], 16)

                def load_chunk(n, j, s):
                    if not (isinstance(n, int) and n < 2):
                        sp.wait_ge(w_lo_ready, START + n - 1)
                    sp.dma_start(raw[s][:, :], w_d[j]).then_inc(raw_loaded[s], 16)

                load_chunk(0, 0, 0)
                sp.dma_start(bias[:, :], bias_d).then_inc(bias_loaded, 16)
                load_source(0, range(0, 4))
                load_chunk(1, 1, 1)
                for g in range(GROUPS):
                    load_source(g, range(0 if g else 4, kt // 2))
                    for s in range(2):
                        load_chunk(g * N + 2 + s, 2 + s, s)
                    load_source(g, range(kt // 2, kt))
                    with sp.Fori(2, N // 2) as i:
                        for s in range(2):
                            load_chunk(g * N + 2 * i + s, 2 * i + s, s)
                    if g + 1 < GROUPS:
                        for s in range(2):
                            load_chunk((g + 1) * N + s, s, s)

            @block.tensor
            def _(pe):
                def tile(g, i, t):
                    first, last_tile = isinstance(i, int) and i + t == 0, isinstance(i, int) and 2 * i + t == mt - 1
                    q = g * mt + 2 * i + t
                    if not (isinstance(q, int) and q < 2):
                        pe.wait_ge(finished, START + q - 1)
                    for c in range(CH):
                        s = (t * CH + c) % 2
                        pe.wait_ge(w_lo_ready, START + q * CH + c + 1)
                        for j in range(CK):
                            k = c * CK + j
                            if first:
                                pe.wait_ge(src_lo_ready, START + g * kt + k + 1)
                            for half in range(cols // NW):
                                h = slice(half * NW, (half + 1) * NW)
                                for wp, sr in ((w_hi, src_hi), (w_hi, src_lo), (w_lo, src_hi)):
                                    last = nc.tensor.matmul(acc[t][:, h], wp[s][:, j * P:(j + 1) * P], sr[:, k, h],
                                                            start=k == 0 and wp is w_hi and sr is src_hi,
                                                            stop=k == kt - 1 and wp is w_lo)
                            if last_tile and g + 1 < GROUPS and j < CK - 1:
                                last.then_inc(src_used, 1)
                        last.then_inc(w_used, 1)

                for g in range(GROUPS):
                    for t in range(2):
                        tile(g, 0, t)
                    with pe.Fori(1, mt // 2 - 1) as i:
                        for t in range(2):
                            tile(g, i, t)
                    for t in range(2):
                        tile(g, mt // 2 - 1, t)

            def on_tiles(eng, split_source, split_chunk, finish):
                for g in range(GROUPS):
                    def step(i, t, splits=CH):
                        for c in range(splits):
                            split_chunk(g * N + (2 * i + t) * CH + c + 2, (t * CH + c) % 2)
                        finish(g, i, t)

                    split_chunk(g * N, 0)
                    split_source(g, range(kt // 2))
                    split_chunk(g * N + 1, 1)
                    if g:
                        finish(g - 1, mt // 2 - 1, 1)
                    split_source(g, range(kt // 2, kt))
                    with eng.Fori(0, mt // 2 - 1) as i:
                        for t in range(2):
                            step(i, t)
                    step(mt // 2 - 1, 0, CH if CH > 1 else 0)
                finish(GROUPS - 1, mt // 2 - 1, 1)

            @block.scalar
            def _(act):
                def split_source(g, tiles):
                    for k in tiles:
                        r = g * kt + k
                        act.wait_ge(staged_loaded[r % STAGING], START + 16 * (r // STAGING + 1))
                        if g:
                            if k % CK < CK - 1:
                                act.wait_ge(src_used, START + (g - 1) * (kt - CH) + k // CK * (CK - 1) + k % CK + 1)
                            else:
                                act.wait_ge(w_used, START + (g - 1) * N + N - CH + k // CK + 1)
                        nc.scalar.activation(src_hi[:, k], staged[r % STAGING][:, :], ACT.Copy).then_inc(src_hi_ready, 1)

                def split_chunk(n, s):
                    act.wait_ge(raw_loaded[s], START + 8 * (n - s) + 16)
                    if not (isinstance(n, int) and n < 2):
                        act.wait_ge(w_used, START + n - 1)
                    nc.scalar.activation(w_hi[s][:, :], raw[s][:, :], ACT.Copy).then_inc(w_hi_ready, 1)

                def load_add(g, m, t):
                    act.dma_start(add[t][:, :], add_d[m][:, g * cols:(g + 1) * cols]).then_inc(add_loaded[t], 16)

                def finish(g, i, t):
                    q = g * mt + 2 * i + t
                    if add_d is None:
                        act.wait_ge(w_used, START + (q + 1) * CH)
                        act.wait_ge(stored[t], START + 8 * (q - t))
                        nc.scalar.activation(out[t][:, :], acc[t][:, :], ACT.Relu,
                                             bias=bias[:, bass.ds(2 * i + t, 1)]).then_inc(finished, 1)
                    act.wait_ge(finished, START + q + 1)
                    act.dma_start(dst_d[2 * i + t][:, g * cols:(g + 1) * cols], out[t][:, :]).then_inc(stored[t], 16)
                    if add_d is not None:
                        if not isinstance(i, int) or 2 * i + t + 2 < mt:
                            load_add(g, 2 * i + t + 2, t)
                        elif g + 1 < GROUPS:
                            load_add(g + 1, t, t)

                if add_d is not None:
                    for t in range(2):
                        load_add(0, t, t)
                act.wait_ge(bias_loaded, START + 16)
                on_tiles(act, split_source, split_chunk, finish)
                for t in range(2):
                    act.wait_ge(stored[t], START + 16 * (GROUPS * mt // 2))

            @block.vector
            def _(v):
                def split_source(g, tiles):
                    for k in tiles:
                        r = g * kt + k
                        v.wait_ge(src_hi_ready, START + r + 1)
                        nc.vector.tensor_tensor(src_lo[:, k], staged[r % STAGING][:, :], src_hi[:, k].bitcast(F32), ALU.subtract).then_inc(src_lo_ready, 1)

                def split_chunk(n, s):
                    v.wait_ge(w_hi_ready, START + n + 1)
                    nc.vector.tensor_tensor(w_lo[s][:, :], raw[s][:, :], w_hi[s][:, :].bitcast(F32), ALU.subtract).then_inc(w_lo_ready, 1)

                def finish(g, i, t):
                    if add_d is not None:
                        q = g * mt + 2 * i + t
                        v.wait_ge(w_used, START + (q + 1) * CH)
                        v.wait_ge(add_loaded[t], START + 8 * (q - t) + 16)
                        v.wait_ge(stored[t], START + 8 * (q - t))
                        nc.vector.scalar_tensor_tensor(out[t][:, :], acc[t][:, :], bias[:, bass.ds(2 * i + t, 1)], add[t][:, :],
                                                       ALU.add, ALU.add).then_inc(finished, 1)

                v.wait_ge(bias_loaded, START + 16)
                on_tiles(v, split_source, split_chunk, finish)


def build(nc, t, out):
    def scratch(name, shape):
        return nc.dram_tensor(f"scratch_{name}", shape, F32, kind="Internal").ap()

    y = scratch("y", [3, C, H, W])
    q_parts, k_parts = scratch("q", [2, C * H, W]), scratch("k", [2, C * H, W])
    v_heads = scratch("v", [NH, P, KT * D])
    att, den, rden = scratch("att", [NH, D, W]), scratch("den", [NH, W]), scratch("rden", [NH, W])
    mixed, x1 = scratch("mixed", [C, H, W]), scratch("x1", [C, H, W])
    u_d, z_d, dt_d, dtu_d, gated_d = (scratch(k, [C, P, DT, W]) for k in ("u", "z", "dt", "dtu", "gated"))
    bc = scratch("bc", [C, 2 * DS, W])
    res_d, h2_d = scratch("res", [C, H, W]), scratch("h2", [C, H, W])
    hid_d = scratch("hid", [MT, P, W])
    norm = nc.alloc_sbuf_tensor("norm", [P, 2 * C], F32)

    stage_project(nc, t["x"], t["w_qkv"], y)
    stage_convolve(nc, y, t["kron"], t["cbias"], t["vbias"], t["rot"], t["cos"], t["sin"], q_parts, k_parts, v_heads)
    stage_attend(nc, q_parts, k_parts, v_heads, t["ident"], t["mask"], att, den)
    stage_recombine(nc, att, den, rden, t["wo"], mixed)
    stage_mix(nc, mixed, t["kmix"], t["x"], t["gavg"], t["sel"], x1, norm)
    stage_inner(nc, x1, norm, t["avg"], t["inw"], t["ln1"], t["taps"], t["xpw"], t["dtw"], bc, u_d, z_d, dt_d, dtu_d)
    stage_scan(nc, dt_d, dtu_d, u_d, z_d, bc, t["alog"], t["dskip"], t["ident"], t["pick"], gated_d)
    stage_outer(nc, gated_d, x1, norm, t["avg"], t["outw"], t["ln2"], res_d, h2_d)
    tiles = lambda a: a.rearrange("c (k p) w -> (c k) p w", p=P)
    stage_perceptron(nc, "up", t["w1"], t["b1"], tiles(h2_d), KD, MT, W, hid_d)
    stage_perceptron(nc, "down", t["w2"], t["b2"], hid_d, MT, KD, NW, tiles(out[0]), tiles(res_d))


def constants():
    p = np.arange(P)
    out = {"ident": np.eye(P, dtype=np.float32)}
    rot = np.zeros((P, P), np.float32)
    rot[p ^ 1, p] = 1
    out["rot"] = rot
    inv = np.float32(1.0) / np.float32(10000.0) ** (np.arange(0, D, 2, dtype=np.float32) / np.float32(D))
    freqs = np.repeat(np.arange(W, dtype=np.float32)[:, None] * inv.astype(np.float32), 2, axis=-1)
    d = p[:, None] % HB + HB * np.arange(2)[None, :]
    sign = np.where(d % 2 == 0, -1.0, 1.0).astype(np.float32)
    out["cos"] = np.ascontiguousarray(np.cos(freqs).T[d])
    out["sin"] = np.ascontiguousarray(np.sin(freqs).T[d] * sign[:, :, None])
    mask = np.zeros((2 * KT, KT, P), np.float32)
    for t in range(KT):
        mask[t, t] = mask[KT + t, t] = 1
    out["mask"] = mask
    out["gavg"] = (p[:, None] // (GROUP * HB) == p[None, :] // (GROUP * HB)).astype(np.float32) / (GROUP * HB)
    out["sel"] = (p[:, None] // HB == np.arange(C)[None, :]).astype(np.float32) / HB
    pick = np.zeros((P, DS, P), np.float32)
    for n in range(DS):
        pick[n, n] = pick[32 + n, n] = 1
    out["pick"] = pick
    out["avg"] = np.full((P, P), 1.0 / H, np.float32)
    return out


def spread_rows(m):
    k = np.zeros((C, HB, C, HB), np.float32)
    for r in range(HB):
        k[:, r, :, r] = m.T
    return k.reshape(P, P)


def cols(v, n):
    return v.reshape(n, P).T


def lay_out(i):
    t = constants()
    t["x"] = i["x"]
    L0, L1 = "L0_conv_", "L1_conv_"

    def contraction_first(w):
        w = np.swapaxes(w, -1, -2)
        w = w.reshape(*w.shape[:-2], w.shape[-2] // P, P, w.shape[-1])
        return np.swapaxes(w, -3, -2)

    parts = [contraction_first(i[f"{L0}W{n}_pw"]).reshape(C, P, HT * H) for n in "qkv"]
    parts += [np.swapaxes(i[f"{L0}b{n}_pw"].reshape(C, HT, P), 1, 2) for n in "qkv"]
    t["w_qkv"] = np.concatenate(parts, axis=2)
    t["kron"] = np.stack([np.stack([spread_rows(i[f"{L0}W{n}_conv"][:, :, 0, tap]) for tap in range(CT)], 1) for n in "qkv"], 1)
    t["cbias"] = np.stack([np.repeat(i[f"{L0}b{n}_conv"], HB) for n in "qk"], 1)
    t["vbias"] = np.broadcast_to(np.repeat(i[f"{L0}bv_conv"], HB), (P, P))
    t["wo"] = contraction_first(i[L0 + "Wo_pw"])
    t["kmix"] = spread_rows(i[L0 + "Wo_dw"])
    t["inw"] = contraction_first(i[L1 + "in_proj_w"])
    for n in "12":
        t["ln" + n] = np.stack([cols(i[f"{L1}n{n}_g"], HT), cols(i[f"{L1}n{n}_b"], HT)], 2)
    taps = [cols(i[L1 + "conv_w"][:, k], DT) for k in range(TAPS)] + [cols(i[L1 + "conv_b"], DT), cols(i[L1 + "dt_proj_b"], DT)]
    t["taps"] = np.stack(taps, 2)
    t["xpw"] = contraction_first(i[L1 + "x_proj_w"])
    t["dtw"] = i[L1 + "dt_proj_w"].T
    t["alog"] = np.swapaxes(i[L1 + "A_log"].reshape(DT, P, DS), 0, 1)
    t["dskip"] = cols(i[L1 + "D_skip"], DT)
    t["outw"] = contraction_first(i[L1 + "out_proj_w"])
    for n, kt, mt in (("1", KD, MT), ("2", MT, KD)):
        w = i[f"{L1}pw{n}_w"].reshape(mt, P, kt // KD, KD, P).transpose(0, 2, 4, 3, 1)
        t["w" + n] = w.reshape(mt * (kt // KD), P, KD * P)
        t["b" + n] = cols(i[f"{L1}pw{n}_b"], mt)
    return t


def kernel(**inputs):
    import concourse.bacc as bacc
    from concourse.bass_utils import run_bass_kernel_spmd

    nc = bacc.Bacc("TRN2", target_bir_lowering=False, num_devices=1)
    arrays, t = {}, {}
    for name, a in lay_out({k: np.asarray(v) for k, v in inputs.items()}).items():
        a = np.ascontiguousarray(a)
        arrays[f"in_{name}"] = a
        t[name] = nc.dram_tensor(f"in_{name}", a.shape, mybir.dt.from_np(a.dtype), kind="ExternalInput").ap()
    out = nc.dram_tensor("out", (1, C, H, W), F32, kind="ExternalOutput").ap()
    build(nc, t, out)
    r = run_bass_kernel_spmd(nc, [arrays], core_ids=[0])
    return r.results[0]["out"]
```
